# Optimizing a Trainium2 kernel written in Bass

```python
import numpy as np
import jax
import jax.numpy as jnp

def _softmax(x, axis=-1):
    return jax.nn.softmax(x, axis=axis)

def _gelu(x):
    return jax.nn.gelu(x, approximate=True)

def _silu(x):
    return jax.nn.silu(x)

def _sigmoid(x):
    return jax.nn.sigmoid(x)

def _layernorm(x, axis=-1, eps=1e-05):
    m = jnp.mean(x, axis=axis, keepdims=True)
    v = jnp.var(x, axis=axis, keepdims=True)
    return (x - m) / jnp.sqrt(v + eps)

def _scatter_add(tgt, idx, src, axis=0):
    return tgt.at[idx].add(src)

def _segment_sum(src, seg, n):
    return jax.ops.segment_sum(src, seg, n)
kernel_name = 'mk_sandwich_d2_jaxref_r8_2bdd86'

def setup_inputs(seed: int=0):
    np.random.seed(seed)
    _w = jnp.asarray

    def _L0_attn_setup():
        import jax, jax.numpy as jnp
        import numpy as np
        DIM = 128
        NUM_HEADS = 16
        HEAD_DIM = DIM // NUM_HEADS
        TAU = 2.0
        V_TH = 1.0
        BN_EPS = 1e-05

        def _branch(x, W, gamma, beta):
            B, N, D = x.shape
            h = jnp.einsum('bnd,ed->bne', x, W)
            hf = h.reshape(B * N, D)
            mean = jnp.mean(hf, axis=0)
            var = jnp.var(hf, axis=0)
            hn = (hf - mean) * jax.lax.rsqrt(var + BN_EPS) * gamma + beta
            hn = hn.reshape(B, N, D)
            return jax.nn.sigmoid(4.0 * (hn - V_TH))

        def _heads(x):
            B, N, D = x.shape
            return x.reshape(B, N, NUM_HEADS, HEAD_DIM).transpose(0, 2, 1, 3)
        key = jax.random.key(seed)
        ks = jax.random.split(key, 12)
        B, N, D = (8, 512, DIM)
        s = 0.02
        return {'x': jax.random.normal(ks[0], (B, N, D), dtype=jnp.float32), 'Wq': jax.random.normal(ks[1], (D, D), dtype=jnp.float32) * s, 'gq': jnp.ones((D,), jnp.float32), 'bq': jnp.zeros((D,), jnp.float32), 'Wk': jax.random.normal(ks[2], (D, D), dtype=jnp.float32) * s, 'gk': jnp.ones((D,), jnp.float32), 'bk': jnp.zeros((D,), jnp.float32), 'Wv': jax.random.normal(ks[3], (D, D), dtype=jnp.float32) * s, 'gv': jnp.ones((D,), jnp.float32), 'bv': jnp.zeros((D,), jnp.float32), 'Wp': jax.random.normal(ks[4], (D, D), dtype=jnp.float32) * s, 'bp': jnp.zeros((D,), jnp.float32)}
    _L0_attn_in = _L0_attn_setup()

    def _L0_ffn_setup():
        import jax, jax.numpy as jnp
        import numpy as np
        TOP_K = 2
        key = jax.random.key(seed)
        ks = jax.random.split(key, 7)
        B, L, D, H, E, S = (2, 256, 128, 64, 16, 256)
        s = lambda fan_in: (1.0 / np.sqrt(fan_in)).astype(np.float32)
        return {'x': jax.random.normal(ks[0], (B, L, D), jnp.float32), 'gate_w': jax.random.normal(ks[1], (E, D), jnp.float32) * s(D), 'w1': jax.random.normal(ks[2], (E, H, D), jnp.float32) * s(D), 'w2': jax.random.normal(ks[3], (E, D, H), jnp.float32) * s(H), 'sfc1': jax.random.normal(ks[4], (S, D), jnp.float32) * s(D), 'sfc2': jax.random.normal(ks[5], (S, D), jnp.float32) * s(D), 'sfc3': jax.random.normal(ks[6], (D, S), jnp.float32) * s(S)}
    _L0_ffn_in = _L0_ffn_setup()

    def _L1_attn_setup():
        import jax, jax.numpy as jnp
        import numpy as np
        import math
        DIM = 128
        HEADS = 16
        HEAD_DIM = DIM // HEADS
        SCALE = math.sqrt(HEAD_DIM)

        def _heads(y, B, T):
            return y.reshape(B, T, HEADS, HEAD_DIM).transpose(0, 2, 1, 3)
        key = jax.random.key(seed)
        ks = jax.random.split(key, 7)
        B, T, C = (2, 256, DIM)
        w = 0.02
        return {'x': jax.random.normal(ks[0], (B, T, C), dtype=jnp.float32), 'W_Q': jax.random.normal(ks[1], (C, C), dtype=jnp.float32) * w, 'W_K': jax.random.normal(ks[2], (C, C), dtype=jnp.float32) * w, 'W_V': jax.random.normal(ks[3], (C, C), dtype=jnp.float32) * w, 'W_K_prime': jax.random.normal(ks[4], (C, C), dtype=jnp.float32) * w, 'W_O': jax.random.normal(ks[5], (C, C), dtype=jnp.float32) * w, 'alpha': jnp.float32(0.5)}
    _L1_attn_in = _L1_attn_setup()

    def _L1_ffn_setup():
        import jax, jax.numpy as jnp
        import numpy as np
        DIM = 128
        DEPTH = 2
        HEADS = 8
        DIM_HEAD = 64
        WINDOW = 64
        INNER = HEADS * DIM_HEAD
        HID = int(DIM * 4 * 2 / 3)
        B, N = (2, 1024)
        QK_SCALE = 8.0

        def shift_token(t):
            t1, t2 = jnp.split(t, 2, axis=-1)
            t2 = jnp.pad(t2, ((0, 0), (1, 0), (0, 0)))[:, :-1]
            return jnp.concatenate([t1, t2], axis=-1)

        def l2norm(t):
            return t / jnp.clip(jnp.linalg.norm(t, axis=-1, keepdims=True), 1e-12)

        def rotate_half(x):
            x1, x2 = jnp.split(x, 2, axis=-1)
            return jnp.concatenate([-x2, x1], axis=-1)

        def rotary_xpos(q, k):
            n = q.shape[-2]
            half_idx = jnp.arange(0, DIM_HEAD, 2, dtype=jnp.float32)
            inv_freq = 1.0 / 10000.0 ** (half_idx / DIM_HEAD)
            t = jnp.arange(n, dtype=jnp.float32)
            freqs = t[:, None] * inv_freq[None, :]
            freqs = jnp.concatenate([freqs, freqs], axis=-1)
            base = (half_idx + 0.4 * DIM_HEAD) / (1.4 * DIM_HEAD)
            power = (t - n // 2) / float(WINDOW // 2)
            scale = base[None, :] ** power[:, None]
            scale = jnp.concatenate([scale, scale], axis=-1)
            cos, sin = (jnp.cos(freqs), jnp.sin(freqs))
            q = q * cos * scale + rotate_half(q) * sin * scale
            k = k * cos / scale + rotate_half(k) * sin / scale
            return (q, k)

        def local_attention(q, k, v):
            b, h, n, d = q.shape
            w = n // WINDOW
            bq = q.reshape(b, h, w, WINDOW, d) * QK_SCALE
            bk = k.reshape(b, h, w, WINDOW, d)
            bv = v.reshape(b, h, w, WINDOW, d)

            def look_around(t):
                p = jnp.pad(t, ((0, 0), (0, 0), (1, 0), (0, 0), (0, 0)))
                return jnp.concatenate([p[:, :, :w], p[:, :, 1:]], axis=3)
            bk, bv = (look_around(bk), look_around(bv))
            bt = jnp.arange(n).reshape(w, WINDOW)
            btp = jnp.pad(bt, ((1, 0), (0, 0)), constant_values=-1)
            btk = jnp.concatenate([btp[:w], btp[1:]], axis=1)
            sim = jnp.einsum('bhwid,bhwjd->bhwij', bq, bk)
            i = bt[:, :, None]
            j = btk[:, None, :]
            mask = (i < j) | (i > j + WINDOW) | (j == -1)
            sim = jnp.where(mask, -jnp.finfo(sim.dtype).max, sim)
            attn = jax.nn.softmax(sim, axis=-1)
            out = jnp.einsum('bhwij,bhwjd->bhwid', attn, bv)
            return out.reshape(b, h, n, d)

        def _layer(x, wqkv, qs, ksc, wo, lg, lb, w1, b1, w2, b2):
            b, n, _ = x.shape
            h = shift_token(x)
            qkv = h @ wqkv
            q, k, v = jnp.split(qkv, 3, axis=-1)
            to_heads = lambda t: t.reshape(b, n, HEADS, DIM_HEAD).transpose(0, 2, 1, 3)
            q, k, v = (to_heads(q), to_heads(k), to_heads(v))
            q = l2norm(q) * qs
            k = l2norm(k) * ksc
            q, k = rotary_xpos(q, k)
            o = local_attention(q, k, v)
            o = o.transpose(0, 2, 1, 3).reshape(b, n, INNER)
            x = x + o @ wo
            h = shift_token(x)
            mu = h.mean(-1, keepdims=True)
            var = h.var(-1, keepdims=True)
            h = (h - mu) / jnp.sqrt(var + 1e-05) * lg + lb
            h = h @ w1 + b1
            a, g = jnp.split(h, 2, axis=-1)
            h = a * jax.nn.gelu(g, approximate=False)
            x = x + h @ w2 + b2
            return x
        key = jax.random.key(seed)
        ks = jax.random.split(key, 6)
        return {'x': jax.random.normal(ks[0], (B, N, DIM), jnp.float32), 'wqkv': jax.random.normal(ks[1], (DEPTH, DIM, 3 * INNER), jnp.float32) * 0.02, 'q_scale': jnp.ones((DEPTH, DIM_HEAD), jnp.float32), 'k_scale': jnp.ones((DEPTH, DIM_HEAD), jnp.float32), 'wo': jax.random.normal(ks[2], (DEPTH, INNER, DIM), jnp.float32) * 0.02, 'ln_g': jnp.ones((DEPTH, DIM), jnp.float32), 'ln_b': jnp.zeros((DEPTH, DIM), jnp.float32), 'w1': jax.random.normal(ks[3], (DEPTH, DIM, 2 * HID), jnp.float32) * 0.02, 'b1': jnp.zeros((DEPTH, 2 * HID), jnp.float32), 'w2': jax.random.normal(ks[4], (DEPTH, HID, DIM), jnp.float32) * 0.02, 'b2': jnp.zeros((DEPTH, DIM), jnp.float32)}
    _L1_ffn_in = _L1_ffn_setup()
    _d = {'L0_attn_x': _L0_attn_in['x'], 'L0_attn_Wq': _L0_attn_in['Wq'], 'L0_attn_gq': _L0_attn_in['gq'], 'L0_attn_bq': _L0_attn_in['bq'], 'L0_attn_Wk': _L0_attn_in['Wk'], 'L0_attn_gk': _L0_attn_in['gk'], 'L0_attn_bk': _L0_attn_in['bk'], 'L0_attn_Wv': _L0_attn_in['Wv'], 'L0_attn_gv': _L0_attn_in['gv'], 'L0_attn_bv': _L0_attn_in['bv'], 'L0_attn_Wp': _L0_attn_in['Wp'], 'L0_attn_bp': _L0_attn_in['bp'], 'L0_ffn_gate_w': _L0_ffn_in['gate_w'], 'L0_ffn_w1': _L0_ffn_in['w1'], 'L0_ffn_w2': _L0_ffn_in['w2'], 'L0_ffn_sfc1': _L0_ffn_in['sfc1'], 'L0_ffn_sfc2': _L0_ffn_in['sfc2'], 'L0_ffn_sfc3': _L0_ffn_in['sfc3'], 'L1_attn_W_Q': _L1_attn_in['W_Q'], 'L1_attn_W_K': _L1_attn_in['W_K'], 'L1_attn_W_V': _L1_attn_in['W_V'], 'L1_attn_W_K_prime': _L1_attn_in['W_K_prime'], 'L1_attn_W_O': _L1_attn_in['W_O'], 'L1_attn_alpha': _L1_attn_in['alpha'], 'L1_ffn_wqkv': _L1_ffn_in['wqkv'], 'L1_ffn_q_scale': _L1_ffn_in['q_scale'], 'L1_ffn_k_scale': _L1_ffn_in['k_scale'], 'L1_ffn_wo': _L1_ffn_in['wo'], 'L1_ffn_ln_g': _L1_ffn_in['ln_g'], 'L1_ffn_ln_b': _L1_ffn_in['ln_b'], 'L1_ffn_w1': _L1_ffn_in['w1'], 'L1_ffn_b1': _L1_ffn_in['b1'], 'L1_ffn_w2': _L1_ffn_in['w2'], 'L1_ffn_b2': _L1_ffn_in['b2']}
    _x0 = _d['L0_attn_x']
    _d['L0_attn_x'] = jax.random.normal(jax.random.fold_in(jax.random.key(seed), 1), (8, 512, 128), dtype=_x0.dtype)
    del _x0
    return _d

def reference(L0_attn_x, L0_attn_Wq, L0_attn_gq, L0_attn_bq, L0_attn_Wk, L0_attn_gk, L0_attn_bk, L0_attn_Wv, L0_attn_gv, L0_attn_bv, L0_attn_Wp, L0_attn_bp, L0_ffn_gate_w, L0_ffn_w1, L0_ffn_w2, L0_ffn_sfc1, L0_ffn_sfc2, L0_ffn_sfc3, L1_attn_W_Q, L1_attn_W_K, L1_attn_W_V, L1_attn_W_K_prime, L1_attn_W_O, L1_attn_alpha, L1_ffn_wqkv, L1_ffn_q_scale, L1_ffn_k_scale, L1_ffn_wo, L1_ffn_ln_g, L1_ffn_ln_b, L1_ffn_w1, L1_ffn_b1, L1_ffn_w2, L1_ffn_b2):

    def _L0_attn_ref(x, Wq, gq, bq, Wk, gk, bk, Wv, gv, bv, Wp, bp):
        import jax, jax.numpy as jnp
        import numpy as np
        DIM = 128
        NUM_HEADS = 16
        HEAD_DIM = DIM // NUM_HEADS
        TAU = 2.0
        V_TH = 1.0
        BN_EPS = 1e-05

        def _branch(x, W, gamma, beta):
            B, N, D = x.shape
            h = jnp.einsum('bnd,ed->bne', x, W)
            hf = h.reshape(B * N, D)
            mean = jnp.mean(hf, axis=0)
            var = jnp.var(hf, axis=0)
            hn = (hf - mean) * jax.lax.rsqrt(var + BN_EPS) * gamma + beta
            hn = hn.reshape(B, N, D)
            return jax.nn.sigmoid(4.0 * (hn - V_TH))

        def _heads(x):
            B, N, D = x.shape
            return x.reshape(B, N, NUM_HEADS, HEAD_DIM).transpose(0, 2, 1, 3)
        B, N, D = x.shape
        scale = HEAD_DIM ** (-0.5)
        q = _branch(x, Wq, gq, bq)
        k = _branch(x, Wk, gk, bk)
        v = _branch(x, Wv, gv, bv)
        qk = _heads(q * k) * scale
        v_h = _heads(v)
        vv = jnp.einsum('bhnd,bhne->bhde', v_h, v_h)
        out = jnp.einsum('bhnd,bhde->bhne', qk, vv)
        out = out.transpose(0, 2, 1, 3).reshape(B, N, D)
        return jnp.einsum('bnd,ed->bne', out, Wp) + bp

    def _L0_ffn_ref(x, gate_w, w1, w2, sfc1, sfc2, sfc3):
        import jax, jax.numpy as jnp
        import numpy as np
        TOP_K = 2
        B, L, D = x.shape
        E = gate_w.shape[0]
        shared = jnp.einsum('bls,ds->bld', jax.nn.silu(jnp.einsum('bld,sd->bls', x, sfc1)) * jnp.einsum('bld,sd->bls', x, sfc2), sfc3)
        logits = jnp.einsum('bld,ed->ble', x, gate_w)
        top_w, top_idx = jax.lax.top_k(logits, TOP_K)
        top_w = jax.nn.softmax(top_w, axis=-1)
        xf = x.reshape(-1, D)
        T = xf.shape[0]
        idx = top_idx.reshape(T, TOP_K)
        wk = top_w.reshape(T, TOP_K)
        dispatch = jnp.zeros((T, E), xf.dtype).at[jnp.arange(T)[:, None], idx].add(wk)
        h = jax.nn.silu(jnp.einsum('td,ehd->teh', xf, w1))
        moe = jnp.einsum('teh,te,edh->td', h, dispatch, w2)
        return moe.reshape(B, L, D) + shared

    def _L1_attn_ref(x, W_Q, W_K, W_V, W_K_prime, W_O, alpha):
        import jax, jax.numpy as jnp
        import numpy as np
        import math
        DIM = 128
        HEADS = 16
        HEAD_DIM = DIM // HEADS
        SCALE = math.sqrt(HEAD_DIM)

        def _heads(y, B, T):
            return y.reshape(B, T, HEADS, HEAD_DIM).transpose(0, 2, 1, 3)
        B, T, C = x.shape
        q = _heads(x @ W_Q.T, B, T)
        k = _heads(x @ W_K.T, B, T)
        v = _heads(x @ W_V.T, B, T)
        kp = _heads(x @ W_K_prime.T, B, T)
        scores = jnp.einsum('bhqd,bhkd->bhqk', q, k) / SCALE
        attn = jax.nn.softmax(scores, axis=-1)
        out_std = jnp.einsum('bhqk,bhkd->bhqd', attn, v)
        scores_p = jnp.einsum('bhqd,bhkd->bhqk', q, kp) / SCALE
        attn_p = jax.nn.softmax(scores_p, axis=-1)
        out_p = jnp.einsum('bhqk,bhkd->bhqd', attn_p, v)
        out = alpha * out_std + (1.0 - alpha) * out_p
        out = out.transpose(0, 2, 1, 3).reshape(B, T, C)
        return out @ W_O.T

    def _L1_ffn_ref(x, wqkv, q_scale, k_scale, wo, ln_g, ln_b, w1, b1, w2, b2):
        import jax, jax.numpy as jnp
        import numpy as np
        DIM = 128
        DEPTH = 2
        HEADS = 8
        DIM_HEAD = 64
        WINDOW = 64
        INNER = HEADS * DIM_HEAD
        HID = int(DIM * 4 * 2 / 3)
        B, N = (2, 1024)
        QK_SCALE = 8.0

        def shift_token(t):
            t1, t2 = jnp.split(t, 2, axis=-1)
            t2 = jnp.pad(t2, ((0, 0), (1, 0), (0, 0)))[:, :-1]
            return jnp.concatenate([t1, t2], axis=-1)

        def l2norm(t):
            return t / jnp.clip(jnp.linalg.norm(t, axis=-1, keepdims=True), 1e-12)

        def rotate_half(x):
            x1, x2 = jnp.split(x, 2, axis=-1)
            return jnp.concatenate([-x2, x1], axis=-1)

        def rotary_xpos(q, k):
            n = q.shape[-2]
            half_idx = jnp.arange(0, DIM_HEAD, 2, dtype=jnp.float32)
            inv_freq = 1.0 / 10000.0 ** (half_idx / DIM_HEAD)
            t = jnp.arange(n, dtype=jnp.float32)
            freqs = t[:, None] * inv_freq[None, :]
            freqs = jnp.concatenate([freqs, freqs], axis=-1)
            base = (half_idx + 0.4 * DIM_HEAD) / (1.4 * DIM_HEAD)
            power = (t - n // 2) / float(WINDOW // 2)
            scale = base[None, :] ** power[:, None]
            scale = jnp.concatenate([scale, scale], axis=-1)
            cos, sin = (jnp.cos(freqs), jnp.sin(freqs))
            q = q * cos * scale + rotate_half(q) * sin * scale
            k = k * cos / scale + rotate_half(k) * sin / scale
            return (q, k)

        def local_attention(q, k, v):
            b, h, n, d = q.shape
            w = n // WINDOW
            bq = q.reshape(b, h, w, WINDOW, d) * QK_SCALE
            bk = k.reshape(b, h, w, WINDOW, d)
            bv = v.reshape(b, h, w, WINDOW, d)

            def look_around(t):
                p = jnp.pad(t, ((0, 0), (0, 0), (1, 0), (0, 0), (0, 0)))
                return jnp.concatenate([p[:, :, :w], p[:, :, 1:]], axis=3)
            bk, bv = (look_around(bk), look_around(bv))
            bt = jnp.arange(n).reshape(w, WINDOW)
            btp = jnp.pad(bt, ((1, 0), (0, 0)), constant_values=-1)
            btk = jnp.concatenate([btp[:w], btp[1:]], axis=1)
            sim = jnp.einsum('bhwid,bhwjd->bhwij', bq, bk)
            i = bt[:, :, None]
            j = btk[:, None, :]
            mask = (i < j) | (i > j + WINDOW) | (j == -1)
            sim = jnp.where(mask, -jnp.finfo(sim.dtype).max, sim)
            attn = jax.nn.softmax(sim, axis=-1)
            out = jnp.einsum('bhwij,bhwjd->bhwid', attn, bv)
            return out.reshape(b, h, n, d)

        def _layer(x, wqkv, qs, ksc, wo, lg, lb, w1, b1, w2, b2):
            b, n, _ = x.shape
            h = shift_token(x)
            qkv = h @ wqkv
            q, k, v = jnp.split(qkv, 3, axis=-1)
            to_heads = lambda t: t.reshape(b, n, HEADS, DIM_HEAD).transpose(0, 2, 1, 3)
            q, k, v = (to_heads(q), to_heads(k), to_heads(v))
            q = l2norm(q) * qs
            k = l2norm(k) * ksc
            q, k = rotary_xpos(q, k)
            o = local_attention(q, k, v)
            o = o.transpose(0, 2, 1, 3).reshape(b, n, INNER)
            x = x + o @ wo
            h = shift_token(x)
            mu = h.mean(-1, keepdims=True)
            var = h.var(-1, keepdims=True)
            h = (h - mu) / jnp.sqrt(var + 1e-05) * lg + lb
            h = h @ w1 + b1
            a, g = jnp.split(h, 2, axis=-1)
            h = a * jax.nn.gelu(g, approximate=False)
            x = x + h @ w2 + b2
            return x
        for l in range(DEPTH):
            x = _layer(x, wqkv[l], q_scale[l], k_scale[l], wo[l], ln_g[l], ln_b[l], w1[l], b1[l], w2[l], b2[l])
        return x
    x = L0_attn_x
    x = x + _layernorm(_L0_attn_ref(_layernorm(x, axis=-1), L0_attn_Wq, L0_attn_gq, L0_attn_bq, L0_attn_Wk, L0_attn_gk, L0_attn_bk, L0_attn_Wv, L0_attn_gv, L0_attn_bv, L0_attn_Wp, L0_attn_bp), axis=-1)
    x = x + _layernorm(_L0_ffn_ref(_layernorm(x, axis=-1), L0_ffn_gate_w, L0_ffn_w1, L0_ffn_w2, L0_ffn_sfc1, L0_ffn_sfc2, L0_ffn_sfc3), axis=-1)
    x = x + _layernorm(_L1_attn_ref(_layernorm(x, axis=-1), L1_attn_W_Q, L1_attn_W_K, L1_attn_W_V, L1_attn_W_K_prime, L1_attn_W_O, L1_attn_alpha), axis=-1)
    x = x + _layernorm(_L1_ffn_ref(_layernorm(x, axis=-1), L1_ffn_wqkv, L1_ffn_q_scale, L1_ffn_k_scale, L1_ffn_wo, L1_ffn_ln_g, L1_ffn_ln_b, L1_ffn_w1, L1_ffn_b1, L1_ffn_w2, L1_ffn_b2), axis=-1)
    return x

_drawn_inputs = setup_inputs


def setup_inputs(seed=0):
    import zlib

    import numpy as np

    out = dict(_drawn_inputs(seed))
    spreads = {'L0_attn_gq': (1.0, 0.2),
     'L0_attn_bq': (0.0, 0.1),
     'L0_attn_gk': (1.0, 0.2),
     'L0_attn_bk': (0.0, 0.1),
     'L0_attn_gv': (1.0, 0.2),
     'L0_attn_bv': (0.0, 0.1),
     'L0_attn_bp': (0.0, 0.1),
     'L1_ffn_q_scale': (1.0, 0.6),
     'L1_ffn_k_scale': (1.0, 0.6),
     'L1_ffn_ln_g': (1.0, 0.6),
     'L1_ffn_ln_b': (0.0, 0.8),
     'L1_ffn_b1': (0.0, 0.8),
     'L1_ffn_b2': (0.0, 2.0)}
    factors = {'L1_attn_W_Q': 8.0,
     'L1_attn_W_K': 8.0,
     'L1_attn_W_K_prime': 8.0,
     'L1_ffn_w1': 8.0,
     'L1_ffn_w2': 8.0}
    for name, (base, spread) in spreads.items():
        noise = np.random.default_rng([zlib.crc32(name.encode()), seed]).standard_normal(out[name].shape)
        drawn = base * np.exp(spread * noise) if base else spread * noise
        out[name] = jnp.asarray(drawn.astype(out[name].dtype))
    for name, factor in factors.items():
        out[name] = (out[name] * factor).astype(out[name].dtype)
    return out
```

```python
from contextlib import ExitStack

import numpy as np
import concourse.bass as bass
from concourse import mybir

ALU = mybir.AluOpType
ACT = mybir.ActivationFunctionType
AX = mybir.AxisListType
F32 = mybir.dt.float32
F32R = mybir.dt.float32r
BF16 = mybir.dt.bfloat16
U32 = mybir.dt.uint32

P = 128
B, N, D = 8, 512, 128
T = N // P
EPS = 1e-5
NEG = -1e30

EXPERTS, HID_E, SHARED = 16, 64, 256
UNITS = SHARED // P + EXPERTS * HID_E // P
HEADS, HD = 16, 8
G = HEADS // 4
LAYERS, LH, LD = 2, 8, 64
INNER = LH * LD
PAIRS = LH // 2
BACK = 64
HID_F = 341
FF = [(0, 128), (128, 128), (256, HID_F - 256)]


class Signal:

    def __init__(self, sem, per):
        self.sem, self.per = sem, per

    def at(self, b, k):
        return b * self.per + k


def build(nc, x, wl0, gb, bp, gate, ew_a, ew_u, ew_d, wl1, alpha, wqkv, qks, wo, lngb, fw1, fb1, fw2, fb2,
          c_mat, c_sel, c_band, c_small, c_rot, out):
    ctx = ExitStack()
    with ctx:
        def sb(name, shape, dt=F32):
            return ctx.enter_context(nc.sbuf_tensor(name, shape, dt))

        def signal(name, per=1):
            return Signal(ctx.enter_context(nc.semaphore(name)), per)

        ps = ctx.enter_context(nc.psum_tensor("ps", [P, 8, 512], F32))

        arena = ctx.enter_context(nc.sbuf_tensor("arena", [P, 8192], F32))

        arena2 = ctx.enter_context(nc.sbuf_tensor("arena2", [P, 4096], F32))

        def part(start, *dims, arena=arena):
            names = "abcdef"[:len(dims)]
            size = int(np.prod(dims))
            flat = arena[:, start:start + size]
            if len(dims) == 1:
                return flat
            return flat.rearrange(f"p ({' '.join(names)}) -> p {' '.join(names)}", **dict(zip(names, dims)))

        w0 = sb("w0", [P, 4, D])
        gb_sb = sb("gb_sb", [P, 6])
        bp_sb = sb("bp_sb", [P, D])
        gate_sb = sb("gate_sb", [P, EXPERTS])
        wa_sb = sb("wa_sb", [P, UNITS, P])
        wu_sb = sb("wu_sb", [P, 2, P])
        wd_sb = sb("wd_sb", [P, UNITS, D])
        w1_in = part(2560, 3, D)
        w1_sb = sb("w1_sb", [P, 2, D])
        waug = sb("waug", [P, 3, G, 4, 4, HD])
        alpha_sb = sb("alpha_sb", [P, 2])
        wqkv_sb = sb("wqkv_sb", [P, LAYERS, 3, INNER])
        qks_sb = sb("qks_sb", [P, LAYERS, 2, LD])
        wo_sb = sb("wo_sb", [P, LAYERS, PAIRS, D])
        lngb_sb = sb("lngb_sb", [P, LAYERS, 2])
        fw1_sb = sb("fw1_sb", [P, LAYERS, 2 * HID_F])
        fb1_sb = sb("fb1_sb", [P, LAYERS, 2, 3])
        fw2_sb = sb("fw2_sb", [P, LAYERS, 3, D])
        fb2_sb = sb("fb2_sb", [P, LAYERS, D])
        mats = sb("mats", [P, 4, P])
        ident, shift, carry, blocks = (mats[:, i, :] for i in range(4))
        ident_bf = sb("ident_bf", [P, P], BF16)
        sel_f = part(0, 8, P)[0:3 * EXPERTS]
        sel = sb("sel", [3 * EXPERTS, 8, P], BF16)
        band_f = part(1024, 2, BACK + P)
        band = sb("band", [P, 2, BACK + P], BF16)
        small = sb("small", [P, 81])
        half_neg = small[:, 0:16]
        iota = small[:, 16:32]
        one_at_hd, zero = small[:, 48:80], small[:, 80:81]
        q_low, k_low, kp_low, k_one, kp_one = (small[:, 32 + i:33 + i] for i in range(5))
        rot_in = part(1536, 4, T, LD)
        rot = sb("rot", [P, LAYERS, 4, T, LD])

        h_stats = sb("h_stats", [P, 3, B, 6])
        h_mv = sb("h_mv", [P, 3, 2])
        bn = sb("bn", [P, 5, 3])
        sig = part(2048, 3, N, arena=arena2)
        vv = sb("vv", [P, D])
        vvw = sb("vvw", [P, D])

        x_in = sb("x_in", [P, T, D])
        xa = sb("xa", [P, T, D])
        xb = sb("xb", [P, T, D])
        xc = sb("xc", [P, T, D])
        o_rows = sb("o_rows", [P, T, D])
        xn = sb("xn", [P, T, D])
        xT = sb("xT", [P, N])
        hT = sb("hT", [P, N])
        y = sb("y", [P, T, D])
        ln_st = sb("ln_st", [P, T, 6])
        ln_mv = sb("ln_mv", [P, T, 2])
        ln_ve = sb("ln_ve", [P, T])
        ln_rs = sb("ln_rs", [P, T])

        logit = sb("logit", [P, T, EXPERTS])
        top_v = sb("top_v", [P, T, 8])
        top_i = sb("top_i", [P, T, 8], U32)
        top_if = sb("top_if", [P, T, 2])
        top_d = sb("top_d", [P, T])
        top_w = sb("top_w", [P, 2, T])
        disp = sb("disp", [P, 4, T, EXPERTS])
        disp_p = sb("disp_p", [P, T, 3 * EXPERTS], BF16)
        disp_T = sb("disp_T", [3 * EXPERTS, N], BF16)
        act_h = sb("act_h", [P, 2, N])
        v_rows = act_h[:, 0, :].rearrange("p (t d) -> p t d", t=T)
        hid = sb("hid", [P, 2, N])

        rnd = sb("rnd", [P, 2, N], F32R)
        qz = sb("qz", [P, HEADS, N], F32R)
        kk = sb("kk", [P, 2, G, N], F32R)
        v_aug = part(0, T, HEADS, 32, arena=arena2)
        mx = sb("mx", [P, 2, T, 8])
        mxT = sb("mxT", [8, 2, N], F32R)
        prob = part(0, 2, 4, 2, N)
        oT = sb("oT", [P, N])
        rec = sb("rec", [P, T, 4])
        o_nrm = sb("o_nrm", [P, T, 4, HD])
        att = o_rows

        sq = part(0, 2, INNER)
        ssq = sb("ssq", [P, 2, LH])
        rn = sb("rn", [P, T, 2, LH])
        ra = part(1024, LH, LD)
        rb = part(1536, LH, LD)
        qk_rows = part(2048, 2, INNER)
        q_bd = part(0, LH, N, arena=arena2)
        kT = part(3072, PAIRS, N)
        v_loc = part(5120, T, INNER)
        l_mx = sb("l_mx", [P, LH])
        l_sc = sb("l_sc", [P, LH])
        l_nb = sb("l_nb", [P, LH])
        l_sum = sb("l_sum", [P, LH])
        l_rec = sb("l_rec", [P, LH])
        l_p = sb("l_p", [P, LH, 2 * P])
        l_pT = part(7168, 2, 2, 2, P)
        l_oT = oT[:, :].rearrange("p (a n) -> p a n", a=PAIRS)

        s_w = signal("s_w")
        s_const = signal("s_const")
        s_zero = signal("s_zero")
        p_x = signal("p_x", 16)
        p_used = signal("p_used")
        p_var = signal("p_var")
        p_rstd = signal("p_rstd")
        p_rows = signal("p_rows")
        p_turned = signal("p_turned")
        p_cols = signal("p_cols")
        p_h = signal("p_h", 3)
        p_kept = signal("p_kept", 3)
        p_store = signal("p_store", 16)
        p_stat = signal("p_stat", 3)
        n_var = signal("n_var")
        n_rstd = signal("n_rstd")
        n_aff = signal("n_aff")

        NORMS = 5 + 1 + LAYERS + 1
        s_x = signal("s_x", 16)
        s_h = signal("s_h", 16)
        s_xused = signal("s_xused")
        s_var = signal("s_var", NORMS)
        s_rstd = signal("s_rstd", NORMS)
        TURNS = 4 + 2 * LAYERS
        s_rows = signal("s_rows", TURNS - 1)
        s_turned = signal("s_turned", TURNS)
        s_cols = signal("s_cols", TURNS)
        s_vone = signal("s_vone")
        s_qzero = signal("s_qzero")
        s_sig = signal("s_sig", 3)
        s_qk = signal("s_qk")
        s_vvps = signal("s_vvps")
        s_vv = signal("s_vv")
        s_vvwps = signal("s_vvwps")
        s_vvw = signal("s_vvw")
        s_oput = signal("s_oput")
        s_logit = signal("s_logit")
        s_top = signal("s_top")
        s_topw = signal("s_topw")
        s_disp = signal("s_disp")
        s_dispps = signal("s_dispps")
        s_dispT = signal("s_dispT")
        s_up = signal("s_up", UNITS)
        s_silu = signal("s_silu", UNITS)
        s_hid = signal("s_hid", UNITS)
        s_down = signal("s_down", UNITS)
        s_vps = signal("s_vps")
        s_vaug = signal("s_vaug")
        s_proj = signal("s_proj", 3 * G)
        s_rnd = signal("s_rnd", 3 * G)
        s_part = signal("s_part", 3 * G)
        s_aps = signal("s_aps", 2 * HEADS * T)
        s_amax = signal("s_amax", 2 * HEADS * T)
        s_mps = signal("s_mps", G)
        s_mT = signal("s_mT", G)
        s_shift = signal("s_shift", 16 * HEADS)
        s_sps = signal("s_sps", 4 * 4 * G)
        s_exp = signal("s_exp", 4 * 4 * G)
        s_pv = signal("s_pv", 4 * G)
        s_oT = signal("s_oT", 2 * G)
        s_ops = signal("s_ops", 2 * G)
        s_onrm = signal("s_onrm", 2 * G)
        s_lout = signal("s_lout")
        l_qkv = signal("l_qkv", LAYERS * T)
        l_sq = signal("l_sq", LAYERS * T)
        l_v = signal("l_v", LAYERS * T)
        l_ss = signal("l_ss", LAYERS * T)
        l_rn = signal("l_rn", LAYERS * T)
        l_rot = signal("l_rot", LAYERS * T)
        l_qkps = signal("l_qkps", LAYERS * T)
        l_qT = signal("l_qT", LAYERS * T)
        l_kT = signal("l_kT", LAYERS * T)
        l_s = signal("l_s", LAYERS * T * PAIRS)
        l_max = signal("l_max", LAYERS * T)
        l_exp = signal("l_exp", LAYERS * T)
        l_r = signal("l_r", LAYERS * T)
        l_pn = signal("l_pn", LAYERS * T)
        l_pps = signal("l_pps", LAYERS * T * PAIRS)
        l_pta = signal("l_pta", LAYERS * T * PAIRS // 2)
        l_ptb = signal("l_ptb", LAYERS * T * PAIRS // 2)
        l_pv = signal("l_pv", LAYERS * T * PAIRS)
        l_o = signal("l_o", LAYERS * T)
        l_wo = signal("l_wo", LAYERS * T)
        l_res = signal("l_res", LAYERS * T)
        l_shps = signal("l_shps", LAYERS)
        l_sh = signal("l_sh", LAYERS)
        f_up = signal("f_up", LAYERS * 3)
        f_act = signal("f_act", LAYERS * 3)
        f_hid = signal("f_hid", LAYERS * 3)
        f_down = signal("f_down", LAYERS * 3)
        s_final = signal("s_final")
        s_out = signal("s_out", 16)

        x_rows = x.rearrange("b (t p) d -> b p t d", p=P)
        h_dram = nc.dram_tensor("h_dram", (B, P, 3, N), F32, kind="Internal").ap()
        out_rows = out.rearrange("b (t p) d -> b p t d", p=P)

        LOADS = [(w0[:], wl0), (gb_sb[:], gb), (bp_sb[:], bp), (gate_sb[:], gate), (wa_sb[:], ew_a), (wu_sb[:], ew_u),
                 (wd_sb[:], ew_d), (w1_in, wl1[:, 0:3, :]), (w1_sb[:], wl1[:, 3:5, :]), (alpha_sb[:, 0:1], alpha), (wqkv_sb[:], wqkv), (qks_sb[:], qks),
                 (wo_sb[:], wo), (lngb_sb[:], lngb), (fw1_sb[:], fw1), (fb1_sb[:], fb1), (fw2_sb[:], fw2),
                 (fb2_sb[:], fb2), (mats[:], c_mat), (sel_f, c_sel), (band_f, c_band), (small[:], c_small),
                 (rot_in, c_rot)]
        LOADED = 16 * len(LOADS)

        block = ctx.enter_context(nc.Block())

        STEPS, LEAD = 2 * G, 3

        @block.sync
        def _(sp):
            for dst, src in LOADS:
                sp.dma_start(dst, src).then_inc(s_w.sem, 16)

            def load_x(b, loaded):
                sp.dma_start(x_in[:, :, :], x_rows[bass.ds(b, 1), :, :, :].rearrange("o p t d -> (o p) t d"))\
                    .then_inc(loaded.sem, 16)

            def load_h(b):
                sp.dma_start(sig[:, :, :], h_dram[bass.ds(b, 1), :, :, :].rearrange("o p i n -> (o p) i n"))\
                    .then_inc(s_h.sem, 16)

            def store_h(b):
                sp.wait_ge(p_kept.sem, p_kept.at(b, 3))
                sp.dma_start(h_dram[bass.ds(b, 1), :, :, :].rearrange("o p i n -> (o p) i n"), sig[:, :, :])\
                    .then_inc(p_store.sem, 16)

            def place_shifts(b):
                for g in range(G):
                    sp.wait_ge(s_mT.sem, s_mT.at(b, g + 1))
                    for j in range(4):
                        sp.dma_start(qz[32 * j + 24:32 * j + 26, 4 * g + j, :].bitcast(F32),
                                     mxT[2 * j:2 * j + 2, g % 2, :].bitcast(F32)).then_inc(s_shift.sem, 16)

            def store_out(b):
                sp.wait_ge(s_final.sem, s_final.at(b, 1))
                sp.dma_start(out_rows[bass.ds(b, 1), :, :, :].rearrange("o p t d -> (o p) t d"), xa[:, :, :])\
                    .then_inc(s_out.sem, 16)

            load_x(0, p_x)
            with sp.Fori(0, B - 1) as b:
                sp.wait_ge(p_used.sem, p_used.at(b, 1))
                load_x(b + 1, p_x)
                store_h(b)
            store_h(B - 1)
            sp.wait_ge(p_used.sem, p_used.at(B, 0))
            load_x(0, s_x)
            sp.wait_ge(p_store.sem, p_store.at(B, 0))
            sp.wait_ge(p_stat.sem, p_stat.at(B, 0))
            load_h(0)
            with sp.Fori(0, B - 1) as b:
                place_shifts(b)
                sp.wait_ge(s_xused.sem, s_xused.at(b, 1))
                load_x(b + 1, s_x)
                sp.wait_ge(l_s.sem, l_s.at(b, l_s.per))
                load_h(b + 1)
                store_out(b)
            place_shifts(B - 1)
            store_out(B - 1)
            sp.wait_ge(s_out.sem, s_out.at(B, 0))

        @block.gpsimd
        def _(pool):
            pool.memset(qz[:, :, :].bitcast(F32), 0.0)
            pool.memset(l_p[:, :, :], 0.0)
            pool.drain()
            pool.memset(hT[64:P, 0:1], 0.0)
            pool.drain().then_inc(s_zero.sem, 1)
            pool.wait_ge(s_w.sem, LOADED)
            with pool.Fori(0, B) as b:
                pool.wait_ge(p_var.sem, p_var.at(b, 1))
                pool.tensor_tensor(ln_rs[:, :], ln_ve[:, :], half_neg[:, 0:T], ALU.pow).then_inc(p_rstd.sem, 1)
            pool.wait_ge(n_var.sem, 1)
            pool.tensor_tensor(bn[:, 1, :], bn[:, 0, :], half_neg[:, 0:3], ALU.pow).then_inc(n_rstd.sem, 1)

            with pool.Fori(0, B) as b:
                def rstd(k):
                    pool.wait_ge(s_var.sem, s_var.at(b, k))
                    pool.tensor_tensor(ln_rs[:, :], ln_ve[:, :], half_neg[:, 0:T], ALU.pow).then_inc(s_rstd.sem, 1)

                pool.tensor_tensor(v_aug[:, :, :, :].rearrange("p t h c -> p (t h) c"),
                                   one_at_hd.unsqueeze(1).to_broadcast([P, T * HEADS, 32]),
                                   zero.unsqueeze(2).to_broadcast([P, T * HEADS, 32]), ALU.add).then_inc(s_vone.sem, 1)
                for k in range(1, 5):
                    rstd(k)
                pool.wait_ge(s_pv.sem, s_pv.at(b, 4 * G))
                zero_b = zero.to_broadcast([P, LH * N])
                pool.tensor_tensor(q_bd[:, :, :].rearrange("p h n -> p (h n)"), zero_b, zero_b, ALU.add)\
                    .then_inc(s_qzero.sem, 1)
                rstd(5)
                rstd(6)
                for l in range(LAYERS):
                    for t in range(T):
                        i = l * T + t + 1
                        pool.wait_ge(l_ss.sem, l_ss.at(b, i))
                        pool.tensor_tensor(rn[:, t, :, :], ssq[:, :, :],
                                           half_neg.rearrange("p (a h) -> p a h", a=2), ALU.pow).then_inc(l_rn.sem, 1)
                    for t in range(T):
                        i = l * T + t + 1
                        lo = P if t == 0 else BACK
                        pool.wait_ge(l_r.sem, l_r.at(b, i))
                        w = 2 * P - lo
                        pool.tensor_tensor(l_p[:, :, lo:2 * P], l_p[:, :, lo:2 * P],
                                           l_rec[:, :].unsqueeze(2).to_broadcast([P, LH, w]), ALU.mult)\
                            .then_inc(l_pn.sem, 1)
                    rstd(7 + l)
                rstd(NORMS)
                pool.wait_ge(l_s.sem, l_s.at(b, l_s.per))

        @block.scalar
        def _(act):
            act.wait_ge(s_zero.sem, 1)
            with act.Fori(0, B) as b:
                act.wait_ge(p_turned.sem, p_turned.at(b, 1))
                act.copy(xT[:, :], ps[:, 0, :]).then_inc(p_cols.sem, 1)
                for i in range(3):
                    act.wait_ge(p_h.sem, p_h.at(b, i + 1))
                    act.copy(sig[:, i, :], ps[:, 1 + i, :]).then_inc(p_kept.sem, 1)
                act.wait_ge(p_store.sem, p_store.at(b, 16))
                act.wait_ge(p_stat.sem, p_stat.at(b, 3))
            act.wait_ge(n_aff.sem, 1)
            with act.Fori(0, B) as b:
                def columns(k, dst):
                    act.wait_ge(s_turned.sem, s_turned.at(b, k))
                    act.copy(dst, ps[:, 0, :]).then_inc(s_cols.sem, 1)

                act.wait_ge(s_h.sem, s_h.at(b, 16))
                for i in range(3):
                    act.activation(sig[:, i, :], sig[:, i, :], ACT.Sigmoid,
                                   bias=bn[:, 3, i:i + 1], scale=bn[:, 2, i:i + 1]).then_inc(s_sig.sem, 1)
                act.wait_ge(s_turned.sem, s_turned.at(b, 1))
                act.copy(act_h[:, 0, :], ps[:, 0, :]).then_inc(s_cols.sem, 1)
                act.wait_ge(s_vvwps.sem, s_vvwps.at(b, 1))
                act.copy(vvw[:, :], ps[:, 1, P:2 * P]).then_inc(s_vvw.sem, 1)

                columns(2, xT[:, :])
                act.wait_ge(s_top.sem, s_top.at(b, 1))
                act.activation(top_w[:, 0, :], top_d[:, :], ACT.Sigmoid, scale=-1.0)
                act.activation(top_w[:, 1, :], top_d[:, :], ACT.Sigmoid).then_inc(s_topw.sem, 1)
                for n in range(UNITS):
                    if n == 2:
                        act.wait_ge(s_dispps.sem, s_dispps.at(b, 1))
                        act.copy(disp_T[:, :], ps[0:3 * EXPERTS, 5, :]).then_inc(s_dispT.sem, 1)
                    act.wait_ge(s_up.sem, s_up.at(b, n + 1))
                    if n >= 2:
                        act.wait_ge(s_hid.sem, s_hid.at(b, n - 1))
                    act.activation(act_h[:, n % 2, :], ps[:, 1 + n % 2, :], ACT.Silu).then_inc(s_silu.sem, 1)

                columns(3, xT[:, :])
                act.wait_ge(s_vone.sem, s_vone.at(b, 1))
                act.wait_ge(s_vps.sem, s_vps.at(b, 1))
                act.copy(v_aug[:, :, :, 0:HD], ps[:, 7, :].rearrange("p (t h d) -> p t h d", t=T, d=HD))\
                    .then_inc(s_vaug.sem, 1)
                for i in range(3 * G):
                    act.wait_ge(s_proj.sem, s_proj.at(b, i + 1))
                    if i >= 2:
                        act.wait_ge(s_part.sem, s_part.at(b, i - 1))
                    act.activation(rnd[:, i % 2, :], ps[:, 1 + i % 2, :], ACT.Identity,
                                   bias=(0.0, k_one, kp_one)[i % 3]).then_inc(s_rnd.sem, 1)

                def shifts(g):
                    act.wait_ge(s_mps.sem, s_mps.at(b, g + 1))
                    if g >= 2:
                        act.wait_ge(s_shift.sem, s_shift.at(b, 64 * (g - 1)))
                    act.copy(mxT[:, g % 2, :], ps[0:8, 7, :]).then_inc(s_mT.sem, 1)

                shifts(0)
                for u in range(2 * STEPS):
                    s, half = divmod(u, 2)
                    for j in range(4):
                        n = 4 * u + j
                        if j == 0 and u >= 2:
                            act.wait_ge(s_pv.sem, s_pv.at(b, u - 1))
                        act.wait_ge(s_sps.sem, s_sps.at(b, n + 1))
                        act.activation(prob[:, u % 2, j, :, :].rearrange("p k n -> p (k n)"),
                                       ps[:, 2 * (n % 2):2 * (n % 2) + 2, :].rearrange("p k n -> p (k n)"),
                                       ACT.Exp, scale=HD ** -0.5).then_inc(s_exp.sem, 1)
                        if (half, j) == (0, 1) and s % 2 and s // 2 + 1 < G:
                            shifts(s // 2 + 1)
                    if half == 0 and s >= 1:
                        act.wait_ge(s_pv.sem, s_pv.at(b, u))
                        if s >= 2:
                            act.wait_ge(s_ops.sem, s_ops.at(b, s - 1))
                        act.copy(oT[:, :], ps[:, 6, :]).then_inc(s_oT.sem, 1)
                act.wait_ge(s_pv.sem, s_pv.at(b, 2 * STEPS))
                act.wait_ge(s_ops.sem, s_ops.at(b, STEPS - 1))
                act.copy(oT[:, :], ps[:, 6, :]).then_inc(s_oT.sem, 1)
                columns(4, xT[:, :])

                act.wait_ge(s_qzero.sem, s_qzero.at(b, 1))
                for l in range(LAYERS):
                    act.wait_ge(s_turned.sem, s_turned.at(b, 5 + 2 * l))
                    act.copy(hT[0:64, :], ps[0:64, 0, :])
                    act.copy(hT[64:P, 1:N], ps[64:P, 0, 0:N - 1]).then_inc(s_cols.sem, 1)

                    def turned_q(t):
                        act.wait_ge(l_qkps.sem, l_qkps.at(b, l * T + t + 1))
                        for e in range(2):
                            r = slice(64 * e, 64 * e + 64)
                            last = act.copy(q_bd[r, e:LH:2, t * P:(t + 1) * P],
                                            ps[r, 6, :].rearrange("p (a n) -> p a n", a=PAIRS))
                        last.then_inc(l_qT.sem, 1)

                    for t in range(T):
                        i = l * T + t + 1
                        q3 = 3 * (t % 2)
                        act.wait_ge(l_qkv.sem, l_qkv.at(b, i))
                        if t >= 1:
                            act.wait_ge(l_ss.sem, l_ss.at(b, i - 1))
                        act.activation(sq[:, 0, :], ps[:, q3, :], ACT.Square)
                        act.activation(sq[:, 1, :], ps[:, q3 + 1, :], ACT.Square).then_inc(l_sq.sem, 1)
                        act.copy(v_loc[:, t, :], ps[:, q3 + 2, :]).then_inc(l_v.sem, 1)
                        if t >= 1:
                            turned_q(t - 1)
                    turned_q(T - 1)
                    for t in range(T):
                        i = l * T + t + 1
                        lo = P if t == 0 else BACK
                        act.wait_ge(l_max.sem, l_max.at(b, i))
                        for h in range(LH):
                            o = (BACK + P) * (h % 2)
                            last = act.activation(l_p[:, h, lo:2 * P], ps[:, h // 2, o + lo - BACK:o + BACK + P], ACT.Exp,
                                               bias=l_nb[:, h:h + 1], scale=l_sc[:, h:h + 1],
                                               accum_out=l_sum[:, h:h + 1])
                        last.then_inc(l_exp.sem, 1)
                        for a in range(0, PAIRS, 2):
                            n = (i - 1) * PAIRS + a + 1
                            act.wait_ge(l_pps.sem, l_pps.at(b, n))
                            if a >= 2:
                                act.wait_ge(l_pv.sem, l_pv.at(b, n - 2))
                            act.copy(l_pT[:, 0, :, :, :].rearrange("p e k n -> p (e k n)"), ps[:, 4, :])\
                                .then_inc(l_pta.sem, 1)
                        act.wait_ge(l_pv.sem, l_pv.at(b, i * PAIRS))
                        act.copy(l_oT[:, :, :].rearrange("p a n -> p (a n)"), ps[:, 6, :]).then_inc(l_o.sem, 1)
                    act.wait_ge(l_shps.sem, l_shps.at(b, l + 1))
                    act.copy(xn[:, :, 64:P], ps[:, 1, 0:T * 64].rearrange("p (t d) -> p t d", t=T)).then_inc(l_sh.sem, 1)
                    act.wait_ge(s_turned.sem, s_turned.at(b, 6 + 2 * l))
                    act.activation(xT[:, :], ps[:, 0, :], ACT.Identity, bias=lngb_sb[:, l, 1:2],
                                   scale=lngb_sb[:, l, 0:1]).then_inc(s_cols.sem, 1)
                    for c, (_, m) in enumerate(FF):
                        i = 3 * l + c + 1
                        act.wait_ge(f_up.sem, f_up.at(b, i))
                        if c >= 2:
                            act.wait_ge(f_hid.sem, f_hid.at(b, i - 2))
                        act.activation(act_h[0:m, c % 2, :], ps[0:m, 2 + 2 * (c % 2), :], ACT.Gelu,
                                       bias=fb1_sb[0:m, l, 1, c:c + 1]).then_inc(f_act.sem, 1)

        @block.vector
        def _(dve):
            dve.wait_ge(s_w.sem, LOADED)
            dve.memset(waug[:, :, :, :, :, :], 0.0)
            dve.tensor_copy(ident_bf[:, :], ident)
            dve.tensor_copy(sel[:, :, :], sel_f[:, :, :])
            dve.tensor_copy(band[:, :, :], band_f[:, :, :])
            dve.tensor_scalar(alpha_sb[:, 1:2], alpha_sb[:, 0:1], -1.0, 1.0, ALU.mult, ALU.add)
            dve.drain()
            for i in range(3):
                for r in range(3):
                    dve.tensor_copy(waug[:, i, :, :, r, :],
                                    w1_in[:, i, :].rearrange("p (g j d) -> p g j d", g=G, d=HD))
            H = LD // 2
            for l in range(LAYERS):
                for i in range(2):
                    sc = qks_sb[:, l, i, :].unsqueeze(1).to_broadcast([P, T, LD])
                    dve.tensor_tensor(rot[:, l, 2 * i, :, :], rot_in[:, 2 * i, :, :], sc, ALU.mult)
                    for a in range(2):
                        dve.tensor_tensor(rot[:, l, 2 * i + 1, :, a * H:(a + 1) * H],
                                          rot_in[:, 2 * i + 1, :, a * H:(a + 1) * H],
                                          qks_sb[:, l, i, (1 - a) * H:(2 - a) * H].unsqueeze(1).to_broadcast([P, T, H]),
                                          ALU.mult)
            dve.drain().then_inc(s_const.sem, 1)

            def moments(src, var):
                for t in range(T):
                    dve.bn_stats(ln_st[:, t, :], src[:, t, :])
                dve.drain()
                for t in range(T):
                    dve.bn_aggr(ln_mv[:, t, :], ln_st[:, t, :])
                dve.drain()
                dve.tensor_scalar(ln_ve[:, :], ln_mv[:, :, 1], EPS, None, ALU.add).then_inc(var.sem, 1)

            def normed(src, dst):
                for t in range(T):
                    dve.tensor_scalar(dst[:, t, :], src[:, t, :], ln_mv[:, t, 0:1], ln_rs[:, t:t + 1],
                                      ALU.subtract, ALU.mult)
                dve.drain()

            with dve.Fori(0, B) as b:
                dve.wait_ge(p_x.sem, p_x.at(b, 16))
                moments(x_in, p_var)
                dve.wait_ge(p_rstd.sem, p_rstd.at(b, 1))
                normed(x_in, xn)
                dve.drain().then_inc(p_rows.sem, 1)
                dve.drain().then_inc(p_used.sem, 1)
                for i in range(3):
                    dve.wait_ge(p_kept.sem, p_kept.at(b, i + 1))
                    dve.bn_stats(h_stats[:, i, bass.ds(b, 1), :].rearrange("p o s -> p (o s)"), sig[:, i, :])\
                        .then_inc(p_stat.sem, 1)
                dve.wait_ge(p_turned.sem, p_turned.at(b, 1))
            dve.drain()
            for i in range(3):
                dve.bn_aggr(h_mv[:, i, :], h_stats[:, i, :, :].rearrange("p b s -> p (b s)"))
            dve.drain()
            dve.tensor_scalar(bn[:, 0, :], h_mv[:, :, 1], EPS, None, ALU.add).then_inc(n_var.sem, 1)
            dve.wait_ge(n_rstd.sem, 1)
            dve.scalar_tensor_tensor(bn[:, 2, :], bn[:, 1, :], 4.0, gb_sb[:, 0:6:2], ALU.mult, ALU.mult)
            dve.tensor_scalar(bn[:, 4, :], gb_sb[:, 1:6:2], 4.0, -4.0, ALU.mult, ALU.add)
            dve.drain()
            dve.tensor_tensor(bn[:, 0, :], bn[:, 2, :], h_mv[:, :, 0], ALU.mult)
            dve.drain()
            dve.tensor_tensor(bn[:, 3, :], bn[:, 4, :], bn[:, 0, :], ALU.subtract).then_inc(n_aff.sem, 1)

            with dve.Fori(0, B) as b:
                def norm(k, src, dst):
                    moments(src, s_var)
                    dve.wait_ge(s_rstd.sem, s_rstd.at(b, k))
                    normed(src, dst)

                def rows_ready():
                    dve.drain().then_inc(s_rows.sem, 1)

                dve.wait_ge(s_sig.sem, s_sig.at(b, 2))
                dve.tensor_tensor(sig[:, 0, :], sig[:, 0, :], sig[:, 1, :], ALU.mult).then_inc(s_qk.sem, 1)
                dve.wait_ge(s_vvps.sem, s_vvps.at(b, 1))
                dve.tensor_tensor(vv[:, :], ps[:, 1, 0:P], blocks, ALU.mult).then_inc(s_vv.sem, 1)
                dve.wait_ge(s_oput.sem, s_oput.at(b, 1))
                dve.tensor_tensor(o_rows[:, :, :], ps[:, 2, :].rearrange("p (t d) -> p t d", t=T),
                                  bp_sb[:, :].unsqueeze(1).to_broadcast([P, T, D]), ALU.add)
                dve.drain()
                norm(1, o_rows, o_rows)
                dve.wait_ge(s_x.sem, s_x.at(b, 16))
                dve.tensor_tensor(xa[:, :, :], x_in[:, :, :], o_rows[:, :, :], ALU.add)
                dve.drain().then_inc(s_xused.sem, 1)

                norm(2, xa, xn)
                rows_ready()
                dve.wait_ge(s_logit.sem, s_logit.at(b, 1))
                dve.tensor_copy(logit[:, :, :], ps[:, 6, 0:T * EXPERTS].rearrange("p (t e) -> p t e", t=T))
                dve.drain()
                for t in range(T):
                    dve.max(top_v[:, t, :], logit[:, t, :])
                dve.drain()
                dve.tensor_tensor(top_d[:, :], top_v[:, :, 1], top_v[:, :, 0], ALU.subtract).then_inc(s_top.sem, 1)
                for t in range(T):
                    dve.max_index(top_i[:, t, :], top_v[:, t, :], logit[:, t, :])
                dve.drain()
                dve.tensor_copy(top_if[:, :, :], top_i[:, :, 0:2])
                dve.drain()
                iota_b = iota.unsqueeze(1).to_broadcast([P, T, EXPERTS])
                for i in range(2):
                    dve.tensor_tensor(disp[:, i, :, :], iota_b,
                                      top_if[:, :, i].unsqueeze(2).to_broadcast([P, T, EXPERTS]), ALU.is_equal)
                dve.drain()
                dve.wait_ge(s_topw.sem, s_topw.at(b, 1))
                for i in range(2):
                    dve.tensor_tensor(disp[:, 2 + i, :, :], disp[:, i, :, :],
                                      top_w[:, i, :].unsqueeze(2).to_broadcast([P, T, EXPERTS]), ALU.mult)
                dve.drain()
                dve.tensor_tensor(disp[:, 0, :, :], disp[:, 2, :, :], disp[:, 3, :, :], ALU.add)
                dve.drain()
                E = EXPERTS
                dve.tensor_copy(disp_p[:, :, 0:E], disp[:, 0, :, :])
                dve.drain()
                dve.tensor_tensor(disp[:, 1, :, :], disp[:, 0, :, :], disp_p[:, :, 0:E], ALU.subtract)
                dve.drain()
                dve.tensor_copy(disp_p[:, :, E:2 * E], disp[:, 1, :, :])
                dve.drain()
                dve.tensor_tensor(disp_p[:, :, 2 * E:3 * E], disp[:, 1, :, :], disp_p[:, :, E:2 * E], ALU.subtract)\
                    .then_inc(s_disp.sem, 1)
                for n in range(UNITS):
                    dve.wait_ge(s_silu.sem, s_silu.at(b, n + 1))
                    if n >= 2:
                        dve.wait_ge(s_down.sem, s_down.at(b, n - 1))
                    dve.tensor_tensor(hid[:, n % 2, :], ps[:, 3 + n % 2, :], act_h[:, n % 2, :], ALU.mult)\
                        .then_inc(s_hid.sem, 1)
                dve.wait_ge(s_down.sem, s_down.at(b, UNITS))
                norm(3, ps[:, 7, :].rearrange("p (t d) -> p t d", t=T), o_rows)
                dve.tensor_tensor(xb[:, :, :], xa[:, :, :], o_rows[:, :, :], ALU.add)
                dve.drain()

                norm(4, xb, xn)
                rows_ready()
                for i in range(3 * G):
                    g, kind = divmod(i, 3)
                    dve.wait_ge(s_rnd.sem, s_rnd.at(b, i + 1))
                    if kind == 0:
                        for j in range(4):
                            r = slice(32 * j, 32 * j + 32)
                            last = dve.scalar_tensor_tensor(qz[r, 4 * g + j, :], rnd[r, i % 2, :], q_low[r, :],
                                                            ps[r, 1 + i % 2, :], ALU.mult, ALU.add)
                    else:
                        last = dve.scalar_tensor_tensor(kk[:, kind - 1, g, :], rnd[:, i % 2, :],
                                                        (k_low, kp_low)[kind - 1], ps[:, 1 + i % 2, :],
                                                        ALU.mult, ALU.add)
                    last.then_inc(s_part.sem, 1)

                def maxima(s, j, qt):
                    g, a = divmod(s, 2)
                    n = (4 * s + j) * T + qt
                    if g >= 2 and (a, j, qt) == (0, 0, 0):
                        dve.wait_ge(s_mps.sem, s_mps.at(b, g - 1))
                    dve.wait_ge(s_aps.sem, s_aps.at(b, n + 1))
                    dve.tensor_reduce(mx[:, g % 2, qt, 2 * j + a:2 * j + a + 1], ps[:, 4 + n % 2, :], AX.X, ALU.max,
                                      negate=True).then_inc(s_amax.sem, 1)

                def output(s):
                    g, a = divmod(s, 2)
                    dve.wait_ge(s_ops.sem, s_ops.at(b, s + 1))
                    o = ps[:, 7, :].rearrange("p (t j c) -> p t j c", t=T, j=4)
                    dve.reciprocal(rec[:, :, :], o[:, :, :, HD])
                    dve.drain()
                    dve.tensor_scalar(rec[:, :, :], rec[:, :, :], alpha_sb[:, a:a + 1], None, ALU.mult)
                    dve.drain()
                    dst = att[:, :, 32 * g:32 * g + 32].rearrange("p t (j d) -> p t j d", j=4)
                    rec_b = rec[:, :, :].unsqueeze(3).to_broadcast([P, T, 4, HD])
                    dve.tensor_tensor(dst if a == 0 else o_nrm[:, :, :, :], o[:, :, :, 0:HD], rec_b, ALU.mult)\
                        .then_inc(s_onrm.sem, 1)
                    dve.drain()
                    if a == 1:
                        dve.tensor_tensor(dst, dst, o_nrm[:, :, :, :], ALU.add)
                        dve.drain()

                for s in range(LEAD):
                    for j in range(4):
                        for qt in range(T):
                            maxima(s, j, qt)
                for u in range(2 * STEPS):
                    s, half = divmod(u, 2)
                    for j in range(4):
                        if s + LEAD < STEPS:
                            for qt in (2 * (j % 2), 2 * (j % 2) + 1):
                                maxima(s + LEAD, 2 * half + j // 2, qt)
                        if (half, j) == (1, 3) and s >= 1:
                            output(s - 1)
                output(STEPS - 1)
                rows_ready()
                dve.wait_ge(s_lout.sem, s_lout.at(b, 1))
                norm(5, ps[:, 1, :].rearrange("p (t d) -> p t d", t=T), o_rows)
                dve.tensor_tensor(xc[:, :, :], xb[:, :, :], o_rows[:, :, :], ALU.add)
                dve.drain()

                norm(6, xc, y)
                rows_ready()
                for l in range(LAYERS):
                    def turned_k(t):
                        dve.wait_ge(l_qkps.sem, l_qkps.at(b, l * T + t + 1))
                        dve.tensor_copy(kT[:, :, t * P:(t + 1) * P], ps[:, 7, :].rearrange("p (a n) -> p a n", a=PAIRS))\
                            .then_inc(l_kT.sem, 1)

                    for t in range(T):
                        i = l * T + t + 1
                        q3 = 3 * (t % 2)
                        dve.wait_ge(l_sq.sem, l_sq.at(b, i))
                        if t >= 1:
                            dve.wait_ge(l_rn.sem, l_rn.at(b, i - 1))
                        dve.tensor_reduce(ssq[:, :, :], sq[:, :, :].rearrange("p i (h d) -> p i h d", d=LD), AX.X, ALU.add)
                        dve.drain()
                        dve.tensor_scalar(ssq[:, :, :], ssq[:, :, :], 1e-24, None, ALU.max).then_inc(l_ss.sem, 1)
                        if t >= 1:
                            turned_k(t - 1)
                        for c in range(2):
                            src = ps[:, q3 + c, :].rearrange("p (h d) -> p h d", d=LD)
                            cos = rot[:, l, 2 * c, t, :].unsqueeze(1).to_broadcast([P, LH, LD])
                            dve.drain()
                            dve.tensor_tensor(ra[:, :, :], src, cos, ALU.mult)
                            for a in range(2):
                                sin = rot[:, l, 2 * c + 1, t, a * H:(a + 1) * H].unsqueeze(1).to_broadcast([P, LH, H])
                                dve.tensor_tensor(rb[:, :, a * H:(a + 1) * H], src[:, :, (1 - a) * H:(2 - a) * H], sin,
                                                  ALU.mult)
                            dve.drain()
                            if c == 0:
                                if t >= 1:
                                    dve.wait_ge(l_qkps.sem, l_qkps.at(b, i - 1))
                                dve.tensor_tensor(qk_rows[:, 0, :].rearrange("p (h d) -> p h d", d=LD), ra[:, :, :],
                                                  rb[:, :, :], ALU.add)
                        dve.tensor_tensor(ra[:, :, :], ra[:, :, :], rb[:, :, :], ALU.add)
                        dve.drain()
                        dve.wait_ge(l_rn.sem, l_rn.at(b, i))
                        dve.tensor_tensor(qk_rows[:, 1, :].rearrange("p (h d) -> p h d", d=LD), ra[:, :, :],
                                          rn[:, t, 1, :].unsqueeze(2).to_broadcast([P, LH, LD]), ALU.mult)
                        dve.drain().then_inc(l_rot.sem, 1)
                    turned_k(T - 1)

                    def local_max(t):
                        i = l * T + t + 1
                        lo = BACK if t == 0 else 0
                        dve.wait_ge(l_s.sem, l_s.at(b, i * PAIRS))
                        s4 = ps[:, 0:PAIRS, 0:2 * (BACK + P)].rearrange("p a (e c) -> p a e c", e=2)
                        dve.tensor_reduce(l_mx[:, :].rearrange("p (a e) -> p a e", e=2), s4[:, :, :, lo:], AX.X, ALU.max,
                                          negate=True)
                        dve.tensor_scalar(l_sc[:, :], rn[:, t, 0, :], 8.0, None, ALU.mult)
                        dve.drain()
                        dve.tensor_tensor(l_nb[:, :], l_mx[:, :], l_sc[:, :], ALU.mult)
                        dve.drain().then_inc(l_max.sem, 1)

                    local_max(0)
                    for t in range(T):
                        i = l * T + t + 1
                        dve.wait_ge(l_exp.sem, l_exp.at(b, i))
                        dve.reciprocal(l_rec[:, :], l_sum[:, :]).then_inc(l_r.sem, 1)
                        if t + 1 < T:
                            local_max(t + 1)
                        for a in range(1, PAIRS, 2):
                            n = (i - 1) * PAIRS + a + 1
                            dve.wait_ge(l_pps.sem, l_pps.at(b, n))
                            if a >= 2:
                                dve.wait_ge(l_pv.sem, l_pv.at(b, n - 2))
                            dve.tensor_copy(l_pT[:, 1, :, :, :].rearrange("p e k n -> p (e k n)"), ps[:, 5, :])\
                                .then_inc(l_ptb.sem, 1)
                        dve.wait_ge(l_wo.sem, l_wo.at(b, i))
                        dve.tensor_tensor(y[:, t, :], y[:, t, :], ps[:, 7, 0:D], ALU.add).then_inc(l_res.sem, 1)
                    dve.drain()
                    dve.tensor_copy(xn[:, :, 0:64], y[:, :, 0:64])
                    dve.drain()
                    dve.wait_ge(l_sh.sem, l_sh.at(b, l + 1))
                    norm(7 + l, xn, xn)
                    rows_ready()
                    for c, (_, m) in enumerate(FF):
                        i = 3 * l + c + 1
                        dve.wait_ge(f_act.sem, f_act.at(b, i))
                        if c >= 2:
                            dve.wait_ge(f_down.sem, f_down.at(b, i - 2))
                        dve.scalar_tensor_tensor(hid[0:m, c % 2, :], ps[0:m, 3 + 2 * (c % 2), :],
                                                 fb1_sb[0:m, l, 0, c:c + 1], act_h[0:m, c % 2, :],
                                                 ALU.add, ALU.mult).then_inc(f_hid.sem, 1)
                    dve.tensor_tensor(y[:, :, :], y[:, :, :], fb2_sb[:, l, :].unsqueeze(1).to_broadcast([P, T, D]), ALU.add)
                    dve.drain()
                    dve.wait_ge(f_down.sem, f_down.at(b, 3 * l + 3))
                    dve.tensor_tensor(y[:, :, :], y[:, :, :], ps[:, 6, :].rearrange("p (t d) -> p t d", t=T), ALU.add)
                    dve.drain()
                    if l + 1 < LAYERS:
                        rows_ready()
                norm(NORMS, y, o_rows)
                dve.tensor_tensor(xa[:, :, :], xc[:, :, :], o_rows[:, :, :], ALU.add)
                dve.drain().then_inc(s_final.sem, 1)
                dve.wait_ge(s_out.sem, s_out.at(b, 16))

        @block.tensor
        def _(pe):
            def turn(src, dst):
                for t in range(T):
                    last = pe.transpose(dst[:, t * P:(t + 1) * P], src[:, t, :], ident)
                return last

            pe.wait_ge(s_const.sem, 1)
            pe.wait_ge(s_zero.sem, 1)
            with pe.Fori(0, B) as b:
                pe.wait_ge(p_rows.sem, p_rows.at(b, 1))
                turn(xn, ps[:, 0, :]).then_inc(p_turned.sem, 1)
                pe.wait_ge(p_cols.sem, p_cols.at(b, 1))
                for i in range(3):
                    pe.matmul(ps[:, 1 + i, :], w0[:, i, :], xT[:, :], start=True, stop=True).then_inc(p_h.sem, 1)
                pe.wait_ge(p_kept.sem, p_kept.at(b, 3))
            with pe.Fori(0, B) as b:
                pe.wait_ge(s_sig.sem, s_sig.at(b, 3))
                for t in range(T):
                    last = pe.transpose(ps[:, 0, t * P:(t + 1) * P], sig[:, 2, t * P:(t + 1) * P], ident)
                last.then_inc(s_turned.sem, 1)
                pe.wait_ge(s_cols.sem, s_cols.at(b, 1))
                for t in range(T):
                    last = pe.matmul(ps[:, 1, 0:P], v_rows[:, t, :], v_rows[:, t, :], start=(t == 0), stop=(t == T - 1))
                last.then_inc(s_vvps.sem, 1)
                pe.wait_ge(s_vv.sem, s_vv.at(b, 1))
                pe.matmul(ps[:, 1, P:2 * P], vv[:, :], w0[:, 3, :], start=True, stop=True).then_inc(s_vvwps.sem, 1)
                pe.wait_ge(s_vvw.sem, s_vvw.at(b, 1))
                pe.wait_ge(s_qk.sem, s_qk.at(b, 1))
                for t in range(T):
                    last = pe.matmul(ps[:, 2, t * P:(t + 1) * P], sig[:, 0, t * P:(t + 1) * P], vvw[:, :],
                                     start=True, stop=True)
                last.then_inc(s_oput.sem, 1)

                def turn_rows(k, src):
                    pe.wait_ge(s_rows.sem, s_rows.at(b, k - 1))
                    turn(src, ps[:, 0, :]).then_inc(s_turned.sem, 1)

                turn_rows(2, xn)
                pe.wait_ge(s_cols.sem, s_cols.at(b, 2))
                for t in range(T):
                    last = pe.matmul(ps[:, 6, t * EXPERTS:(t + 1) * EXPERTS], xT[:, t * P:(t + 1) * P], gate_sb[:, :],
                                     start=True, stop=True)
                last.then_inc(s_logit.sem, 1)

                def down(n):
                    pe.wait_ge(s_hid.sem, s_hid.at(b, n + 1))
                    for t in range(T):
                        last = pe.matmul(ps[:, 7, t * P:(t + 1) * P], hid[:, n % 2, t * P:(t + 1) * P], wd_sb[:, n, :],
                                         start=(n == 0 and t == 0), stop=(n == UNITS - 1), skip_group_check=True)
                    last.then_inc(s_down.sem, 1)

                for n in range(UNITS):
                    if n == 2:
                        pe.wait_ge(s_disp.sem, s_disp.at(b, 1))
                        for t in range(T):
                            last = pe.matmul(ps[0:3 * EXPERTS, 5, t * P:(t + 1) * P], disp_p[:, t, :], ident_bf[:, :],
                                             start=True, stop=True)
                        last.then_inc(s_dispps.sem, 1)
                    if n >= 2:
                        pe.wait_ge(s_hid.sem, s_hid.at(b, n - 1))
                    pe.matmul(ps[:, 1 + n % 2, :], wa_sb[:, n, :], xT[:, :], start=True, stop=True)
                    if n < 2:
                        last = pe.matmul(ps[:, 3 + n % 2, :], wu_sb[:, n, :], xT[:, :], start=True, stop=True)
                    else:
                        if n == 2:
                            pe.wait_ge(s_dispT.sem, s_dispT.at(b, 1))
                        last = pe.matmul(ps[:, 3 + n % 2, :], sel[:, n - 2, :], disp_T[:, :], start=True, stop=True)
                    last.then_inc(s_up.sem, 1)
                    if n >= 1:
                        down(n - 1)
                down(UNITS - 1)

                turn_rows(3, xn)
                pe.wait_ge(s_cols.sem, s_cols.at(b, 3))
                for t in range(T):
                    last = pe.matmul(ps[:, 7, t * P:(t + 1) * P], xT[:, t * P:(t + 1) * P], w1_sb[:, 0, :],
                                     start=True, stop=True)
                last.then_inc(s_vps.sem, 1)
                for i in range(3 * G):
                    g, kind = divmod(i, 3)
                    if i >= 2:
                        pe.wait_ge(s_part.sem, s_part.at(b, i - 1))
                    pe.matmul(ps[:, 1 + i % 2, :], waug[:, kind, g, :, :, :].rearrange("p j r d -> p (j r d)"), xT[:, :],
                              start=True, stop=True).then_inc(s_proj.sem, 1)

                def scores_for_maxima(s, j, qt):
                    g, a = divmod(s, 2)
                    n = (4 * s + j) * T + qt
                    if (j, qt) == (0, 0):
                        pe.wait_ge(s_part.sem, s_part.at(b, 3 * g + 3))
                    if n >= 2:
                        pe.wait_ge(s_amax.sem, s_amax.at(b, n - 1))
                    pe.matmul(ps[:, 4 + n % 2, :], qz[:, 4 * g + j, qt * P:(qt + 1) * P], kk[:, a, g, :],
                              start=True, stop=True).then_inc(s_aps.sem, 1)

                def turn_maxima(g, outputs):
                    pe.wait_ge(s_amax.sem, s_amax.at(b, 32 * (g + 1)))
                    if g == 0:
                        pe.wait_ge(s_vaug.sem, s_vaug.at(b, 1))
                    if outputs:
                        pe.wait_ge(s_onrm.sem, s_onrm.at(b, outputs))
                    for qt in range(T):
                        last = pe.transpose(ps[0:8, 7, qt * P:(qt + 1) * P], mx[:, g % 2, qt, :], ident)
                    last.then_inc(s_mps.sem, 1)

                def weigh(u, k):
                    s, half = divmod(u, 2)
                    kt = 2 * half + k
                    if k == 0:
                        pe.wait_ge(s_exp.sem, s_exp.at(b, 4 * u + 4))
                        if half == 0 and s >= 1:
                            pe.wait_ge(s_oT.sem, s_oT.at(b, s))
                    for j in range(4):
                        last = pe.matmul(ps[32 * j:32 * j + 32, 6, :], v_aug[:, kt, 4 * (s // 2) + j, :],
                                         prob[:, u % 2, j, k, :], start=(kt == 0), stop=(kt == T - 1))
                    if k == 1:
                        last.then_inc(s_pv.sem, 1)

                def turn_output(s, maxima):
                    pe.wait_ge(s_oT.sem, s_oT.at(b, s + 1))
                    pe.wait_ge(s_mT.sem, s_mT.at(b, maxima))
                    if s >= 1:
                        pe.wait_ge(s_onrm.sem, s_onrm.at(b, s))
                    for t in range(T):
                        last = pe.transpose(ps[:, 7, t * P:(t + 1) * P], oT[:, t * P:(t + 1) * P], ident)
                    last.then_inc(s_ops.sem, 1)

                for s in range(LEAD):
                    for j in range(4):
                        for qt in range(T):
                            scores_for_maxima(s, j, qt)
                    if s == 1:
                        turn_maxima(0, 0)
                turned_max = 1
                for u in range(2 * STEPS):
                    s, half = divmod(u, 2)
                    g, a = divmod(s, 2)
                    for j in range(4):
                        n = 4 * u + j
                        if n >= 2:
                            pe.wait_ge(s_exp.sem, s_exp.at(b, n - 1))
                        if (a, half, j) == (0, 0, 0):
                            pe.wait_ge(s_shift.sem, s_shift.at(b, 64 * (g + 1)))
                        for k in range(2):
                            kt = 2 * half + k
                            last = pe.matmul(ps[:, 2 * (n % 2) + k, :], kk[:, a, g, kt * P:(kt + 1) * P],
                                             qz[:, 4 * g + j, :], start=True, stop=True)
                        last.then_inc(s_sps.sem, 1)
                        if s + LEAD < STEPS:
                            for qt in (2 * (j % 2), 2 * (j % 2) + 1):
                                scores_for_maxima(s + LEAD, 2 * half + j // 2, qt)
                        if (half, j) == (0, 1) and s % 2 and s // 2 + 1 < G:
                            turn_maxima(s // 2 + 1, s - 1)
                            turned_max += 1
                        if j % 2 and u >= 1:
                            weigh(u - 1, j // 2)
                        if (half, j) == (1, 2) and s >= 1:
                            turn_output(s - 1, turned_max)
                weigh(2 * STEPS - 1, 0)
                weigh(2 * STEPS - 1, 1)
                turn_output(STEPS - 1, turned_max)
                turn_rows(4, att)
                pe.wait_ge(s_cols.sem, s_cols.at(b, 4))
                for t in range(T):
                    last = pe.matmul(ps[:, 1, t * P:(t + 1) * P], xT[:, t * P:(t + 1) * P], w1_sb[:, 1, :],
                                     start=True, stop=True)
                last.then_inc(s_lout.sem, 1)

                for l in range(LAYERS):
                    turn_rows(5 + 2 * l, y)
                    pe.wait_ge(s_cols.sem, s_cols.at(b, 5 + 2 * l))

                    def project(t):
                        i = l * T + t + 1
                        if t >= 2:
                            pe.wait_ge(l_rot.sem, l_rot.at(b, i - 2))
                            pe.wait_ge(l_v.sem, l_v.at(b, i - 2))
                        for c in range(3):
                            last = pe.matmul(ps[:, 3 * (t % 2) + c, :], hT[:, t * P:(t + 1) * P], wqkv_sb[:, l, c, :],
                                             start=True, stop=True)
                        last.then_inc(l_qkv.sem, 1)

                    project(0)
                    for t in range(T):
                        i = l * T + t + 1
                        if t + 1 < T:
                            project(t + 1)
                        pe.wait_ge(l_rot.sem, l_rot.at(b, i))
                        if t >= 1:
                            pe.wait_ge(l_qT.sem, l_qT.at(b, i - 1))
                            pe.wait_ge(l_kT.sem, l_kT.at(b, i - 1))
                        for c in range(2):
                            for a in range(PAIRS):
                                last = pe.transpose(ps[:, 6 + c, a * P:(a + 1) * P],
                                                    qk_rows[:, c, a * P:(a + 1) * P], ident)
                        last.then_inc(l_qkps.sem, 1)

                    def local_scores(t):
                        i = l * T + t + 1
                        pe.wait_ge(l_qT.sem, l_qT.at(b, i))
                        pe.wait_ge(l_kT.sem, l_kT.at(b, i))
                        if t == 0:
                            pe.wait_ge(l_rot.sem, l_rot.at(b, l * T + T))
                            pe.wait_ge(l_v.sem, l_v.at(b, l * T + T))
                        else:
                            pe.wait_ge(l_exp.sem, l_exp.at(b, i - 1))
                        lo = BACK if t == 0 else 0
                        for a in range(PAIRS):
                            for e in range(2):
                                o = (BACK + P) * e
                                pe.matmul(ps[:, a, o + lo:o + BACK + P], q_bd[:, 2 * a + e, t * P:(t + 1) * P],
                                          kT[:, a, t * P - BACK + lo:(t + 1) * P], start=(e == 0), stop=False,
                                          skip_group_check=True)
                            both = ps[:, a, 0:2 * (BACK + P)].rearrange("p (e c) -> p e c", e=2)
                            pe.matmul(both[:, :, lo:], ident_bf[:, :], band[:, :, lo:], start=False, stop=True,
                                      skip_group_check=True).then_inc(l_s.sem, 1)

                    def local_weigh(t, a):
                        i = l * T + t + 1
                        sig_pt = (l_pta, l_ptb)[a % 2]
                        pe.wait_ge(sig_pt.sem, sig_pt.at(b, (i - 1) * 2 + a // 2 + 1))
                        if a == 0 and t >= 1:
                            pe.wait_ge(l_o.sem, l_o.at(b, i - 1))
                        for e in range(2):
                            h = 2 * a + e
                            for k in range(0 if t else 1, 2):
                                last = pe.matmul(ps[64 * e:64 * e + 64, 6, a * P:(a + 1) * P],
                                                 v_loc[:, t - 1 + k, h * LD:(h + 1) * LD], l_pT[:, a % 2, e, k, :],
                                                 start=(a == 0 and k == (0 if t else 1)), stop=(k == 1),
                                                 skip_group_check=True)
                        last.then_inc(l_pv.sem, 1)

                    local_scores(0)
                    for t in range(T):
                        i = l * T + t + 1
                        if t + 1 < T:
                            local_scores(t + 1)
                        pe.wait_ge(l_pn.sem, l_pn.at(b, i))
                        for a in range(PAIRS):
                            if a >= 2:
                                sig_pt = (l_pta, l_ptb)[a % 2]
                                pe.wait_ge(sig_pt.sem, sig_pt.at(b, (i - 1) * 2 + a // 2))
                            for e in range(2):
                                for k in range(0 if t else 1, 2):
                                    o = (2 * e + k) * P
                                    last = pe.transpose(ps[:, 4 + a % 2, o:o + P], l_p[:, 2 * a + e, k * P:(k + 1) * P],
                                                        ident)
                            last.then_inc(l_pps.sem, 1)
                            if a >= 1:
                                local_weigh(t, a - 1)
                        local_weigh(t, PAIRS - 1)
                        pe.wait_ge(l_o.sem, l_o.at(b, i))
                        if t >= 1:
                            pe.wait_ge(l_res.sem, l_res.at(b, i - 1))
                        for a in range(PAIRS):
                            last = pe.matmul(ps[:, 7, 0:D], l_oT[:, a, :], wo_sb[:, l, a, :],
                                             start=(a == 0), stop=(a == PAIRS - 1))
                        last.then_inc(l_wo.sem, 1)

                    pe.wait_ge(l_res.sem, l_res.at(b, l * T + T))
                    pe.matmul(ps[:, 1, 0:T * 64].rearrange("p (t d) -> p t d", t=T), shift, y[:, :, 64:P],
                              start=True, stop=False)
                    pe.matmul(ps[:, 1, 64:T * 64].rearrange("p (t d) -> p t d", t=T - 1), carry, y[:, 0:T - 1, 64:P],
                              start=False, stop=True).then_inc(l_shps.sem, 1)
                    turn_rows(6 + 2 * l, xn)
                    pe.wait_ge(s_cols.sem, s_cols.at(b, 6 + 2 * l))

                    def ff_down(c):
                        m = FF[c][1]
                        pe.wait_ge(f_hid.sem, f_hid.at(b, 3 * l + c + 1))
                        for t in range(T):
                            last = pe.matmul(ps[:, 6, t * P:(t + 1) * P], hid[0:m, c % 2, t * P:(t + 1) * P],
                                             fw2_sb[0:m, l, c, :], start=(c == 0 and t == 0), stop=(c == 2),
                                             skip_group_check=True)
                        last.then_inc(f_down.sem, 1)

                    for c, (o, m) in enumerate(FF):
                        if c >= 2:
                            pe.wait_ge(f_hid.sem, f_hid.at(b, 3 * l + c - 1))
                        for a in range(2):
                            w = (1 - a) * HID_F + o
                            last = pe.matmul(ps[0:m, 2 + 2 * (c % 2) + a, :], fw1_sb[:, l, w:w + m], xT[:, :],
                                             start=True, stop=True)
                        last.then_inc(f_up.sem, 1)
                        if c >= 1:
                            ff_down(c - 1)
                    ff_down(2)


def rotary_tables():
    half = np.arange(0, LD, 2, dtype=np.float32)
    inv_freq = (np.float32(1.0) / np.float32(10000.0) ** (half / np.float32(LD))).astype(np.float32)
    t = np.arange(N, dtype=np.float32)
    freqs = (t[:, None] * inv_freq[None, :]).astype(np.float32)
    freqs = np.concatenate([freqs, freqs], axis=-1)
    base = (half + np.float32(0.4 * LD)) / np.float32(1.4 * LD)
    power = (t - N // 2) / np.float32(32.0)
    scale = base[None, :] ** power[:, None]
    scale = np.concatenate([scale, scale], axis=-1)
    sign = np.where(np.arange(LD) < LD // 2, -1.0, 1.0).astype(np.float32)
    cos, sin = np.cos(freqs), np.sin(freqs) * sign
    tables = np.stack([cos * scale, sin * scale, cos / scale, sin / scale])
    return tables.astype(np.float32).reshape(4, T, P, LD).transpose(2, 0, 1, 3)


def constants():
    mats = np.zeros((P, 4, P), np.float32)
    mats[:, 0] = np.eye(P)
    mats[:, 1] = np.eye(P, k=1)
    mats[P - 1, 2, 0] = 1.0
    mats[:, 3] = np.kron(np.eye(HEADS), np.ones((HD, HD))) * HD ** -0.5
    sel = np.zeros((3 * EXPERTS, 8, P), np.float32)
    for e in range(EXPERTS):
        sel[e::EXPERTS, e // 2, HID_E * (e % 2):HID_E * (e % 2) + HID_E] = 1.0
    q, c = np.arange(P)[:, None], np.arange(BACK + P)[None, :]
    band = np.repeat(np.where((q <= c) & (c <= q + BACK), 0.0, NEG)[:, None, :], 2, axis=1)
    small = np.zeros((P, 81), np.float32)
    small[:, 48 + HD] = 1.0
    small[:, 0:16] = -0.5
    small[:, 16:32] = np.arange(16)
    r = np.arange(P) % 32
    small[:, 32] = np.where((r >= 16) & (r < 24), -1.0, 0.0)
    for i in range(2):
        small[:, 33 + i] = np.where((r >= 8) & (r < 16), -1.0, 0.0) + (r == 24 + i)
        small[:, 35 + i] = r == 24 + i
    return [mats, sel, band.astype(np.float32), small, rotary_tables()]


def kernel(**inputs):
    import concourse.bacc as bacc
    from concourse.bass_utils import run_bass_kernel_spmd

    i = {k: np.asarray(v) for k, v in inputs.items()}
    L0, F0, L1, F1 = "L0_attn_", "L0_ffn_", "L1_attn_", "L1_ffn_"

    def cat(parts, axis=1):
        return np.concatenate(parts, axis=axis)

    def rows(v, shape):
        return np.broadcast_to(v, shape)

    fb1 = np.zeros((LAYERS, 2, 3 * P), np.float32)
    fb1[:, :, 0:HID_F] = i[F1 + "b1"].reshape(LAYERS, 2, HID_F)
    fw2 = np.zeros((LAYERS, 3 * P, D), np.float32)
    fw2[:, 0:HID_F] = i[F1 + "w2"]
    arrays = {
        "x": i[L0 + "x"],
        "wl0": np.stack([i[L0 + w].T for w in ("Wq", "Wk", "Wv", "Wp")], axis=1),
        "gb": np.stack([i[L0 + w] for w in ("gq", "bq", "gk", "bk", "gv", "bv")], axis=1),
        "bp": rows(i[L0 + "bp"], (P, D)),
        "gate": i[F0 + "gate_w"].T,
        "ew_a": cat([i[F0 + "sfc1"].T, i[F0 + "w1"].reshape(EXPERTS * HID_E, D).T]).reshape(D, UNITS, P),
        "ew_u": i[F0 + "sfc2"].T.reshape(D, 2, P),
        "ew_d": cat([i[F0 + "sfc3"].T, i[F0 + "w2"].transpose(0, 2, 1).reshape(EXPERTS * HID_E, D)], 0)
                .reshape(UNITS, P, D).transpose(1, 0, 2),
        "wl1": np.stack([i[L1 + w].T for w in ("W_Q", "W_K", "W_K_prime", "W_V", "W_O")], axis=1),
        "alpha": rows(i[L1 + "alpha"].reshape(1, 1), (P, 1)),
        "wqkv": i[F1 + "wqkv"].reshape(LAYERS, D, 3, INNER).transpose(1, 0, 2, 3),
        "qks": rows(np.stack([i[F1 + "q_scale"], i[F1 + "k_scale"]], axis=1)[None], (P, LAYERS, 2, LD)),
        "wo": i[F1 + "wo"].reshape(LAYERS, PAIRS, P, D).transpose(2, 0, 1, 3),
        "lngb": np.stack([i[F1 + "ln_g"], i[F1 + "ln_b"]], axis=1).transpose(2, 0, 1),
        "fw1": i[F1 + "w1"].transpose(1, 0, 2),
        "fb1": fb1.reshape(LAYERS, 2, 3, P).transpose(3, 0, 1, 2),
        "fw2": fw2.reshape(LAYERS, 3, P, D).transpose(2, 0, 1, 3),
        "fb2": rows(i[F1 + "b2"][None], (P, LAYERS, D)),
    }
    for name, a in zip(("c_mat", "c_sel", "c_band", "c_small", "c_rot"), constants()):
        arrays[name] = a
    arrays = {k: np.ascontiguousarray(a) for k, a in arrays.items()}

    nc = bacc.Bacc("TRN2", target_bir_lowering=False, num_devices=1)
    args = [nc.dram_tensor(k, a.shape, mybir.dt.from_np(a.dtype), kind="ExternalInput").ap() for k, a in arrays.items()]
    args.append(nc.dram_tensor("out", (B, N, D), F32, kind="ExternalOutput").ap())
    build(nc, *args)
    result = run_bass_kernel_spmd(nc, [arrays], core_ids=[0])
    return result.results[0]["out"]
```

```python
from contextlib import ExitStack

import numpy as np
import concourse.bass as bass
from concourse import mybir

ALU = mybir.AluOpType
ACT = mybir.ActivationFunctionType
AX = mybir.AxisListType
F32 = mybir.dt.float32
F32R = mybir.dt.float32r
BF16 = mybir.dt.bfloat16
U32 = mybir.dt.uint32

P = 128
B, N, D = 8, 512, 128
T = N // P
EPS = 1e-5
NEG = -1e30

EXPERTS, HID_E, SHARED = 16, 64, 256
UNITS = SHARED // P + EXPERTS * HID_E // P
HEADS, HD = 16, 8
G = HEADS // 4
LAYERS, LH, LD = 2, 8, 64
INNER = LH * LD
PAIRS = LH // 2
BACK = 64
HID_F = 341
FF = [(0, 128), (128, 128), (256, HID_F - 256)]


class Signal:

    def __init__(self, sem, per):
        self.sem, self.per = sem, per

    def at(self, b, k):
        return b * self.per + k


def build(nc, x, wl0, gb, bp, gate, ew_a, ew_u, ew_d, wl1, alpha, wqkv, qks, wo, lngb, fw1, fb1, fw2, fb2,
          c_mat, c_sel, c_band, c_small, c_rot, out):
    ctx = ExitStack()
    with ctx:
        def sb(name, shape, dt=F32):
            return ctx.enter_context(nc.sbuf_tensor(name, shape, dt))

        def signal(name, per=1):
            return Signal(ctx.enter_context(nc.semaphore(name)), per)

        ps = ctx.enter_context(nc.psum_tensor("ps", [P, 8, 512], F32))

        arena = ctx.enter_context(nc.sbuf_tensor("arena", [P, 8192], F32))

        arena2 = ctx.enter_context(nc.sbuf_tensor("arena2", [P, 4096], F32))

        def part(start, *dims, arena=arena):
            names = "abcdef"[:len(dims)]
            size = int(np.prod(dims))
            flat = arena[:, start:start + size]
            if len(dims) == 1:
                return flat
            return flat.rearrange(f"p ({' '.join(names)}) -> p {' '.join(names)}", **dict(zip(names, dims)))

        w0 = sb("w0", [P, 4, D])
        gb_sb = sb("gb_sb", [P, 6])
        bp_sb = sb("bp_sb", [P, D])
        gate_sb = sb("gate_sb", [P, EXPERTS])
        wa_sb = sb("wa_sb", [P, UNITS, P])
        wu_sb = sb("wu_sb", [P, 2, P])
        wd_sb = sb("wd_sb", [P, UNITS, D])
        w1_in = part(2560, 3, D)
        w1_sb = sb("w1_sb", [P, 2, D])
        waug = sb("waug", [P, 3, G, 4, 4, HD])
        alpha_sb = sb("alpha_sb", [P, 2])
        wqkv_sb = sb("wqkv_sb", [P, LAYERS, 3, INNER])
        qks_sb = sb("qks_sb", [P, LAYERS, 2, LD])
        wo_sb = sb("wo_sb", [P, LAYERS, PAIRS, D])
        lngb_sb = sb("lngb_sb", [P, LAYERS, 2])
        fw1_sb = sb("fw1_sb", [P, LAYERS, 2 * HID_F])
        fb1_sb = sb("fb1_sb", [P, LAYERS, 2, 3])
        fw2_sb = sb("fw2_sb", [P, LAYERS, 3, D])
        fb2_sb = sb("fb2_sb", [P, LAYERS, D])
        mats = sb("mats", [P, 4, P])
        ident, shift, carry, blocks = (mats[:, i, :] for i in range(4))
        ident_bf = sb("ident_bf", [P, P], BF16)
        sel_f = part(0, 8, P)[0:3 * EXPERTS]
        sel = sb("sel", [3 * EXPERTS, 8, P], BF16)
        band_f = part(1024, 2, BACK + P)
        band = sb("band", [P, 2, BACK + P], BF16)
        small = sb("small", [P, 81])
        half_neg = small[:, 0:16]
        iota = small[:, 16:32]
        one_at_hd, zero = small[:, 48:80], small[:, 80:81]
        q_low, k_low, kp_low, k_one, kp_one = (small[:, 32 + i:33 + i] for i in range(5))
        rot_in = part(1536, 4, T, LD)
        rot = sb("rot", [P, LAYERS, 4, T, LD])

        h_stats = sb("h_stats", [P, 3, B, 6])
        h_mv = sb("h_mv", [P, 3, 2])
        bn = sb("bn", [P, 5, 3])
        sig = part(2048, 3, N, arena=arena2)
        vv = sb("vv", [P, D])
        vvw = sb("vvw", [P, D])

        x_in = sb("x_in", [P, T, D])
        xa = sb("xa", [P, T, D])
        xb = sb("xb", [P, T, D])
        xc = sb("xc", [P, T, D])
        o_rows = sb("o_rows", [P, T, D])
        xn = sb("xn", [P, T, D])
        xT = sb("xT", [P, N])
        hT = sb("hT", [P, N])
        y = sb("y", [P, T, D])
        ln_st = sb("ln_st", [P, T, 6])
        ln_mv = sb("ln_mv", [P, T, 2])
        ln_ve = sb("ln_ve", [P, T])
        ln_rs = sb("ln_rs", [P, T])

        logit = sb("logit", [P, T, EXPERTS])
        top_v = sb("top_v", [P, T, 8])
        top_i = sb("top_i", [P, T, 8], U32)
        top_if = sb("top_if", [P, T, 2])
        top_d = sb("top_d", [P, T])
        top_w = sb("top_w", [P, 2, T])
        disp = sb("disp", [P, 4, T, EXPERTS])
        disp_p = sb("disp_p", [P, T, 3 * EXPERTS], BF16)
        disp_T = sb("disp_T", [3 * EXPERTS, N], BF16)
        act_h = sb("act_h", [P, 2, N])
        v_rows = act_h[:, 0, :].rearrange("p (t d) -> p t d", t=T)
        hid = sb("hid", [P, 2, N])

        rnd = sb("rnd", [P, 2, N], F32R)
        qz = sb("qz", [P, HEADS, N], F32R)
        kk = sb("kk", [P, 2, G, N], F32R)
        v_aug = part(0, T, HEADS, 32, arena=arena2)
        mx = sb("mx", [P, 2, T, 8])
        mxT = sb("mxT", [8, 2, N], F32R)
        prob = part(0, 2, 4, 2, N)
        oT = sb("oT", [P, N])
        rec = sb("rec", [P, T, 4])
        o_nrm = sb("o_nrm", [P, T, 4, HD])
        att = o_rows

        sq = part(0, 2, INNER)
        ssq = sb("ssq", [P, 2, LH])
        rn = sb("rn", [P, T, 2, LH])
        ra = part(1024, LH, LD)
        rb = part(1536, LH, LD)
        qk_rows = part(2048, 2, INNER)
        q_bd = part(0, LH, N, arena=arena2)
        kT = part(3072, PAIRS, N)
        v_loc = part(5120, T, INNER)
        l_mx = sb("l_mx", [P, LH])
        l_sc = sb("l_sc", [P, 2, LH])
        l_nb = sb("l_nb", [P, LH])
        l_sum = sb("l_sum", [P, LH])
        l_rec = sb("l_rec", [P, LH])
        l_p = sb("l_p", [P, LH, 2 * P])
        l_pT = part(7168, 2, 2, 2, P)
        l_oT = oT[:, :].rearrange("p (a n) -> p a n", a=PAIRS)

        s_w = signal("s_w")
        s_const = signal("s_const")
        s_zero = signal("s_zero")
        p_x = signal("p_x", 16)
        p_used = signal("p_used")
        p_var = signal("p_var")
        p_rstd = signal("p_rstd")
        p_rows = signal("p_rows")
        p_turned = signal("p_turned")
        p_cols = signal("p_cols")
        p_h = signal("p_h", 3)
        p_kept = signal("p_kept", 3)
        p_store = signal("p_store", 16)
        p_stat = signal("p_stat", 3)
        n_var = signal("n_var")
        n_rstd = signal("n_rstd")
        n_aff = signal("n_aff")

        NORMS = 5 + 1 + LAYERS + 1
        s_x = signal("s_x", 16)
        s_h = signal("s_h", 16)
        s_xused = signal("s_xused")
        s_var = signal("s_var", NORMS)
        s_rstd = signal("s_rstd", NORMS)
        TURNS = 4 + 2 * LAYERS
        s_rows = signal("s_rows", TURNS - 1)
        s_turned = signal("s_turned", TURNS)
        s_cols = signal("s_cols", TURNS)
        s_vone = signal("s_vone")
        s_qzero = signal("s_qzero")
        s_sig = signal("s_sig", 3)
        s_qk = signal("s_qk")
        s_vvps = signal("s_vvps")
        s_vv = signal("s_vv")
        s_vvwps = signal("s_vvwps")
        s_vvw = signal("s_vvw")
        s_oput = signal("s_oput")
        s_logit = signal("s_logit")
        s_top = signal("s_top")
        s_topw = signal("s_topw")
        s_disp = signal("s_disp")
        s_dispps = signal("s_dispps")
        s_dispT = signal("s_dispT")
        s_up = signal("s_up", UNITS)
        s_silu = signal("s_silu", UNITS)
        s_hid = signal("s_hid", UNITS)
        s_down = signal("s_down", UNITS)
        s_vps = signal("s_vps")
        s_vaug = signal("s_vaug")
        s_proj = signal("s_proj", 3 * G)
        s_rnd = signal("s_rnd", 3 * G)
        s_part = signal("s_part", 3 * G)
        s_qput = signal("s_qput", 64 * G)
        s_aps = signal("s_aps", 2 * HEADS * T)
        s_amax = signal("s_amax", 2 * HEADS * T)
        s_mps = signal("s_mps", G)
        s_mT = signal("s_mT", G)
        s_shift = signal("s_shift", 16 * HEADS)
        s_sps = signal("s_sps", 8 * 4 * G)
        s_exp = [signal(f"s_exp{i}", 4 * 4 * G) for i in range(2)]
        s_pv = signal("s_pv", 4 * G)
        s_oT = signal("s_oT", 2 * G)
        s_ops = signal("s_ops", 2 * G)
        s_onrm = signal("s_onrm", 2 * G)
        s_lout = signal("s_lout")
        l_qkv = signal("l_qkv", LAYERS * T)
        l_sq = signal("l_sq", LAYERS * T)
        l_v = signal("l_v", LAYERS * T)
        l_ss = signal("l_ss", LAYERS * T)
        l_rn = signal("l_rn", LAYERS * T)
        l_qrow = signal("l_qrow", LAYERS * T)
        l_kread = signal("l_kread", LAYERS * T)
        l_krow = signal("l_krow", LAYERS * T)
        l_qps = signal("l_qps", LAYERS * T)
        l_kps = signal("l_kps", LAYERS * T)
        l_qT = signal("l_qT", LAYERS * T)
        l_kT = signal("l_kT", LAYERS * T)
        l_s = signal("l_s", LAYERS * T * PAIRS)
        l_max = signal("l_max", LAYERS * T * PAIRS)
        l_exp = signal("l_exp", LAYERS * T * PAIRS)
        l_r = signal("l_r", LAYERS * T * PAIRS)
        l_pn = signal("l_pn", LAYERS * T * PAIRS)
        l_pps = signal("l_pps", LAYERS * T * PAIRS)
        l_pT_in = signal("l_pT_in", LAYERS * T * PAIRS)
        l_pv = signal("l_pv", LAYERS * T * PAIRS)
        l_o = signal("l_o", LAYERS * T)
        l_wo = signal("l_wo", LAYERS * T)
        l_res = signal("l_res", LAYERS * T)
        l_shps = signal("l_shps", LAYERS)
        l_sh = signal("l_sh", LAYERS)
        f_up = signal("f_up", LAYERS * 3)
        f_act = signal("f_act", LAYERS * 3)
        f_hid = signal("f_hid", LAYERS * 3)
        f_down = signal("f_down", LAYERS * 3)
        s_final = signal("s_final")
        s_out = signal("s_out", 16)

        x_rows = x.rearrange("b (t p) d -> b p t d", p=P)
        h_dram = nc.dram_tensor("h_dram", (B, P, 3, N), F32, kind="Internal").ap()
        out_rows = out.rearrange("b (t p) d -> b p t d", p=P)

        LOADS = [(w0[:], wl0), (gb_sb[:], gb), (bp_sb[:], bp), (gate_sb[:], gate), (wa_sb[:], ew_a), (wu_sb[:], ew_u),
                 (wd_sb[:], ew_d), (w1_in, wl1[:, 0:3, :]), (w1_sb[:], wl1[:, 3:5, :]), (alpha_sb[:, 0:1], alpha), (wqkv_sb[:], wqkv), (qks_sb[:], qks),
                 (wo_sb[:], wo), (lngb_sb[:], lngb), (fw1_sb[:], fw1), (fb1_sb[:], fb1), (fw2_sb[:], fw2),
                 (fb2_sb[:], fb2), (mats[:], c_mat), (sel_f, c_sel), (band_f, c_band), (small[:], c_small),
                 (rot_in, c_rot)]
        LOADED = 16 * len(LOADS)

        block = ctx.enter_context(nc.Block())

        STEPS = 2 * G
        MAXIMA = 16 * STEPS
        AHEAD = 40
        PROJECT_EARLY = {4: 3, 8: 4, 12: 5}
        PROJECT_IN = {1: 6, 4: 7, 7: 8, 17: 9, 20: 10, 24: 11}

        def maxima_in(k):
            return range(min(AHEAD + 2 * k, MAXIMA), min(AHEAD + 2 * k + 2, MAXIMA))

        def maxima_done(k):
            return min(AHEAD + 2 * k + 2, MAXIMA) // 32

        def proj_bank(i):
            return i % 3 if i < 6 else 7

        ALL_PAIRS, LAG = T * PAIRS, 3
        SLOTS = ALL_PAIRS + LAG + 1

        @block.sync
        def _(sp):
            for dst, src in LOADS:
                sp.dma_start(dst, src).then_inc(s_w.sem, 16)

            def load_x(b, loaded):
                sp.dma_start(x_in[:, :, :], x_rows[bass.ds(b, 1), :, :, :].rearrange("o p t d -> (o p) t d"))\
                    .then_inc(loaded.sem, 16)

            def load_h(b):
                sp.dma_start(sig[:, :, :], h_dram[bass.ds(b, 1), :, :, :].rearrange("o p i n -> (o p) i n"))\
                    .then_inc(s_h.sem, 16)

            def store_h(b):
                sp.wait_ge(p_kept.sem, p_kept.at(b, 3))
                sp.dma_start(h_dram[bass.ds(b, 1), :, :, :].rearrange("o p i n -> (o p) i n"), sig[:, :, :])\
                    .then_inc(p_store.sem, 16)

            def place_q(b, g):
                sp.wait_ge(s_part.sem, s_part.at(b, 3 * g + 1))
                for j in range(4):
                    r = slice(32 * j, 32 * j + 32)
                    sp.dma_start(qz[r, 4 * g + j, :].bitcast(F32), rnd[r, 3 * g % 2, :].bitcast(F32))\
                        .then_inc(s_qput.sem, 16)

            def place_shifts(b, g):
                sp.wait_ge(s_mT.sem, s_mT.at(b, g + 1))
                for j in range(4):
                    sp.dma_start(qz[32 * j + 24:32 * j + 26, 4 * g + j, :].bitcast(F32),
                                 mxT[2 * j:2 * j + 2, g % 2, :].bitcast(F32)).then_inc(s_shift.sem, 16)

            def place(b):
                place_q(b, 0)
                for g in range(G):
                    if g + 1 < G:
                        place_q(b, g + 1)
                    place_shifts(b, g)

            def store_out(b):
                sp.wait_ge(s_final.sem, s_final.at(b, 1))
                sp.dma_start(out_rows[bass.ds(b, 1), :, :, :].rearrange("o p t d -> (o p) t d"), xa[:, :, :])\
                    .then_inc(s_out.sem, 16)

            load_x(0, p_x)
            with sp.Fori(0, B - 1) as b:
                sp.wait_ge(p_used.sem, p_used.at(b, 1))
                load_x(b + 1, p_x)
                store_h(b)
            store_h(B - 1)
            sp.wait_ge(p_used.sem, p_used.at(B, 0))
            load_x(0, s_x)
            sp.wait_ge(p_store.sem, p_store.at(B, 0))
            sp.wait_ge(p_stat.sem, p_stat.at(B, 0))
            load_h(0)
            with sp.Fori(0, B - 1) as b:
                place(b)
                sp.wait_ge(s_xused.sem, s_xused.at(b, 1))
                load_x(b + 1, s_x)
                sp.wait_ge(l_s.sem, l_s.at(b, l_s.per))
                load_h(b + 1)
                store_out(b)
            place(B - 1)
            store_out(B - 1)
            sp.wait_ge(s_out.sem, s_out.at(B, 0))

        @block.gpsimd
        def _(pool):
            pool.memset(qz[:, :, :].bitcast(F32), 0.0)
            pool.memset(l_p[:, :, :], 0.0)
            pool.drain()
            pool.memset(hT[64:P, 0:1], 0.0)
            pool.drain().then_inc(s_zero.sem, 1)
            pool.wait_ge(s_w.sem, LOADED)
            with pool.Fori(0, B) as b:
                pool.wait_ge(p_var.sem, p_var.at(b, 1))
                pool.tensor_tensor(ln_rs[:, :], ln_ve[:, :], half_neg[:, 0:T], ALU.pow).then_inc(p_rstd.sem, 1)
            pool.wait_ge(n_var.sem, 1)
            pool.tensor_tensor(bn[:, 1, :], bn[:, 0, :], half_neg[:, 0:3], ALU.pow).then_inc(n_rstd.sem, 1)

            with pool.Fori(0, B) as b:
                def rstd(k):
                    pool.wait_ge(s_var.sem, s_var.at(b, k))
                    pool.tensor_tensor(ln_rs[:, :], ln_ve[:, :], half_neg[:, 0:T], ALU.pow).then_inc(s_rstd.sem, 1)

                pool.tensor_tensor(v_aug[:, :, :, :].rearrange("p t h c -> p (t h) c"),
                                   one_at_hd.unsqueeze(1).to_broadcast([P, T * HEADS, 32]),
                                   zero.unsqueeze(2).to_broadcast([P, T * HEADS, 32]), ALU.add).then_inc(s_vone.sem, 1)
                for k in range(1, 5):
                    rstd(k)
                pool.wait_ge(s_pv.sem, s_pv.at(b, 4 * G))
                zero_b = zero.to_broadcast([P, LH * N])
                pool.tensor_tensor(q_bd[:, :, :].rearrange("p h n -> p (h n)"), zero_b, zero_b, ALU.add)\
                    .then_inc(s_qzero.sem, 1)
                rstd(5)
                rstd(6)
                for l in range(LAYERS):
                    def inverse_norms(t):
                        i = l * T + t + 1
                        pool.wait_ge(l_ss.sem, l_ss.at(b, i))
                        pool.tensor_tensor(rn[:, t, :, :], ssq[:, :, :],
                                           half_neg.rearrange("p (a h) -> p a h", a=2), ALU.pow).then_inc(l_rn.sem, 1)

                    def norm_probs(n):
                        t, a = divmod(n, PAIRS)
                        lo = P if t == 0 else BACK
                        r = slice(2 * a, 2 * a + 2)
                        pool.wait_ge(l_r.sem, l_r.at(b, l * ALL_PAIRS + n + 1))
                        pool.tensor_tensor(l_p[:, r, lo:2 * P], l_p[:, r, lo:2 * P],
                                           l_rec[:, r].unsqueeze(2).to_broadcast([P, 2, 2 * P - lo]), ALU.mult)\
                            .then_inc(l_pn.sem, 1)

                    inverse_norms(0)
                    for n in range(ALL_PAIRS):
                        t, a = divmod(n, PAIRS)
                        norm_probs(n)
                        if a == 0 and t + 1 < T:
                            inverse_norms(t + 1)
                    rstd(7 + l)
                rstd(NORMS)
                pool.wait_ge(l_s.sem, l_s.at(b, l_s.per))

        @block.scalar
        def _(act):
            act.wait_ge(s_zero.sem, 1)
            with act.Fori(0, B) as b:
                act.wait_ge(p_turned.sem, p_turned.at(b, 1))
                act.copy(xT[:, :], ps[:, 0, :]).then_inc(p_cols.sem, 1)
                for i in range(3):
                    act.wait_ge(p_h.sem, p_h.at(b, i + 1))
                    act.copy(sig[:, i, :], ps[:, 1 + i, :]).then_inc(p_kept.sem, 1)
                act.wait_ge(p_store.sem, p_store.at(b, 16))
                act.wait_ge(p_stat.sem, p_stat.at(b, 3))
            act.wait_ge(n_aff.sem, 1)
            with act.Fori(0, B) as b:
                def columns(k, dst):
                    act.wait_ge(s_turned.sem, s_turned.at(b, k))
                    act.copy(dst, ps[:, 0, :]).then_inc(s_cols.sem, 1)

                act.wait_ge(s_h.sem, s_h.at(b, 16))
                for i in range(3):
                    act.activation(sig[:, i, :], sig[:, i, :], ACT.Sigmoid,
                                   bias=bn[:, 3, i:i + 1], scale=bn[:, 2, i:i + 1]).then_inc(s_sig.sem, 1)
                act.wait_ge(s_turned.sem, s_turned.at(b, 1))
                act.copy(act_h[:, 0, :], ps[:, 0, :]).then_inc(s_cols.sem, 1)
                act.wait_ge(s_vvwps.sem, s_vvwps.at(b, 1))
                act.copy(vvw[:, :], ps[:, 1, P:2 * P]).then_inc(s_vvw.sem, 1)

                columns(2, xT[:, :])
                act.wait_ge(s_top.sem, s_top.at(b, 1))
                act.activation(top_w[:, 0, :], top_d[:, :], ACT.Sigmoid, scale=-1.0)
                act.activation(top_w[:, 1, :], top_d[:, :], ACT.Sigmoid).then_inc(s_topw.sem, 1)
                for n in range(UNITS):
                    if n == 2:
                        act.wait_ge(s_dispps.sem, s_dispps.at(b, 1))
                        act.copy(disp_T[:, :], ps[0:3 * EXPERTS, 5, :]).then_inc(s_dispT.sem, 1)
                    act.wait_ge(s_up.sem, s_up.at(b, n + 1))
                    if n >= 2:
                        act.wait_ge(s_hid.sem, s_hid.at(b, n - 1))
                    act.activation(act_h[:, n % 2, :], ps[:, 1 + n % 2, :], ACT.Silu).then_inc(s_silu.sem, 1)

                columns(3, xT[:, :])

                def rounded(i):
                    act.wait_ge(s_proj.sem, s_proj.at(b, i + 1))
                    if i >= 2 and (i - 2) % 3 == 0:
                        act.wait_ge(s_qput.sem, s_qput.at(b, 64 * ((i - 2) // 3 + 1)))
                    elif i >= 2:
                        act.wait_ge(s_part.sem, s_part.at(b, i - 1))
                    act.activation(rnd[:, i % 2, :], ps[:, proj_bank(i), :], ACT.Identity,
                                   bias=(0.0, k_one, kp_one)[i % 3]).then_inc(s_rnd.sem, 1)

                def shifts(g):
                    act.wait_ge(s_mps.sem, s_mps.at(b, g + 1))
                    if g >= 2:
                        act.wait_ge(s_shift.sem, s_shift.at(b, 64 * (g - 1)))
                    act.copy(mxT[:, g % 2, :], ps[0:8, 7, :]).then_inc(s_mT.sem, 1)

                for i in range(2):
                    rounded(i)
                act.wait_ge(s_vone.sem, s_vone.at(b, 1))
                act.wait_ge(s_vps.sem, s_vps.at(b, 1))
                act.copy(v_aug[:, :, :, 0:HD], ps[:, 7, :].rearrange("p (t h d) -> p t h d", t=T, d=HD))\
                    .then_inc(s_vaug.sem, 1)
                for i in range(2, 6):
                    rounded(i)
                shifts(0)
                for k in range(8 * STEPS):
                    s, u, j = k // 8, k // 4, k % 4
                    if j == 0 and u >= 2:
                        act.wait_ge(s_pv.sem, s_pv.at(b, u - 1))
                    for i in range(2):
                        m = 2 * k + i
                        act.wait_ge(s_sps.sem, s_sps.at(b, m + 1))
                        act.activation(prob[:, u % 2, j, i, :], ps[:, m % 3, :], ACT.Exp, scale=HD ** -0.5)\
                            .then_inc(s_exp[i].sem, 1)
                    if k >= 1 and maxima_done(k - 1) > maxima_done(k - 2):
                        shifts(maxima_done(k - 1) - 1)
                    if k in PROJECT_IN:
                        rounded(PROJECT_IN[k])
                    if k % 8 == 3 and s >= 1:
                        act.wait_ge(s_pv.sem, s_pv.at(b, u))
                        if s >= 2:
                            act.wait_ge(s_ops.sem, s_ops.at(b, s - 1))
                        act.copy(oT[:, :], ps[:, 6, :]).then_inc(s_oT.sem, 1)
                act.wait_ge(s_pv.sem, s_pv.at(b, 2 * STEPS))
                act.wait_ge(s_ops.sem, s_ops.at(b, STEPS - 1))
                act.copy(oT[:, :], ps[:, 6, :]).then_inc(s_oT.sem, 1)
                columns(4, xT[:, :])

                act.wait_ge(s_qzero.sem, s_qzero.at(b, 1))
                for l in range(LAYERS):
                    act.wait_ge(s_turned.sem, s_turned.at(b, 5 + 2 * l))
                    act.copy(hT[0:64, :], ps[0:64, 0, :])
                    act.copy(hT[64:P, 1:N], ps[64:P, 0, 0:N - 1]).then_inc(s_cols.sem, 1)

                    def squares(t):
                        i = l * T + t + 1
                        act.wait_ge(l_qkv.sem, l_qkv.at(b, i))
                        if t >= 1:
                            act.wait_ge(l_ss.sem, l_ss.at(b, i - 1))
                        act.activation(sq[:, 0, :], ps[:, 0, :], ACT.Square)
                        act.activation(sq[:, 1, :], ps[:, 1, :], ACT.Square).then_inc(l_sq.sem, 1)
                        act.copy(v_loc[:, t, :], ps[:, 2, :]).then_inc(l_v.sem, 1)

                    def turned_q(t):
                        act.wait_ge(l_qps.sem, l_qps.at(b, l * T + t + 1))
                        for e in range(2):
                            r = slice(64 * e, 64 * e + 64)
                            last = act.copy(q_bd[r, e:LH:2, t * P:(t + 1) * P],
                                            ps[r, 3, :].rearrange("p (a n) -> p a n", a=PAIRS))
                        last.then_inc(l_qT.sem, 1)

                    def turned_probs(n):
                        k = l * ALL_PAIRS + n + 1
                        act.wait_ge(l_pps.sem, l_pps.at(b, k))
                        if n >= 2:
                            act.wait_ge(l_pv.sem, l_pv.at(b, k - 2))
                        act.copy(l_pT[:, n % 2, :, :, :].rearrange("p e k n -> p (e k n)"), ps[:, 5 + n % 2, :])\
                            .then_inc(l_pT_in.sem, 1)

                    def exps(n):
                        t, a = divmod(n, PAIRS)
                        k = l * ALL_PAIRS + n + 1
                        lo = P if t == 0 else BACK
                        act.wait_ge(l_max.sem, l_max.at(b, k))
                        if t >= 1:
                            act.wait_ge(l_pps.sem, l_pps.at(b, k - PAIRS))
                        for h in (2 * a, 2 * a + 1):
                            o = (BACK + P) * (h % 2)
                            last = act.activation(l_p[:, h, lo:2 * P], ps[:, 3 + a % 2, o + lo - BACK:o + BACK + P],
                                                  ACT.Exp, bias=l_nb[:, h:h + 1], scale=l_sc[:, t % 2, h:h + 1],
                                                  accum_out=l_sum[:, h:h + 1])
                        last.then_inc(l_exp.sem, 1)

                    squares(0)
                    squares(1)
                    turned_q(0)
                    for n in range(SLOTS):
                        t, a = divmod(n, PAIRS)
                        if 0 <= n - LAG < ALL_PAIRS:
                            turned_probs(n - LAG)
                        if n < ALL_PAIRS:
                            exps(n)
                        w = n - LAG - 1
                        if w >= 0 and w % PAIRS == PAIRS - 1:
                            act.wait_ge(l_pv.sem, l_pv.at(b, l * ALL_PAIRS + w + 1))
                            act.copy(l_oT[:, :, :].rearrange("p a n -> p (a n)"), ps[:, 7, :]).then_inc(l_o.sem, 1)
                        if a == 3 and t + 1 < T:
                            turned_q(t + 1)
                        if a == 3 and t + 2 < T:
                            squares(t + 2)
                    act.wait_ge(l_shps.sem, l_shps.at(b, l + 1))
                    act.copy(xn[:, :, 64:P], ps[:, 1, 0:T * 64].rearrange("p (t d) -> p t d", t=T)).then_inc(l_sh.sem, 1)
                    act.wait_ge(s_turned.sem, s_turned.at(b, 6 + 2 * l))
                    act.activation(xT[:, :], ps[:, 0, :], ACT.Identity, bias=lngb_sb[:, l, 1:2],
                                   scale=lngb_sb[:, l, 0:1]).then_inc(s_cols.sem, 1)
                    for c, (_, m) in enumerate(FF):
                        i = 3 * l + c + 1
                        act.wait_ge(f_up.sem, f_up.at(b, i))
                        if c >= 2:
                            act.wait_ge(f_hid.sem, f_hid.at(b, i - 2))
                        act.activation(act_h[0:m, c % 2, :], ps[0:m, 2 + 2 * (c % 2), :], ACT.Gelu,
                                       bias=fb1_sb[0:m, l, 1, c:c + 1]).then_inc(f_act.sem, 1)

        @block.vector
        def _(dve):
            dve.wait_ge(s_w.sem, LOADED)
            dve.memset(waug[:, :, :, :, :, :], 0.0)
            dve.tensor_copy(ident_bf[:, :], ident)
            dve.tensor_copy(sel[:, :, :], sel_f[:, :, :])
            dve.tensor_copy(band[:, :, :], band_f[:, :, :])
            dve.tensor_scalar(alpha_sb[:, 1:2], alpha_sb[:, 0:1], -1.0, 1.0, ALU.mult, ALU.add)
            dve.drain()
            for i in range(3):
                for r in range(3):
                    dve.tensor_copy(waug[:, i, :, :, r, :],
                                    w1_in[:, i, :].rearrange("p (g j d) -> p g j d", g=G, d=HD))
            H = LD // 2
            for l in range(LAYERS):
                for i in range(2):
                    sc = qks_sb[:, l, i, :].unsqueeze(1).to_broadcast([P, T, LD])
                    dve.tensor_tensor(rot[:, l, 2 * i, :, :], rot_in[:, 2 * i, :, :], sc, ALU.mult)
                    for a in range(2):
                        dve.tensor_tensor(rot[:, l, 2 * i + 1, :, a * H:(a + 1) * H],
                                          rot_in[:, 2 * i + 1, :, a * H:(a + 1) * H],
                                          qks_sb[:, l, i, (1 - a) * H:(2 - a) * H].unsqueeze(1).to_broadcast([P, T, H]),
                                          ALU.mult)
            dve.drain().then_inc(s_const.sem, 1)

            def moments(src, var):
                for t in range(T):
                    dve.bn_stats(ln_st[:, t, :], src[:, t, :])
                dve.drain()
                for t in range(T):
                    dve.bn_aggr(ln_mv[:, t, :], ln_st[:, t, :])
                dve.drain()
                dve.tensor_scalar(ln_ve[:, :], ln_mv[:, :, 1], EPS, None, ALU.add).then_inc(var.sem, 1)

            def normed(src, dst):
                for t in range(T):
                    dve.tensor_scalar(dst[:, t, :], src[:, t, :], ln_mv[:, t, 0:1], ln_rs[:, t:t + 1],
                                      ALU.subtract, ALU.mult)
                dve.drain()

            with dve.Fori(0, B) as b:
                dve.wait_ge(p_x.sem, p_x.at(b, 16))
                moments(x_in, p_var)
                dve.wait_ge(p_rstd.sem, p_rstd.at(b, 1))
                normed(x_in, xn)
                dve.drain().then_inc(p_rows.sem, 1)
                dve.drain().then_inc(p_used.sem, 1)
                for i in range(3):
                    dve.wait_ge(p_kept.sem, p_kept.at(b, i + 1))
                    dve.bn_stats(h_stats[:, i, bass.ds(b, 1), :].rearrange("p o s -> p (o s)"), sig[:, i, :])\
                        .then_inc(p_stat.sem, 1)
                dve.wait_ge(p_turned.sem, p_turned.at(b, 1))
            dve.drain()
            for i in range(3):
                dve.bn_aggr(h_mv[:, i, :], h_stats[:, i, :, :].rearrange("p b s -> p (b s)"))
            dve.drain()
            dve.tensor_scalar(bn[:, 0, :], h_mv[:, :, 1], EPS, None, ALU.add).then_inc(n_var.sem, 1)
            dve.wait_ge(n_rstd.sem, 1)
            dve.scalar_tensor_tensor(bn[:, 2, :], bn[:, 1, :], 4.0, gb_sb[:, 0:6:2], ALU.mult, ALU.mult)
            dve.tensor_scalar(bn[:, 4, :], gb_sb[:, 1:6:2], 4.0, -4.0, ALU.mult, ALU.add)
            dve.drain()
            dve.tensor_tensor(bn[:, 0, :], bn[:, 2, :], h_mv[:, :, 0], ALU.mult)
            dve.drain()
            dve.tensor_tensor(bn[:, 3, :], bn[:, 4, :], bn[:, 0, :], ALU.subtract).then_inc(n_aff.sem, 1)

            with dve.Fori(0, B) as b:
                def norm(k, src, dst):
                    moments(src, s_var)
                    dve.wait_ge(s_rstd.sem, s_rstd.at(b, k))
                    normed(src, dst)

                def rows_ready():
                    dve.drain().then_inc(s_rows.sem, 1)

                dve.wait_ge(s_sig.sem, s_sig.at(b, 2))
                dve.tensor_tensor(sig[:, 0, :], sig[:, 0, :], sig[:, 1, :], ALU.mult).then_inc(s_qk.sem, 1)
                dve.wait_ge(s_vvps.sem, s_vvps.at(b, 1))
                dve.tensor_tensor(vv[:, :], ps[:, 1, 0:P], blocks, ALU.mult).then_inc(s_vv.sem, 1)
                dve.wait_ge(s_oput.sem, s_oput.at(b, 1))
                dve.tensor_tensor(o_rows[:, :, :], ps[:, 2, :].rearrange("p (t d) -> p t d", t=T),
                                  bp_sb[:, :].unsqueeze(1).to_broadcast([P, T, D]), ALU.add)
                dve.drain()
                norm(1, o_rows, o_rows)
                dve.wait_ge(s_x.sem, s_x.at(b, 16))
                dve.tensor_tensor(xa[:, :, :], x_in[:, :, :], o_rows[:, :, :], ALU.add)
                dve.drain().then_inc(s_xused.sem, 1)

                norm(2, xa, xn)
                rows_ready()
                dve.wait_ge(s_logit.sem, s_logit.at(b, 1))
                dve.tensor_copy(logit[:, :, :], ps[:, 6, 0:T * EXPERTS].rearrange("p (t e) -> p t e", t=T))
                dve.drain()
                for t in range(T):
                    dve.max(top_v[:, t, :], logit[:, t, :])
                dve.drain()
                dve.tensor_tensor(top_d[:, :], top_v[:, :, 1], top_v[:, :, 0], ALU.subtract).then_inc(s_top.sem, 1)
                for t in range(T):
                    dve.max_index(top_i[:, t, :], top_v[:, t, :], logit[:, t, :])
                dve.drain()
                dve.tensor_copy(top_if[:, :, :], top_i[:, :, 0:2])
                dve.drain()
                iota_b = iota.unsqueeze(1).to_broadcast([P, T, EXPERTS])
                for i in range(2):
                    dve.tensor_tensor(disp[:, i, :, :], iota_b,
                                      top_if[:, :, i].unsqueeze(2).to_broadcast([P, T, EXPERTS]), ALU.is_equal)
                dve.drain()
                dve.wait_ge(s_topw.sem, s_topw.at(b, 1))
                for i in range(2):
                    dve.tensor_tensor(disp[:, 2 + i, :, :], disp[:, i, :, :],
                                      top_w[:, i, :].unsqueeze(2).to_broadcast([P, T, EXPERTS]), ALU.mult)
                dve.drain()
                dve.tensor_tensor(disp[:, 0, :, :], disp[:, 2, :, :], disp[:, 3, :, :], ALU.add)
                dve.drain()
                E = EXPERTS
                dve.tensor_copy(disp_p[:, :, 0:E], disp[:, 0, :, :])
                dve.drain()
                dve.tensor_tensor(disp[:, 1, :, :], disp[:, 0, :, :], disp_p[:, :, 0:E], ALU.subtract)
                dve.drain()
                dve.tensor_copy(disp_p[:, :, E:2 * E], disp[:, 1, :, :])
                dve.drain()
                dve.tensor_tensor(disp_p[:, :, 2 * E:3 * E], disp[:, 1, :, :], disp_p[:, :, E:2 * E], ALU.subtract)\
                    .then_inc(s_disp.sem, 1)
                for n in range(UNITS):
                    dve.wait_ge(s_silu.sem, s_silu.at(b, n + 1))
                    if n >= 2:
                        dve.wait_ge(s_down.sem, s_down.at(b, n - 1))
                    dve.tensor_tensor(hid[:, n % 2, :], ps[:, 3 + n % 2, :], act_h[:, n % 2, :], ALU.mult)\
                        .then_inc(s_hid.sem, 1)
                dve.wait_ge(s_down.sem, s_down.at(b, UNITS))
                norm(3, ps[:, 7, :].rearrange("p (t d) -> p t d", t=T), o_rows)
                dve.tensor_tensor(xb[:, :, :], xa[:, :, :], o_rows[:, :, :], ALU.add)
                dve.drain()

                norm(4, xb, xn)
                rows_ready()
                def parts(i):
                    g, kind = divmod(i, 3)
                    dve.wait_ge(s_rnd.sem, s_rnd.at(b, i + 1))
                    dst = rnd[:, i % 2, :] if kind == 0 else kk[:, kind - 1, g, :]
                    dve.scalar_tensor_tensor(dst, rnd[:, i % 2, :], (q_low, k_low, kp_low)[kind],
                                             ps[:, proj_bank(i), :], ALU.mult, ALU.add).then_inc(s_part.sem, 1)

                def maxima(n):
                    s, j, qt = n // 16, n // T % 4, n % T
                    g, a = divmod(s, 2)
                    if g >= 2 and n % 32 == 0:
                        dve.wait_ge(s_mps.sem, s_mps.at(b, g - 1))
                    dve.wait_ge(s_aps.sem, s_aps.at(b, n + 1))
                    dve.tensor_reduce(mx[:, g % 2, qt, 2 * j + a:2 * j + a + 1], ps[:, 3 + n % 3, :], AX.X, ALU.max,
                                      negate=True).then_inc(s_amax.sem, 1)

                def output(s):
                    g, a = divmod(s, 2)
                    dve.wait_ge(s_ops.sem, s_ops.at(b, s + 1))
                    o = ps[:, 7, :].rearrange("p (t j c) -> p t j c", t=T, j=4)
                    dve.reciprocal(rec[:, :, :], o[:, :, :, HD])
                    dve.drain()
                    dve.tensor_scalar(rec[:, :, :], rec[:, :, :], alpha_sb[:, a:a + 1], None, ALU.mult)
                    dve.drain()
                    dst = att[:, :, 32 * g:32 * g + 32].rearrange("p t (j d) -> p t j d", j=4)
                    rec_b = rec[:, :, :].unsqueeze(3).to_broadcast([P, T, 4, HD])
                    dve.tensor_tensor(dst if a == 0 else o_nrm[:, :, :, :], o[:, :, :, 0:HD], rec_b, ALU.mult)\
                        .then_inc(s_onrm.sem, 1)
                    dve.drain()
                    if a == 1:
                        dve.tensor_tensor(dst, dst, o_nrm[:, :, :, :], ALU.add)
                        dve.drain()

                for i in range(3):
                    parts(i)
                for n in range(AHEAD):
                    maxima(n)
                    if n - 2 in PROJECT_EARLY:
                        parts(PROJECT_EARLY[n - 2])
                for k in range(8 * STEPS):
                    for n in maxima_in(k):
                        maxima(n)
                    if k - 1 in PROJECT_IN:
                        parts(PROJECT_IN[k - 1])
                    if k % 8 == 7 and k >= 8:
                        output(k // 8 - 1)
                output(STEPS - 1)
                rows_ready()
                dve.wait_ge(s_lout.sem, s_lout.at(b, 1))
                norm(5, ps[:, 1, :].rearrange("p (t d) -> p t d", t=T), o_rows)
                dve.tensor_tensor(xc[:, :, :], xb[:, :, :], o_rows[:, :, :], ALU.add)
                dve.drain()

                norm(6, xc, y)
                rows_ready()
                for l in range(LAYERS):
                    def turned_k(t):
                        dve.wait_ge(l_kps.sem, l_kps.at(b, l * T + t + 1))
                        dve.tensor_copy(kT[:, :, t * P:(t + 1) * P], ps[:, 4, :].rearrange("p (a n) -> p a n", a=PAIRS))\
                            .then_inc(l_kT.sem, 1)

                    def sums(t):
                        i = l * T + t + 1
                        dve.wait_ge(l_sq.sem, l_sq.at(b, i))
                        if t >= 1:
                            dve.wait_ge(l_rn.sem, l_rn.at(b, i - 1))
                        dve.tensor_reduce(ssq[:, :, :], sq[:, :, :].rearrange("p i (h d) -> p i h d", d=LD), AX.X, ALU.add)
                        dve.drain()
                        dve.tensor_scalar(ssq[:, :, :], ssq[:, :, :], 1e-24, None, ALU.max).then_inc(l_ss.sem, 1)

                    def rotated(t, c):
                        src = ps[:, c, :].rearrange("p (h d) -> p h d", d=LD)
                        cos = rot[:, l, 2 * c, t, :].unsqueeze(1).to_broadcast([P, LH, LD])
                        dve.tensor_tensor(ra[:, :, :], src, cos, ALU.mult)
                        for a in range(2):
                            sin = rot[:, l, 2 * c + 1, t, a * H:(a + 1) * H].unsqueeze(1).to_broadcast([P, LH, H])
                            dve.tensor_tensor(rb[:, :, a * H:(a + 1) * H], src[:, :, (1 - a) * H:(2 - a) * H], sin,
                                              ALU.mult)
                        dve.drain()
                        dst = qk_rows[:, 0, :].rearrange("p (h d) -> p h d", d=LD) if c == 0 else ra[:, :, :]
                        dve.tensor_tensor(dst, ra[:, :, :], rb[:, :, :], ALU.add)\
                            .then_inc((l_qrow if c == 0 else l_kread).sem, 1)

                    def scaled_k(t):
                        i = l * T + t + 1
                        dve.wait_ge(l_rn.sem, l_rn.at(b, i))
                        dve.wait_ge(l_kread.sem, l_kread.at(b, i))
                        dve.tensor_tensor(qk_rows[:, 1, :].rearrange("p (h d) -> p h d", d=LD), ra[:, :, :],
                                          rn[:, t, 1, :].unsqueeze(2).to_broadcast([P, LH, LD]), ALU.mult)\
                            .then_inc(l_krow.sem, 1)

                    def local_max(n):
                        t, a = divmod(n, PAIRS)
                        r = slice(2 * a, 2 * a + 2)
                        if a == 0:
                            dve.wait_ge(l_rn.sem, l_rn.at(b, l * T + t + 1))
                            dve.tensor_scalar(l_sc[:, t % 2, :], rn[:, t, 0, :], 8.0, None, ALU.mult)
                        dve.wait_ge(l_s.sem, l_s.at(b, l * ALL_PAIRS + n + 1))
                        s2 = ps[:, 3 + a % 2, 0:2 * (BACK + P)].rearrange("p (e c) -> p e c", e=2)
                        dve.tensor_reduce(l_mx[:, r], s2[:, :, BACK if t == 0 else 0:], AX.X, ALU.max, negate=True)
                        dve.drain()
                        dve.tensor_tensor(l_nb[:, r], l_mx[:, r], l_sc[:, t % 2, r], ALU.mult).then_inc(l_max.sem, 1)

                    def reciprocals(n):
                        r = slice(2 * (n % PAIRS), 2 * (n % PAIRS) + 2)
                        dve.wait_ge(l_exp.sem, l_exp.at(b, l * ALL_PAIRS + n + 1))
                        dve.reciprocal(l_rec[:, r], l_sum[:, r]).then_inc(l_r.sem, 1)

                    sums(0)
                    rotated(0, 0)
                    dve.drain()
                    rotated(0, 1)
                    scaled_k(0)
                    turned_k(0)
                    for n in range(SLOTS):
                        t, a = divmod(n, PAIRS)
                        if n < ALL_PAIRS:
                            local_max(n)
                        if 1 <= n <= ALL_PAIRS:
                            reciprocals(n - 1)
                        if t + 1 < T:
                            if a == 0:
                                sums(t + 1)
                            elif a < 3:
                                rotated(t + 1, a - 1)
                            else:
                                scaled_k(t + 1)
                                turned_k(t + 1)
                        w = n - LAG - 1
                        if w >= 0 and w % PAIRS == PAIRS - 1:
                            u = w // PAIRS
                            dve.wait_ge(l_wo.sem, l_wo.at(b, l * T + u + 1))
                            dve.tensor_tensor(y[:, u, :], y[:, u, :], ps[:, 7, 0:D], ALU.add).then_inc(l_res.sem, 1)
                    dve.drain()
                    dve.tensor_copy(xn[:, :, 0:64], y[:, :, 0:64])
                    dve.drain()
                    dve.wait_ge(l_sh.sem, l_sh.at(b, l + 1))
                    norm(7 + l, xn, xn)
                    rows_ready()
                    for c, (_, m) in enumerate(FF):
                        i = 3 * l + c + 1
                        dve.wait_ge(f_act.sem, f_act.at(b, i))
                        if c >= 2:
                            dve.wait_ge(f_down.sem, f_down.at(b, i - 2))
                        dve.scalar_tensor_tensor(hid[0:m, c % 2, :], ps[0:m, 3 + 2 * (c % 2), :],
                                                 fb1_sb[0:m, l, 0, c:c + 1], act_h[0:m, c % 2, :],
                                                 ALU.add, ALU.mult).then_inc(f_hid.sem, 1)
                    dve.tensor_tensor(y[:, :, :], y[:, :, :], fb2_sb[:, l, :].unsqueeze(1).to_broadcast([P, T, D]), ALU.add)
                    dve.drain()
                    dve.wait_ge(f_down.sem, f_down.at(b, 3 * l + 3))
                    dve.tensor_tensor(y[:, :, :], y[:, :, :], ps[:, 6, :].rearrange("p (t d) -> p t d", t=T), ALU.add)
                    dve.drain()
                    if l + 1 < LAYERS:
                        rows_ready()
                norm(NORMS, y, o_rows)
                dve.tensor_tensor(xa[:, :, :], xc[:, :, :], o_rows[:, :, :], ALU.add)
                dve.drain().then_inc(s_final.sem, 1)
                dve.wait_ge(s_out.sem, s_out.at(b, 16))

        @block.tensor
        def _(pe):
            def turn(src, dst):
                for t in range(T):
                    last = pe.transpose(dst[:, t * P:(t + 1) * P], src[:, t, :], ident)
                return last

            pe.wait_ge(s_const.sem, 1)
            pe.wait_ge(s_zero.sem, 1)
            with pe.Fori(0, B) as b:
                pe.wait_ge(p_rows.sem, p_rows.at(b, 1))
                turn(xn, ps[:, 0, :]).then_inc(p_turned.sem, 1)
                pe.wait_ge(p_cols.sem, p_cols.at(b, 1))
                for i in range(3):
                    pe.matmul(ps[:, 1 + i, :], w0[:, i, :], xT[:, :], start=True, stop=True).then_inc(p_h.sem, 1)
                pe.wait_ge(p_kept.sem, p_kept.at(b, 3))
            with pe.Fori(0, B) as b:
                pe.wait_ge(s_sig.sem, s_sig.at(b, 3))
                for t in range(T):
                    last = pe.transpose(ps[:, 0, t * P:(t + 1) * P], sig[:, 2, t * P:(t + 1) * P], ident)
                last.then_inc(s_turned.sem, 1)
                pe.wait_ge(s_cols.sem, s_cols.at(b, 1))
                for t in range(T):
                    last = pe.matmul(ps[:, 1, 0:P], v_rows[:, t, :], v_rows[:, t, :], start=(t == 0), stop=(t == T - 1))
                last.then_inc(s_vvps.sem, 1)
                pe.wait_ge(s_vv.sem, s_vv.at(b, 1))
                pe.matmul(ps[:, 1, P:2 * P], vv[:, :], w0[:, 3, :], start=True, stop=True).then_inc(s_vvwps.sem, 1)
                pe.wait_ge(s_vvw.sem, s_vvw.at(b, 1))
                pe.wait_ge(s_qk.sem, s_qk.at(b, 1))
                for t in range(T):
                    last = pe.matmul(ps[:, 2, t * P:(t + 1) * P], sig[:, 0, t * P:(t + 1) * P], vvw[:, :],
                                     start=True, stop=True)
                last.then_inc(s_oput.sem, 1)

                def turn_rows(k, src):
                    pe.wait_ge(s_rows.sem, s_rows.at(b, k - 1))
                    turn(src, ps[:, 0, :]).then_inc(s_turned.sem, 1)

                turn_rows(2, xn)
                pe.wait_ge(s_cols.sem, s_cols.at(b, 2))
                for t in range(T):
                    last = pe.matmul(ps[:, 6, t * EXPERTS:(t + 1) * EXPERTS], xT[:, t * P:(t + 1) * P], gate_sb[:, :],
                                     start=True, stop=True)
                last.then_inc(s_logit.sem, 1)

                def down(n):
                    pe.wait_ge(s_hid.sem, s_hid.at(b, n + 1))
                    for t in range(T):
                        last = pe.matmul(ps[:, 7, t * P:(t + 1) * P], hid[:, n % 2, t * P:(t + 1) * P], wd_sb[:, n, :],
                                         start=(n == 0 and t == 0), stop=(n == UNITS - 1), skip_group_check=True)
                    last.then_inc(s_down.sem, 1)

                for n in range(UNITS):
                    if n == 2:
                        pe.wait_ge(s_disp.sem, s_disp.at(b, 1))
                        for t in range(T):
                            last = pe.matmul(ps[0:3 * EXPERTS, 5, t * P:(t + 1) * P], disp_p[:, t, :], ident_bf[:, :],
                                             start=True, stop=True)
                        last.then_inc(s_dispps.sem, 1)
                    if n >= 2:
                        pe.wait_ge(s_hid.sem, s_hid.at(b, n - 1))
                    pe.matmul(ps[:, 1 + n % 2, :], wa_sb[:, n, :], xT[:, :], start=True, stop=True)
                    if n < 2:
                        last = pe.matmul(ps[:, 3 + n % 2, :], wu_sb[:, n, :], xT[:, :], start=True, stop=True)
                    else:
                        if n == 2:
                            pe.wait_ge(s_dispT.sem, s_dispT.at(b, 1))
                        last = pe.matmul(ps[:, 3 + n % 2, :], sel[:, n - 2, :], disp_T[:, :], start=True, stop=True)
                    last.then_inc(s_up.sem, 1)
                    if n >= 1:
                        down(n - 1)
                down(UNITS - 1)

                turn_rows(3, xn)
                pe.wait_ge(s_cols.sem, s_cols.at(b, 3))

                def project_heads(i):
                    g, kind = divmod(i, 3)
                    pe.matmul(ps[:, proj_bank(i), :], waug[:, kind, g, :, :, :].rearrange("p j r d -> p (j r d)"),
                              xT[:, :], start=True, stop=True).then_inc(s_proj.sem, 1)

                def scores_for_maxima(n):
                    s, j, qt = n // 16, n // T % 4, n % T
                    g, a = divmod(s, 2)
                    if n % 32 == 0:
                        pe.wait_ge(s_qput.sem, s_qput.at(b, 64 * (g + 1)))
                    if n % 16 == 0:
                        pe.wait_ge(s_part.sem, s_part.at(b, 3 * g + 2 + a))
                    if n >= 3:
                        pe.wait_ge(s_amax.sem, s_amax.at(b, n - 2))
                    pe.matmul(ps[:, 3 + n % 3, :], qz[:, 4 * g + j, qt * P:(qt + 1) * P], kk[:, a, g, :],
                              start=True, stop=True).then_inc(s_aps.sem, 1)

                def turn_maxima(g):
                    pe.wait_ge(s_amax.sem, s_amax.at(b, 32 * (g + 1)))
                    for qt in range(T):
                        last = pe.transpose(ps[0:8, 7, qt * P:(qt + 1) * P], mx[:, g % 2, qt, :], ident)
                    last.then_inc(s_mps.sem, 1)

                def weigh(u, k):
                    s, half = divmod(u, 2)
                    kt = 2 * half + k
                    if k == 0:
                        pe.wait_ge(s_exp[1].sem, s_exp[1].at(b, 4 * u + 4))
                        if half == 0 and s >= 1:
                            pe.wait_ge(s_oT.sem, s_oT.at(b, s))
                    for j in range(4):
                        last = pe.matmul(ps[32 * j:32 * j + 32, 6, :], v_aug[:, kt, 4 * (s // 2) + j, :],
                                         prob[:, u % 2, j, k, :], start=(kt == 0), stop=(kt == T - 1))
                    if k == 1:
                        last.then_inc(s_pv.sem, 1)

                def turn_output(s):
                    pe.wait_ge(s_oT.sem, s_oT.at(b, s + 1))
                    for t in range(T):
                        last = pe.transpose(ps[:, 7, t * P:(t + 1) * P], oT[:, t * P:(t + 1) * P], ident)
                    last.then_inc(s_ops.sem, 1)

                for i in range(3):
                    project_heads(i)
                for t in range(T):
                    last = pe.matmul(ps[:, 7, t * P:(t + 1) * P], xT[:, t * P:(t + 1) * P], w1_sb[:, 0, :],
                                     start=True, stop=True)
                last.then_inc(s_vps.sem, 1)
                for n in range(AHEAD):
                    scores_for_maxima(n)
                    if n in PROJECT_EARLY:
                        i = PROJECT_EARLY[n]
                        pe.wait_ge(s_part.sem, s_part.at(b, i - 2))
                        project_heads(i)
                    if n == 34:
                        pe.wait_ge(s_vaug.sem, s_vaug.at(b, 1))
                        turn_maxima(0)
                free = (s_mT, 1)
                for k in range(8 * STEPS):
                    s, u, j = k // 8, k // 4, k % 4
                    g, a = divmod(s, 2)
                    if k == 0:
                        pe.wait_ge(s_part.sem, s_part.at(b, 6))
                    if k % 16 == 0:
                        pe.wait_ge(s_shift.sem, s_shift.at(b, 64 * (g + 1)))
                    ahead = maxima_in(k)
                    for i in range(2):
                        if i < len(ahead):
                            scores_for_maxima(ahead[i])
                        m, kt = 2 * k + i, 2 * (u % 2) + i
                        if m >= 3:
                            before = s_exp[(m - 3) % 2]
                            pe.wait_ge(before.sem, before.at(b, (m - 3) // 2 + 1))
                        pe.matmul(ps[:, m % 3, :], kk[:, a, g, kt * P:(kt + 1) * P], qz[:, 4 * g + j, :],
                                  start=True, stop=True).then_inc(s_sps.sem, 1)
                    if k >= 1 and maxima_done(k - 1) > maxima_done(k - 2):
                        m = maxima_done(k - 1) - 1
                        pe.wait_ge(free[0].sem, free[0].at(b, free[1]))
                        turn_maxima(m)
                        free = (s_mT, m + 1)
                    if k in PROJECT_IN:
                        pe.wait_ge(free[0].sem, free[0].at(b, free[1]))
                        project_heads(PROJECT_IN[k])
                        free = (s_part, PROJECT_IN[k] + 1)
                    if j % 2 and u >= 1:
                        weigh(u - 1, j // 2)
                    if k % 8 == 6 and s >= 1:
                        pe.wait_ge(free[0].sem, free[0].at(b, free[1]))
                        turn_output(s - 1)
                        free = (s_onrm, s)
                weigh(2 * STEPS - 1, 0)
                weigh(2 * STEPS - 1, 1)
                pe.wait_ge(free[0].sem, free[0].at(b, free[1]))
                turn_output(STEPS - 1)
                turn_rows(4, att)
                pe.wait_ge(s_cols.sem, s_cols.at(b, 4))
                for t in range(T):
                    last = pe.matmul(ps[:, 1, t * P:(t + 1) * P], xT[:, t * P:(t + 1) * P], w1_sb[:, 1, :],
                                     start=True, stop=True)
                last.then_inc(s_lout.sem, 1)

                for l in range(LAYERS):
                    turn_rows(5 + 2 * l, y)
                    pe.wait_ge(s_cols.sem, s_cols.at(b, 5 + 2 * l))

                    def project(t):
                        i = l * T + t + 1
                        if t >= 1:
                            pe.wait_ge(l_v.sem, l_v.at(b, i - 1))
                            pe.wait_ge(l_qrow.sem, l_qrow.at(b, i - 1))
                            pe.wait_ge(l_kread.sem, l_kread.at(b, i - 1))
                        for c in range(3):
                            last = pe.matmul(ps[:, c, :], hT[:, t * P:(t + 1) * P], wqkv_sb[:, l, c, :],
                                             start=True, stop=True)
                        last.then_inc(l_qkv.sem, 1)

                    def turn_q_or_k(t, c):
                        i = l * T + t + 1
                        rows, turned = ((l_qrow, l_qps), (l_krow, l_kps))[c]
                        pe.wait_ge(rows.sem, rows.at(b, i))
                        if t >= 1:
                            pe.wait_ge(l_exp.sem, l_exp.at(b, (i - 1) * PAIRS - 1 + c))
                        for a in range(PAIRS):
                            last = pe.transpose(ps[:, 3 + c, a * P:(a + 1) * P], qk_rows[:, c, a * P:(a + 1) * P], ident)
                        last.then_inc(turned.sem, 1)

                    def local_scores(n):
                        t, a = divmod(n, PAIRS)
                        if a == 0:
                            pe.wait_ge(l_qT.sem, l_qT.at(b, l * T + t + 1))
                            pe.wait_ge(l_kT.sem, l_kT.at(b, l * T + t + 1))
                        if a >= 2:
                            pe.wait_ge(l_exp.sem, l_exp.at(b, l * ALL_PAIRS + n - 1))
                        lo = BACK if t == 0 else 0
                        bank = 3 + a % 2
                        for e in range(2):
                            o = (BACK + P) * e
                            pe.matmul(ps[:, bank, o + lo:o + BACK + P], q_bd[:, 2 * a + e, t * P:(t + 1) * P],
                                      kT[:, a, t * P - BACK + lo:(t + 1) * P], start=(e == 0), stop=False,
                                      skip_group_check=True)
                        both = ps[:, bank, 0:2 * (BACK + P)].rearrange("p (e c) -> p e c", e=2)
                        pe.matmul(both[:, :, lo:], ident_bf[:, :], band[:, :, lo:], start=False, stop=True,
                                  skip_group_check=True).then_inc(l_s.sem, 1)

                    def turn_probs(n):
                        t, a = divmod(n, PAIRS)
                        k = l * ALL_PAIRS + n + 1
                        pe.wait_ge(l_pn.sem, l_pn.at(b, k))
                        if n >= 2:
                            pe.wait_ge(l_pT_in.sem, l_pT_in.at(b, k - 2))
                        for e in range(2):
                            for k in range(0 if t else 1, 2):
                                o = (2 * e + k) * P
                                last = pe.transpose(ps[:, 5 + a % 2, o:o + P], l_p[:, 2 * a + e, k * P:(k + 1) * P], ident)
                        last.then_inc(l_pps.sem, 1)

                    def local_weigh(n):
                        t, a = divmod(n, PAIRS)
                        pe.wait_ge(l_pT_in.sem, l_pT_in.at(b, l * ALL_PAIRS + n + 1))
                        if a == 0 and t >= 1:
                            pe.wait_ge(l_res.sem, l_res.at(b, l * T + t))
                        for e in range(2):
                            h = 2 * a + e
                            for k in range(0 if t else 1, 2):
                                last = pe.matmul(ps[64 * e:64 * e + 64, 7, a * P:(a + 1) * P],
                                                 v_loc[:, t - 1 + k, h * LD:(h + 1) * LD], l_pT[:, a % 2, e, k, :],
                                                 start=(a == 0 and k == (0 if t else 1)), stop=(k == 1),
                                                 skip_group_check=True)
                        last.then_inc(l_pv.sem, 1)

                    project(0)
                    project(1)
                    turn_q_or_k(0, 0)
                    turn_q_or_k(0, 1)
                    for n in range(SLOTS):
                        t, a = divmod(n, PAIRS)
                        if 0 <= n - LAG < ALL_PAIRS:
                            turn_probs(n - LAG)
                        if n < ALL_PAIRS:
                            local_scores(n)
                        w = n - LAG - 1
                        if w >= 0:
                            local_weigh(w)
                        if a == 3 and t + 1 < T:
                            turn_q_or_k(t + 1, 0)
                            if t + 2 < T:
                                project(t + 2)
                            turn_q_or_k(t + 1, 1)
                        if w >= 0 and w % PAIRS == PAIRS - 1:
                            pe.wait_ge(l_o.sem, l_o.at(b, l * T + w // PAIRS + 1))
                            for a in range(PAIRS):
                                last = pe.matmul(ps[:, 7, 0:D], l_oT[:, a, :], wo_sb[:, l, a, :],
                                                 start=(a == 0), stop=(a == PAIRS - 1))
                            last.then_inc(l_wo.sem, 1)

                    pe.wait_ge(l_res.sem, l_res.at(b, l * T + T))
                    pe.matmul(ps[:, 1, 0:T * 64].rearrange("p (t d) -> p t d", t=T), shift, y[:, :, 64:P],
                              start=True, stop=False)
                    pe.matmul(ps[:, 1, 64:T * 64].rearrange("p (t d) -> p t d", t=T - 1), carry, y[:, 0:T - 1, 64:P],
                              start=False, stop=True).then_inc(l_shps.sem, 1)
                    turn_rows(6 + 2 * l, xn)
                    pe.wait_ge(s_cols.sem, s_cols.at(b, 6 + 2 * l))

                    def ff_down(c):
                        m = FF[c][1]
                        pe.wait_ge(f_hid.sem, f_hid.at(b, 3 * l + c + 1))
                        for t in range(T):
                            last = pe.matmul(ps[:, 6, t * P:(t + 1) * P], hid[0:m, c % 2, t * P:(t + 1) * P],
                                             fw2_sb[0:m, l, c, :], start=(c == 0 and t == 0), stop=(c == 2),
                                             skip_group_check=True)
                        last.then_inc(f_down.sem, 1)

                    for c, (o, m) in enumerate(FF):
                        if c >= 2:
                            pe.wait_ge(f_hid.sem, f_hid.at(b, 3 * l + c - 1))
                        for a in range(2):
                            w = (1 - a) * HID_F + o
                            last = pe.matmul(ps[0:m, 2 + 2 * (c % 2) + a, :], fw1_sb[:, l, w:w + m], xT[:, :],
                                             start=True, stop=True)
                        last.then_inc(f_up.sem, 1)
                        if c >= 1:
                            ff_down(c - 1)
                    ff_down(2)


def rotary_tables():
    half = np.arange(0, LD, 2, dtype=np.float32)
    inv_freq = (np.float32(1.0) / np.float32(10000.0) ** (half / np.float32(LD))).astype(np.float32)
    t = np.arange(N, dtype=np.float32)
    freqs = (t[:, None] * inv_freq[None, :]).astype(np.float32)
    freqs = np.concatenate([freqs, freqs], axis=-1)
    base = (half + np.float32(0.4 * LD)) / np.float32(1.4 * LD)
    power = (t - N // 2) / np.float32(32.0)
    scale = base[None, :] ** power[:, None]
    scale = np.concatenate([scale, scale], axis=-1)
    sign = np.where(np.arange(LD) < LD // 2, -1.0, 1.0).astype(np.float32)
    cos, sin = np.cos(freqs), np.sin(freqs) * sign
    tables = np.stack([cos * scale, sin * scale, cos / scale, sin / scale])
    return tables.astype(np.float32).reshape(4, T, P, LD).transpose(2, 0, 1, 3)


def constants():
    mats = np.zeros((P, 4, P), np.float32)
    mats[:, 0] = np.eye(P)
    mats[:, 1] = np.eye(P, k=1)
    mats[P - 1, 2, 0] = 1.0
    mats[:, 3] = np.kron(np.eye(HEADS), np.ones((HD, HD))) * HD ** -0.5
    sel = np.zeros((3 * EXPERTS, 8, P), np.float32)
    for e in range(EXPERTS):
        sel[e::EXPERTS, e // 2, HID_E * (e % 2):HID_E * (e % 2) + HID_E] = 1.0
    q, c = np.arange(P)[:, None], np.arange(BACK + P)[None, :]
    band = np.repeat(np.where((q <= c) & (c <= q + BACK), 0.0, NEG)[:, None, :], 2, axis=1)
    small = np.zeros((P, 81), np.float32)
    small[:, 48 + HD] = 1.0
    small[:, 0:16] = -0.5
    small[:, 16:32] = np.arange(16)
    r = np.arange(P) % 32
    small[:, 32] = np.where((r >= 16) & (r < 24), -1.0, 0.0)
    for i in range(2):
        small[:, 33 + i] = np.where((r >= 8) & (r < 16), -1.0, 0.0) + (r == 24 + i)
        small[:, 35 + i] = r == 24 + i
    return [mats, sel, band.astype(np.float32), small, rotary_tables()]


def kernel(**inputs):
    import concourse.bacc as bacc
    from concourse.bass_utils import run_bass_kernel_spmd

    i = {k: np.asarray(v) for k, v in inputs.items()}
    L0, F0, L1, F1 = "L0_attn_", "L0_ffn_", "L1_attn_", "L1_ffn_"

    def cat(parts, axis=1):
        return np.concatenate(parts, axis=axis)

    def rows(v, shape):
        return np.broadcast_to(v, shape)

    fb1 = np.zeros((LAYERS, 2, 3 * P), np.float32)
    fb1[:, :, 0:HID_F] = i[F1 + "b1"].reshape(LAYERS, 2, HID_F)
    fw2 = np.zeros((LAYERS, 3 * P, D), np.float32)
    fw2[:, 0:HID_F] = i[F1 + "w2"]
    arrays = {
        "x": i[L0 + "x"],
        "wl0": np.stack([i[L0 + w].T for w in ("Wq", "Wk", "Wv", "Wp")], axis=1),
        "gb": np.stack([i[L0 + w] for w in ("gq", "bq", "gk", "bk", "gv", "bv")], axis=1),
        "bp": rows(i[L0 + "bp"], (P, D)),
        "gate": i[F0 + "gate_w"].T,
        "ew_a": cat([i[F0 + "sfc1"].T, i[F0 + "w1"].reshape(EXPERTS * HID_E, D).T]).reshape(D, UNITS, P),
        "ew_u": i[F0 + "sfc2"].T.reshape(D, 2, P),
        "ew_d": cat([i[F0 + "sfc3"].T, i[F0 + "w2"].transpose(0, 2, 1).reshape(EXPERTS * HID_E, D)], 0)
                .reshape(UNITS, P, D).transpose(1, 0, 2),
        "wl1": np.stack([i[L1 + w].T for w in ("W_Q", "W_K", "W_K_prime", "W_V", "W_O")], axis=1),
        "alpha": rows(i[L1 + "alpha"].reshape(1, 1), (P, 1)),
        "wqkv": i[F1 + "wqkv"].reshape(LAYERS, D, 3, INNER).transpose(1, 0, 2, 3),
        "qks": rows(np.stack([i[F1 + "q_scale"], i[F1 + "k_scale"]], axis=1)[None], (P, LAYERS, 2, LD)),
        "wo": i[F1 + "wo"].reshape(LAYERS, PAIRS, P, D).transpose(2, 0, 1, 3),
        "lngb": np.stack([i[F1 + "ln_g"], i[F1 + "ln_b"]], axis=1).transpose(2, 0, 1),
        "fw1": i[F1 + "w1"].transpose(1, 0, 2),
        "fb1": fb1.reshape(LAYERS, 2, 3, P).transpose(3, 0, 1, 2),
        "fw2": fw2.reshape(LAYERS, 3, P, D).transpose(2, 0, 1, 3),
        "fb2": rows(i[F1 + "b2"][None], (P, LAYERS, D)),
    }
    for name, a in zip(("c_mat", "c_sel", "c_band", "c_small", "c_rot"), constants()):
        arrays[name] = a
    arrays = {k: np.ascontiguousarray(a) for k, a in arrays.items()}

    nc = bacc.Bacc("TRN2", target_bir_lowering=False, num_devices=1)
    args = [nc.dram_tensor(k, a.shape, mybir.dt.from_np(a.dtype), kind="ExternalInput").ap() for k, a in arrays.items()]
    args.append(nc.dram_tensor("out", (B, N, D), F32, kind="ExternalOutput").ap())
    build(nc, *args)
    result = run_bass_kernel_spmd(nc, [arrays], core_ids=[0])
    return result.results[0]["out"]
```

```python
from contextlib import ExitStack

import numpy as np
import concourse.bass as bass
from concourse import mybir

ALU = mybir.AluOpType
ACT = mybir.ActivationFunctionType
AX = mybir.AxisListType
F32 = mybir.dt.float32
F32R = mybir.dt.float32r
BF16 = mybir.dt.bfloat16
U32 = mybir.dt.uint32

P = 128
B, N, D = 8, 512, 128
T = N // P
EPS = 1e-5
NEG = -1e30

EXPERTS, HID_E, SHARED = 16, 64, 256
UNITS = SHARED // P + EXPERTS * HID_E // P
HEADS, HD = 16, 8
G = HEADS // 4
LAYERS, LH, LD = 2, 8, 64
INNER = LH * LD
PAIRS = LH // 2
BACK = 64
HID_F = 341
FF = [(0, 128), (128, 128), (256, HID_F - 256)]


class Signal:

    def __init__(self, sem, per, start=0):
        self.sem, self.per, self.start = sem, per, start

    def at(self, b, k):
        return b * self.per + (self.start + k)


def build(nc, x, wl0, gb, bp, gate, ew_a, ew_u, ew_d, wl1, alpha, wqkv, qks, wo, lngb, fw1, fb1, fw2, fb2,
          c_mat, c_sel, c_band, c_small, c_rot, out):
    ctx = ExitStack()
    with ctx:
        def sb(name, shape, dt=F32):
            return ctx.enter_context(nc.sbuf_tensor(name, shape, dt))

        def signal(name, per=1, start=0):
            return Signal(ctx.enter_context(nc.semaphore(name)), per, start)

        ps = ctx.enter_context(nc.psum_tensor("ps", [P, 8, 512], F32))

        arena = ctx.enter_context(nc.sbuf_tensor("arena", [P, 8192], F32))

        arena2 = ctx.enter_context(nc.sbuf_tensor("arena2", [P, 4096], F32))

        def part(start, *dims, arena=arena):
            names = "abcdef"[:len(dims)]
            size = int(np.prod(dims))
            flat = arena[:, start:start + size]
            if len(dims) == 1:
                return flat
            return flat.rearrange(f"p ({' '.join(names)}) -> p {' '.join(names)}", **dict(zip(names, dims)))

        w0 = sb("w0", [P, 4, D])
        gb_sb = sb("gb_sb", [P, 6])
        bp_sb = sb("bp_sb", [P, D])
        gate_sb = sb("gate_sb", [P, EXPERTS])
        wa_sb = sb("wa_sb", [P, UNITS, P])
        wu_sb = sb("wu_sb", [P, 2, P])
        wd_sb = sb("wd_sb", [P, UNITS, D])
        w1_in = part(2560, 3, D)
        w1_sb = sb("w1_sb", [P, 2, D])
        waug = sb("waug", [P, 3, G, 4, 4, HD])
        alpha_sb = sb("alpha_sb", [P, 2])
        wqkv_sb = sb("wqkv_sb", [P, LAYERS, 3, INNER])
        qks_sb = sb("qks_sb", [P, LAYERS, 2, LD])
        wo_sb = sb("wo_sb", [P, LAYERS, PAIRS, D])
        lngb_sb = sb("lngb_sb", [P, LAYERS, 2])
        fw1_sb = sb("fw1_sb", [P, LAYERS, 2 * HID_F])
        fb1_sb = sb("fb1_sb", [P, LAYERS, 2, 3])
        fw2_sb = sb("fw2_sb", [P, LAYERS, 3, D])
        fb2_sb = sb("fb2_sb", [P, LAYERS, D])
        mats = sb("mats", [P, 4, P])
        ident, shift, carry, blocks = (mats[:, i, :] for i in range(4))
        ident_bf = sb("ident_bf", [P, P], BF16)
        sel_f = part(0, 8, P)[0:3 * EXPERTS]
        sel = sb("sel", [3 * EXPERTS, 8, P], BF16)
        band_f = part(1024, 2, BACK + P)
        band = sb("band", [P, 2, BACK + P], BF16)
        small = sb("small", [P, 81])
        half_neg = small[:, 0:16]
        iota = small[:, 16:32]
        one_at_hd, zero = small[:, 48:80], small[:, 80:81]
        q_low, k_low, kp_low, k_one, kp_one = (small[:, 32 + i:33 + i] for i in range(5))
        rot_in = part(1536, 4, T, LD)
        rot = sb("rot", [P, LAYERS, 4, T, LD])

        h_stats = sb("h_stats", [P, 3, B, 6])
        h_mv = sb("h_mv", [P, 3, 2])
        bn = sb("bn", [P, 5, 3])
        sig = part(2048, 3, N, arena=arena2)
        vv = sb("vv", [P, D])
        vvw = sb("vvw", [P, D])

        x_in = sb("x_in", [P, T, D])
        xa = sb("xa", [P, T, D])
        xb = sb("xb", [P, T, D])
        xc = sb("xc", [P, T, D])
        o_rows = sb("o_rows", [P, T, D])
        xn = sb("xn", [P, T, D])
        xT = sb("xT", [P, N])
        hT = sb("hT", [P, N])
        y = sb("y", [P, T, D])
        ln_st = sb("ln_st", [P, T, 6])
        ln_mv = sb("ln_mv", [P, T, 2])
        ln_ve = sb("ln_ve", [P, T])
        ln_rs = sb("ln_rs", [P, T])
        ln_nm = sb("ln_nm", [P, T])

        logit = sb("logit", [P, T, EXPERTS])
        top_v = sb("top_v", [P, T, 8])
        top_i = sb("top_i", [P, T, 8], U32)
        top_if = sb("top_if", [P, T, 2])
        top_d = sb("top_d", [P, T])
        top_w = sb("top_w", [P, 2, T])
        disp = sb("disp", [P, 4, T, EXPERTS])
        disp_p = sb("disp_p", [P, T, 3 * EXPERTS], BF16)
        disp_T = sb("disp_T", [3 * EXPERTS, N], BF16)
        act_h = sb("act_h", [P, 2, N])
        hid = sb("hid", [P, 2, N])

        rnd = sb("rnd", [P, 2, N], F32R)
        qz = sb("qz", [P, HEADS, N], F32R)
        kk = sb("kk", [P, 2, G, N], F32R)
        v_aug = part(0, T, HEADS, 32, arena=arena2)
        mx = sb("mx", [P, 2, T, 8])
        mxT = sb("mxT", [8, 2, N], F32R)
        prob = part(0, 2, 4, 2, N)
        oT = sb("oT", [P, N])
        rec = sb("rec", [P, T, 4])
        o_nrm = sb("o_nrm", [P, T, 4, HD])
        att = o_rows

        sq = part(0, 2, INNER)
        ssq = sb("ssq", [P, 2, LH])
        rn = sb("rn", [P, T, 2, LH])
        ra = part(1024, LH, LD)
        rb = part(1536, LH, LD)
        qk_rows = part(2048, 2, INNER)
        v_rows = part(3072, T, D)
        q_bd = part(0, LH, N, arena=arena2)
        rq = hid
        kT = part(3072, PAIRS, N)
        v_loc = part(5120, T, INNER)
        rows_of = (y, o_rows, y)
        half_st = sb("half_st", [P, 2, 2, 6])
        l_mx = sb("l_mx", [P, LH])
        l_sc = sb("l_sc", [P, 2, LH])
        l_nb = sb("l_nb", [P, LH])
        l_sum = sb("l_sum", [P, LH])
        l_rec = sb("l_rec", [P, LH])
        l_p = sb("l_p", [P, LH, 2 * P])
        l_pT = part(7168, 2, 2, 2, P)
        l_oT = oT[:, :].rearrange("p (a n) -> p a n", a=PAIRS)

        s_w0 = signal("s_w0")
        s_w = signal("s_w")
        s_const = signal("s_const")
        s_zero = signal("s_zero")
        p_x = signal("p_x", 16)
        p_used = signal("p_used")
        p_var = signal("p_var")
        p_rstd = signal("p_rstd")
        p_rows = signal("p_rows")
        p_turned = signal("p_turned")
        p_cols = signal("p_cols")
        p_h = signal("p_h", 3)
        p_kept = signal("p_kept", 3)
        p_store = signal("p_store", 16)
        p_stat = signal("p_stat", 3)
        n_var = signal("n_var")
        n_rstd = signal("n_rstd")
        n_aff = signal("n_aff")

        NORMS = 3 + 1 + 2 * LAYERS + 1
        s_x = signal("s_x", 16)
        s_h = signal("s_h", 16)
        s_xused = signal("s_xused")
        s_var = signal("s_var", NORMS)
        s_rstd = signal("s_rstd", NORMS)
        TURNS = 2 + 4 * LAYERS
        s_rows = signal("s_rows", 2 * T + 2 * (TURNS - 2))
        s_turned = signal("s_turned", TURNS)
        s_cols = signal("s_cols", TURNS)
        s_vone = signal("s_vone")
        s_qzero = signal("s_qzero")
        a_var = signal("a_var", 2)
        a_rstd = signal("a_rstd", 2)
        a_rows = signal("a_rows", T)
        a_turned = signal("a_turned", 2)
        a_cols = signal("a_cols", 2)
        s_sig = signal("s_sig", 3)
        s_qk = signal("s_qk")
        s_vvps = signal("s_vvps")
        s_vv = signal("s_vv")
        s_vvwps = signal("s_vvwps")
        s_vvw = signal("s_vvw")
        s_oput = signal("s_oput")
        s_logit = signal("s_logit")
        s_top = signal("s_top")
        s_topw = signal("s_topw")
        s_disp = signal("s_disp")
        s_dispps = signal("s_dispps")
        s_dispT = signal("s_dispT")
        s_up = signal("s_up", UNITS)
        s_silu = signal("s_silu", UNITS)
        s_hid = signal("s_hid", UNITS)
        s_down = signal("s_down", UNITS)
        s_vps = signal("s_vps")
        s_vaug = signal("s_vaug")
        s_proj = signal("s_proj", 3 * G)
        s_rnd = signal("s_rnd", 3 * G)
        s_part = signal("s_part", 3 * G)
        s_qput = signal("s_qput", 64 * G)
        s_aps = signal("s_aps", 2 * HEADS * T)
        s_amax = signal("s_amax", 2 * HEADS * T)
        s_mps = signal("s_mps", G)
        s_mT = signal("s_mT", G)
        s_shift = signal("s_shift", 16 * HEADS)
        s_sps = signal("s_sps", 8 * 4 * G)
        s_exp = [signal(f"s_exp{i}", 4 * 4 * G) for i in range(2)]
        s_pv = signal("s_pv", 4 * G)
        s_oT = signal("s_oT", 2 * G)
        s_ops = signal("s_ops", 2 * G)
        s_onrm = signal("s_onrm", 2 * G)
        s_lout = signal("s_lout")
        l_qkv = signal("l_qkv", 3 * LAYERS * T)
        l_sq = signal("l_sq", LAYERS * T)
        l_v = signal("l_v", LAYERS * T)
        l_ss = signal("l_ss", LAYERS * T)
        l_rnk = signal("l_rnk", LAYERS * T)
        l_rnq = signal("l_rnq", LAYERS * T)
        l_qprod = signal("l_qprod", LAYERS * T)
        l_qrow = signal("l_qrow", LAYERS * T)
        l_kread = signal("l_kread", LAYERS * T)
        l_krow = signal("l_krow", LAYERS * T)
        l_qps = signal("l_qps", LAYERS * T)
        l_kps = signal("l_kps", LAYERS * T)
        l_qT = signal("l_qT", LAYERS * T)
        l_kT = signal("l_kT", LAYERS * T)
        l_s = signal("l_s", LAYERS * T * PAIRS)
        l_max = signal("l_max", LAYERS * T * PAIRS)
        l_exp = signal("l_exp", LAYERS * T * PAIRS)
        l_r = signal("l_r", LAYERS * T * PAIRS)
        l_pn = signal("l_pn", LAYERS * T * PAIRS)
        l_pps = signal("l_pps", LAYERS * T * PAIRS)
        l_pT_in = signal("l_pT_in", LAYERS * T * PAIRS)
        l_pv = signal("l_pv", LAYERS * T * PAIRS)
        l_o = signal("l_o", LAYERS * T)
        l_wo = signal("l_wo", LAYERS * T)
        l_res = signal("l_res", LAYERS * T)
        l_shps = signal("l_shps", LAYERS * 2)
        f_up = signal("f_up", LAYERS * 6)
        f_act = signal("f_act", LAYERS * 6)
        f_hid = signal("f_hid", LAYERS * 6)
        f_down = signal("f_down", LAYERS * 6)
        s_final = signal("s_final")
        s_out = signal("s_out", 16, start=16)

        x_rows = x.rearrange("b (t p) d -> b p t d", p=P)
        h_dram = nc.dram_tensor("h_dram", (B, P, 3, N), F32, kind="Internal").ap()
        out_rows = out.rearrange("b (t p) d -> b p t d", p=P)

        FIRST_LOADS = [(w0[:], wl0), (mats[:], c_mat), (small[:], c_small)]
        LOADS = [(gb_sb[:], gb), (bp_sb[:], bp), (gate_sb[:], gate), (wa_sb[:], ew_a), (wu_sb[:], ew_u),
                 (wd_sb[:], ew_d), (w1_in, wl1[:, 0:3, :]), (w1_sb[:], wl1[:, 3:5, :]), (alpha_sb[:, 0:1], alpha),
                 (wqkv_sb[:], wqkv), (qks_sb[:], qks), (wo_sb[:], wo), (lngb_sb[:], lngb), (fw1_sb[:], fw1),
                 (fb1_sb[:], fb1), (fw2_sb[:], fw2), (fb2_sb[:], fb2), (sel_f, c_sel), (band_f, c_band),
                 (rot_in, c_rot)]
        FIRST_LOADED = 16 * len(FIRST_LOADS)
        LOADED = 16 * len(LOADS)

        block = ctx.enter_context(nc.Block())

        STEPS = 2 * G
        MAXIMA = 16 * STEPS
        AHEAD = 44
        PROJECT_EARLY = {4: 3, 8: 4, 12: 5}
        PROJECT_IN = {1: 6, 4: 7, 7: 8, 17: 9, 20: 10, 24: 11}

        def maxima_in(k):
            return range(min(AHEAD + 2 * k, MAXIMA), min(AHEAD + 2 * k + 2, MAXIMA))

        def maxima_done(k):
            return min(AHEAD + 2 * k + 2, MAXIMA) // 32

        def proj_bank(i):
            return i % 3 if i < 6 else 7

        ALL_PAIRS, LAG = T * PAIRS, 3
        SLOTS = ALL_PAIRS + LAG + 1

        HALF_SHIFT, HALF_STATS, HALF_FF = 13, 14, 16
        H2 = N // 2
        sum_bank, up_bank = (0, 7), (1, 5)

        def qkv_bank(t, c):
            return (5, 6, 2)[c] if t == 1 else c

        def turn_no(l, what, h):
            return 3 + 4 * l + 2 * what + h

        def tiles_before(k):
            return T * (k - 1) if k <= 2 else 2 * T + 2 * (k - 3)

        def chunk_no(l, h, c):
            return 6 * l + 3 * h + c

        def of_first(sig, k):
            return sig.at(0, k)

        def of_next(b):
            return lambda sig, k: sig.at(b, sig.per + k)

        @block.sync
        def _(sp):
            def load_x(b, loaded):
                sp.dma_start(x_in[:, :, :], x_rows[bass.ds(b, 1), :, :, :].rearrange("o p t d -> (o p) t d"))\
                    .then_inc(loaded.sem, 16)

            def load_h(b):
                sp.dma_start(sig[:, :, :], h_dram[bass.ds(b, 1), :, :, :].rearrange("o p i n -> (o p) i n"))\
                    .then_inc(s_h.sem, 16)

            def store_h(b):
                sp.wait_ge(p_kept.sem, p_kept.at(b, 3))
                sp.dma_start(h_dram[bass.ds(b, 1), :, :, :].rearrange("o p i n -> (o p) i n"), sig[:, :, :])\
                    .then_inc(p_store.sem, 16)

            def place_q(b, g):
                sp.wait_ge(s_part.sem, s_part.at(b, 3 * g + 1))
                for j in range(4):
                    r = slice(32 * j, 32 * j + 32)
                    sp.dma_start(qz[r, 4 * g + j, :].bitcast(F32), rnd[r, 3 * g % 2, :].bitcast(F32))\
                        .then_inc(s_qput.sem, 16)

            def place_shifts(b, g):
                sp.wait_ge(s_mT.sem, s_mT.at(b, g + 1))
                for j in range(4):
                    sp.dma_start(qz[32 * j + 24:32 * j + 26, 4 * g + j, :].bitcast(F32),
                                 mxT[2 * j:2 * j + 2, g % 2, :].bitcast(F32)).then_inc(s_shift.sem, 16)

            def place(b):
                place_q(b, 0)
                for g in range(G):
                    if g + 1 < G:
                        place_q(b, g + 1)
                    place_shifts(b, g)

            def store_out(b):
                sp.wait_ge(s_final.sem, s_final.at(b, 1))
                sp.dma_start(out_rows[bass.ds(b, 1), :, :, :].rearrange("o p t d -> (o p) t d"), xc[:, :, :])\
                    .then_inc(s_out.sem, 16)

            load_x(0, p_x)
            for dst, src in FIRST_LOADS:
                sp.dma_start(dst, src).then_inc(s_w0.sem, 16)
            with sp.Fori(0, B - 1) as b:
                sp.wait_ge(p_used.sem, p_used.at(b, 1))
                load_x(b + 1, p_x)
                store_h(b)
            store_h(B - 1)
            sp.wait_ge(p_used.sem, p_used.at(B, 0))
            load_x(0, s_x)
            sp.wait_ge(p_store.sem, p_store.at(B, 0))
            sp.wait_ge(p_stat.sem, p_stat.at(B, 0))
            load_h(0)
            def sequence(b, following):
                place(b)
                sp.wait_ge(s_xused.sem, s_xused.at(b, 1))
                load_x(following, s_x)
                sp.wait_ge(l_s.sem, l_s.at(b, l_s.per))
                load_h(following)
                store_out(b)

            with sp.Fori(0, B - 1) as b:
                sequence(b, b + 1)
            sequence(B - 1, B - 1)
            sp.wait_ge(s_out.sem, s_out.at(B, 0))

        @block.gpsimd
        def _(pool):
            pool.wait_ge(s_w0.sem, FIRST_LOADED)
            with pool.Fori(0, B) as b:
                pool.wait_ge(p_var.sem, p_var.at(b, 1))
                pool.tensor_tensor(ln_rs[:, :], ln_ve[:, :], half_neg[:, 0:T], ALU.pow).then_inc(p_rstd.sem, 1)
            pool.wait_ge(n_var.sem, 1)
            pool.tensor_tensor(bn[:, 1, :], bn[:, 0, :], half_neg[:, 0:3], ALU.pow).then_inc(n_rstd.sem, 1)
            pool.memset(qz[:, :, :].bitcast(F32), 0.0)
            pool.memset(l_p[:, :, :], 0.0)
            pool.drain()
            pool.memset(hT[64:P, 0:1], 0.0)
            pool.drain().then_inc(s_zero.sem, 1)

            def attention_rstd(at):
                for k in range(1, 3):
                    pool.wait_ge(a_var.sem, at(a_var, k))
                    pool.tensor_tensor(ln_rs[:, :], ln_ve[:, :], half_neg[:, 0:T], ALU.pow).then_inc(a_rstd.sem, 1)

            attention_rstd(of_first)
            with pool.Fori(0, B) as b:
                def rstd(k, m=T):
                    pool.wait_ge(s_var.sem, s_var.at(b, k))
                    pool.tensor_tensor(ln_rs[:, 0:m], ln_ve[:, 0:m], half_neg[:, 0:m], ALU.pow).then_inc(s_rstd.sem, 1)

                pool.tensor_tensor(v_aug[:, :, :, :].rearrange("p t h c -> p (t h) c"),
                                   one_at_hd.unsqueeze(1).to_broadcast([P, T * HEADS, 32]),
                                   zero.unsqueeze(2).to_broadcast([P, T * HEADS, 32]), ALU.add).then_inc(s_vone.sem, 1)
                rstd(1)
                rstd(2)
                pool.wait_ge(s_pv.sem, s_pv.at(b, 4 * G))
                zero_b = zero.to_broadcast([P, LH * N])
                pool.tensor_tensor(q_bd[:, :, :].rearrange("p h n -> p (h n)"), zero_b, zero_b, ALU.add)\
                    .then_inc(s_qzero.sem, 1)
                rstd(3)
                rstd(4)
                for l in range(LAYERS):
                    def inverse_norms(t, c):
                        pool.wait_ge(l_ss.sem, l_ss.at(b, l * T + t + 1))
                        pool.tensor_tensor(rn[:, t, c, :], ssq[:, c, :], half_neg[:, 0:LH], ALU.pow)\
                            .then_inc((l_rnq, l_rnk)[c].sem, 1)

                    def q_rows(t):
                        pool.wait_ge(l_qprod.sem, l_qprod.at(b, l * T + t + 1))
                        pool.tensor_tensor(qk_rows[:, 0, :], rq[:, 0, :], rq[:, 1, :], ALU.add).then_inc(l_qrow.sem, 1)

                    def norm_probs(n):
                        t, a = divmod(n, PAIRS)
                        lo = P if t == 0 else BACK
                        r = slice(2 * a, 2 * a + 2)
                        pool.wait_ge(l_r.sem, l_r.at(b, l * ALL_PAIRS + n + 1))
                        pool.tensor_tensor(l_p[:, r, lo:2 * P], l_p[:, r, lo:2 * P],
                                           l_rec[:, r].unsqueeze(2).to_broadcast([P, 2, 2 * P - lo]), ALU.mult)\
                            .then_inc(l_pn.sem, 1)

                    inverse_norms(0, 1)
                    q_rows(0)
                    inverse_norms(0, 0)
                    inverse_norms(1, 1)
                    inverse_norms(1, 0)
                    for n in range(ALL_PAIRS):
                        t, a = divmod(n, PAIRS)
                        if a == 3 and t + 2 < T:
                            inverse_norms(t + 2, 1)
                        norm_probs(n)
                        if a == 3 and t + 2 < T:
                            inverse_norms(t + 2, 0)
                        if a == 0 and t + 1 < T:
                            q_rows(t + 1)
                        if n == HALF_STATS - 1:
                            rstd(5 + 2 * l, 2)
                    rstd(6 + 2 * l, 2)
                attention_rstd(of_next(b))
                rstd(NORMS)
                pool.wait_ge(l_s.sem, l_s.at(b, l_s.per))

        @block.scalar
        def _(act):
            def copy_turned(value):
                act.wait_ge(p_turned.sem, value)
                act.copy(xT[:, :], ps[:, 0, :]).then_inc(p_cols.sem, 1)

            def keep_h(b):
                for i in range(3):
                    act.wait_ge(p_h.sem, p_h.at(b, i + 1))
                    act.copy(sig[:, i, :], ps[:, 1 + i, :]).then_inc(p_kept.sem, 1)

            copy_turned(1)
            act.wait_ge(p_x.sem, 32)
            for dst, src in LOADS:
                act.dma_start(dst, src).then_inc(s_w.sem, 16)
            with act.Fori(0, B - 1) as b:
                keep_h(b)
                copy_turned(p_turned.at(b, 2))
                act.wait_ge(p_store.sem, p_store.at(b, 16))
                act.wait_ge(p_stat.sem, p_stat.at(b, 3))
            keep_h(B - 1)
            act.wait_ge(n_aff.sem, 1)

            def attention_sigmoids(at):
                act.wait_ge(s_h.sem, at(s_h, 16))
                for i in range(3):
                    act.activation(sig[:, i, :], sig[:, i, :], ACT.Sigmoid,
                                   bias=bn[:, 3, i:i + 1], scale=bn[:, 2, i:i + 1]).then_inc(s_sig.sem, 1)

            def attention_values(at):
                act.wait_ge(a_turned.sem, at(a_turned, 1))
                act.copy(v_rows.rearrange("p t d -> p (t d)"), ps[:, 3, :]).then_inc(a_cols.sem, 1)

            def attention_weights(at):
                act.wait_ge(s_vvwps.sem, at(s_vvwps, 1))
                act.copy(vvw[:, :], ps[:, 4, P:2 * P]).then_inc(s_vvw.sem, 1)

            attention_sigmoids(of_first)
            attention_values(of_first)
            attention_weights(of_first)
            act.wait_ge(s_zero.sem, 1)
            with act.Fori(0, B) as b:
                def columns(k, dst):
                    act.wait_ge(s_turned.sem, s_turned.at(b, k))
                    act.copy(dst, ps[:, 0, :]).then_inc(s_cols.sem, 1)

                act.wait_ge(a_turned.sem, a_turned.at(b, 2))
                act.copy(xT[:, :], ps[:, 0, :]).then_inc(a_cols.sem, 1)
                act.wait_ge(s_top.sem, s_top.at(b, 1))
                act.activation(top_w[:, 0, :], top_d[:, :], ACT.Sigmoid, scale=-1.0)
                act.activation(top_w[:, 1, :], top_d[:, :], ACT.Sigmoid).then_inc(s_topw.sem, 1)
                for n in range(UNITS):
                    if n == 2:
                        act.wait_ge(s_dispps.sem, s_dispps.at(b, 1))
                        act.copy(disp_T[:, :], ps[0:3 * EXPERTS, 5, :]).then_inc(s_dispT.sem, 1)
                    act.wait_ge(s_up.sem, s_up.at(b, n + 1))
                    if n >= 2:
                        act.wait_ge(s_hid.sem, s_hid.at(b, n - 1))
                    act.activation(act_h[:, n % 2, :], ps[:, 1 + n % 2, :], ACT.Silu).then_inc(s_silu.sem, 1)

                columns(1, xT[:, :])

                def rounded(i):
                    act.wait_ge(s_proj.sem, s_proj.at(b, i + 1))
                    if i >= 2 and (i - 2) % 3 == 0:
                        act.wait_ge(s_qput.sem, s_qput.at(b, 64 * ((i - 2) // 3 + 1)))
                    elif i >= 2:
                        act.wait_ge(s_part.sem, s_part.at(b, i - 1))
                    act.activation(rnd[:, i % 2, :], ps[:, proj_bank(i), :], ACT.Identity,
                                   bias=(0.0, k_one, kp_one)[i % 3]).then_inc(s_rnd.sem, 1)

                def shifts(g):
                    act.wait_ge(s_mps.sem, s_mps.at(b, g + 1))
                    if g >= 2:
                        act.wait_ge(s_shift.sem, s_shift.at(b, 64 * (g - 1)))
                    act.copy(mxT[:, g % 2, :], ps[0:8, 7, :]).then_inc(s_mT.sem, 1)

                for i in range(2):
                    rounded(i)
                act.wait_ge(s_vone.sem, s_vone.at(b, 1))
                act.wait_ge(s_vps.sem, s_vps.at(b, 1))
                act.copy(v_aug[:, :, :, 0:HD], ps[:, 7, :].rearrange("p (t h d) -> p t h d", t=T, d=HD))\
                    .then_inc(s_vaug.sem, 1)
                for i in range(2, 6):
                    rounded(i)
                shifts(0)
                for k in range(8 * STEPS):
                    s, u, j = k // 8, k // 4, k % 4
                    if j == 0 and u >= 2:
                        act.wait_ge(s_pv.sem, s_pv.at(b, u - 1))
                    for i in range(2):
                        m = 2 * k + i
                        act.wait_ge(s_sps.sem, s_sps.at(b, m + 1))
                        act.activation(prob[:, u % 2, j, i, :], ps[:, m % 3, :], ACT.Exp, scale=HD ** -0.5)\
                            .then_inc(s_exp[i].sem, 1)
                    if k >= 1 and maxima_done(k - 1) > maxima_done(k - 2):
                        shifts(maxima_done(k - 1) - 1)
                    if k in PROJECT_IN:
                        rounded(PROJECT_IN[k])
                    if k % 8 == 3 and s >= 1:
                        act.wait_ge(s_pv.sem, s_pv.at(b, u))
                        if s >= 2:
                            act.wait_ge(s_ops.sem, s_ops.at(b, s - 1))
                        act.copy(oT[:, :], ps[:, 6, :]).then_inc(s_oT.sem, 1)
                act.wait_ge(s_pv.sem, s_pv.at(b, 2 * STEPS))
                act.wait_ge(s_ops.sem, s_ops.at(b, STEPS - 1))
                act.copy(oT[:, :], ps[:, 6, :]).then_inc(s_oT.sem, 1)
                columns(2, xT[:, :])

                act.wait_ge(s_qzero.sem, s_qzero.at(b, 1))
                def columns_late(l, h):
                    act.wait_ge(s_turned.sem, s_turned.at(b, turn_no(l, 0, h)))
                    act.copy(hT[0:64, H2 * h:H2 * h + H2], ps[0:64, sum_bank[h], H2:N])
                    w = H2 - h
                    act.copy(hT[64:P, H2 * h + 1:H2 * h + 1 + w], ps[64:P, sum_bank[h], H2:H2 + w])\
                        .then_inc(s_cols.sem, 1)

                def normed_columns(l, h):
                    act.wait_ge(s_turned.sem, s_turned.at(b, turn_no(l, 1, h)))
                    act.activation(xT[:, H2 * h:H2 * h + H2], ps[:, sum_bank[h], 0:H2], ACT.Identity,
                                   bias=lngb_sb[:, l, 1:2], scale=lngb_sb[:, l, 0:1]).then_inc(s_cols.sem, 1)

                def gelu(l, h, c):
                    i, m = chunk_no(l, h, c), FF[c][1]
                    act.wait_ge(f_up.sem, f_up.at(b, i + 1))
                    if i >= 2:
                        act.wait_ge(f_hid.sem, f_hid.at(b, i - 1))
                    act.activation(act_h[0:m, i % 2, 0:H2], ps[0:m, up_bank[h] + c % 2, 0:H2], ACT.Gelu,
                                   bias=fb1_sb[0:m, l, 1, c:c + 1]).then_inc(f_act.sem, 1)

                def squares(l, t):
                    i = l * T + t + 1
                    if t >= 1:
                        act.wait_ge(l_ss.sem, l_ss.at(b, i - 1))
                    for c in range(2):
                        act.wait_ge(l_qkv.sem, l_qkv.at(b, 3 * (i - 1) + c + 1))
                        last = act.activation(sq[:, c, :], ps[:, qkv_bank(t, c), :], ACT.Square)
                    last.then_inc(l_sq.sem, 1)
                    act.wait_ge(l_qkv.sem, l_qkv.at(b, 3 * i))
                    act.copy(v_loc[:, t, :], ps[:, 2, :]).then_inc(l_v.sem, 1)

                def turned_q(l, t):
                    act.wait_ge(l_qps.sem, l_qps.at(b, l * T + t + 1))
                    for e in range(2):
                        r = slice(64 * e, 64 * e + 64)
                        last = act.copy(q_bd[r, e:LH:2, t * P:(t + 1) * P],
                                        ps[r, 3, :].rearrange("p (a n) -> p a n", a=PAIRS))
                    last.then_inc(l_qT.sem, 1)

                def turned_probs(l, n):
                    k = l * ALL_PAIRS + n + 1
                    act.wait_ge(l_pps.sem, l_pps.at(b, k))
                    if n >= 2:
                        act.wait_ge(l_pv.sem, l_pv.at(b, k - 2))
                    act.copy(l_pT[:, n % 2, :, :, :].rearrange("p e k n -> p (e k n)"), ps[:, 5 + n % 2, :])\
                        .then_inc(l_pT_in.sem, 1)

                def exps(l, n):
                    t, a = divmod(n, PAIRS)
                    k = l * ALL_PAIRS + n + 1
                    lo = P if t == 0 else BACK
                    act.wait_ge(l_max.sem, l_max.at(b, k))
                    if t >= 1:
                        act.wait_ge(l_pps.sem, l_pps.at(b, k - PAIRS))
                    for h in (2 * a, 2 * a + 1):
                        o = (BACK + P) * (h % 2)
                        last = act.activation(l_p[:, h, lo:2 * P], ps[:, 3 + a % 2, o + lo - BACK:o + BACK + P],
                                              ACT.Exp, bias=l_nb[:, h:h + 1], scale=l_sc[:, t % 2, h:h + 1],
                                              accum_out=l_sum[:, h:h + 1])
                    last.then_inc(l_exp.sem, 1)

                columns_late(0, 0)
                squares(0, 0)
                columns_late(0, 1)
                squares(0, 1)
                for l in range(LAYERS):
                    turned_q(l, 0)
                    for n in range(SLOTS):
                        t, a = divmod(n, PAIRS)
                        if 0 <= n - LAG < ALL_PAIRS:
                            turned_probs(l, n - LAG)
                        if n < ALL_PAIRS:
                            exps(l, n)
                        w = n - LAG - 1
                        if w >= 0 and w % PAIRS == PAIRS - 1:
                            act.wait_ge(l_pv.sem, l_pv.at(b, l * ALL_PAIRS + w + 1))
                            act.copy(l_oT[:, :, :].rearrange("p a n -> p (a n)"), ps[:, 7, :]).then_inc(l_o.sem, 1)
                        if a == 3 and t + 1 < T:
                            turned_q(l, t + 1)
                        if a == 3 and t + 2 < T:
                            squares(l, t + 2)
                        if n == HALF_FF:
                            normed_columns(l, 0)
                        if l == LAYERS - 1 and n == HALF_FF + 1:
                            attention_sigmoids(of_next(b))
                        if n > HALF_FF:
                            gelu(l, 0, n - HALF_FF - 1)
                        if l == LAYERS - 1 and n == HALF_FF + 2:
                            attention_values(of_next(b))
                    if l == LAYERS - 1:
                        attention_weights(of_next(b))
                    normed_columns(l, 1)
                    gelu(l, 1, 0)
                    if l + 1 < LAYERS:
                        columns_late(l + 1, 0)
                    gelu(l, 1, 1)
                    gelu(l, 1, 2)
                    if l + 1 < LAYERS:
                        squares(l + 1, 0)
                        columns_late(l + 1, 1)
                        squares(l + 1, 1)

        @block.vector
        def _(dve):
            H = LD // 2

            def moments(src, var):
                for t in range(T):
                    dve.bn_stats(ln_st[:, t, :], src[:, t, :])
                dve.drain()
                for t in range(T):
                    dve.bn_aggr(ln_mv[:, t, :], ln_st[:, t, :])
                dve.drain()
                dve.tensor_scalar(ln_ve[:, :], ln_mv[:, :, 1], EPS, None, ALU.add).then_inc(var.sem, 1)

            def normed(src, dst, rows=None):
                for t in range(T):
                    tile = dve.tensor_scalar(dst[:, t, :], src[:, t, :], ln_mv[:, t, 0:1], ln_rs[:, t:t + 1],
                                             ALU.subtract, ALU.mult)
                    if rows:
                        tile.then_inc(rows.sem, 1)
                dve.drain()

            def residual(src, x_old, shifted, x_new, used, var):
                for t in range(T):
                    last = dve.scalar_tensor_tensor(shifted[:, t, :], src[:, t, :], ln_rs[:, t:t + 1], x_old[:, t, :],
                                                    ALU.mult, ALU.add)
                if used:
                    last.then_inc(used.sem, 1)
                dve.tensor_tensor(ln_nm[:, :], ln_mv[:, :, 0], ln_rs[:, :], ALU.mult)
                dve.drain()
                moments(shifted, var)
                for t in range(T):
                    dve.tensor_scalar(x_new[:, t, :], shifted[:, t, :], ln_nm[:, t:t + 1], None, ALU.subtract)

            def statistics(b, h_stats_b):
                for i in range(3):
                    dve.wait_ge(p_kept.sem, p_kept.at(b, i + 1))
                    dve.bn_stats(h_stats_b(i), sig[:, i, :]).then_inc(p_stat.sem, 1)

            dve.wait_ge(p_x.sem, 16)
            moments(x_in, p_var)
            dve.wait_ge(p_rstd.sem, 1)
            normed(x_in, xn)
            dve.drain().then_inc(p_rows.sem, 1)
            dve.drain().then_inc(p_used.sem, 1)
            with dve.Fori(0, B - 1) as b:
                dve.wait_ge(p_x.sem, p_x.at(b, 32))
                moments(x_in, p_var)
                dve.wait_ge(p_rstd.sem, p_rstd.at(b, 2))
                dve.wait_ge(p_turned.sem, p_turned.at(b, 1))
                normed(x_in, xn)
                dve.drain().then_inc(p_rows.sem, 1)
                dve.drain().then_inc(p_used.sem, 1)
                statistics(b, lambda i: h_stats[:, i, bass.ds(b, 1), :].rearrange("p o s -> p (o s)"))
            statistics(B - 1, lambda i: h_stats[:, i, B - 1, :])
            dve.drain()
            for i in range(3):
                dve.bn_aggr(h_mv[:, i, :], h_stats[:, i, :, :].rearrange("p b s -> p (b s)"))
            dve.drain()
            dve.tensor_scalar(bn[:, 0, :], h_mv[:, :, 1], EPS, None, ALU.add).then_inc(n_var.sem, 1)
            dve.wait_ge(s_w.sem, LOADED)
            dve.wait_ge(n_rstd.sem, 1)
            dve.scalar_tensor_tensor(bn[:, 2, :], bn[:, 1, :], 4.0, gb_sb[:, 0:6:2], ALU.mult, ALU.mult)
            dve.tensor_scalar(bn[:, 4, :], gb_sb[:, 1:6:2], 4.0, -4.0, ALU.mult, ALU.add)
            dve.drain()
            dve.tensor_tensor(bn[:, 0, :], bn[:, 2, :], h_mv[:, :, 0], ALU.mult)
            dve.drain()
            dve.tensor_tensor(bn[:, 3, :], bn[:, 4, :], bn[:, 0, :], ALU.subtract).then_inc(n_aff.sem, 1)

            dve.memset(waug[:, :, :, :, :, :], 0.0)
            dve.tensor_copy(ident_bf[:, :], ident)
            dve.tensor_copy(sel[:, :, :], sel_f[:, :, :])
            dve.tensor_copy(band[:, :, :], band_f[:, :, :])
            dve.tensor_scalar(alpha_sb[:, 1:2], alpha_sb[:, 0:1], -1.0, 1.0, ALU.mult, ALU.add)
            dve.drain()
            for i in range(3):
                for r in range(3):
                    dve.tensor_copy(waug[:, i, :, :, r, :],
                                    w1_in[:, i, :].rearrange("p (g j d) -> p g j d", g=G, d=HD))
            for l in range(LAYERS):
                for i in range(2):
                    sc = qks_sb[:, l, i, :].unsqueeze(1).to_broadcast([P, T, LD])
                    dve.tensor_tensor(rot[:, l, 2 * i, :, :], rot_in[:, 2 * i, :, :], sc, ALU.mult)
                    for a in range(2):
                        dve.tensor_tensor(rot[:, l, 2 * i + 1, :, a * H:(a + 1) * H],
                                          rot_in[:, 2 * i + 1, :, a * H:(a + 1) * H],
                                          qks_sb[:, l, i, (1 - a) * H:(2 - a) * H].unsqueeze(1).to_broadcast([P, T, H]),
                                          ALU.mult)
            dve.drain().then_inc(s_const.sem, 1)
            dve.drain().then_inc(s_out.sem, 16)

            def attention_qk(at):
                dve.wait_ge(s_sig.sem, at(s_sig, 2))
                dve.tensor_tensor(sig[:, 0, :], sig[:, 0, :], sig[:, 1, :], ALU.mult).then_inc(s_qk.sem, 1)

            def attention_heads(at):
                dve.wait_ge(s_vvps.sem, at(s_vvps, 1))
                dve.tensor_tensor(vv[:, :], ps[:, 4, 0:P], blocks, ALU.mult).then_inc(s_vv.sem, 1)

            def attention_output(at):
                dve.wait_ge(s_oput.sem, at(s_oput, 1))
                dve.tensor_tensor(xb[:, :, :], ps[:, 3, :].rearrange("p (t d) -> p t d", t=T),
                                  bp_sb[:, :].unsqueeze(1).to_broadcast([P, T, D]), ALU.add)
                dve.drain()
                moments(xb, a_var)

            def attention_residual(at):
                dve.wait_ge(a_rstd.sem, at(a_rstd, 1))
                dve.wait_ge(s_x.sem, at(s_x, 16))
                residual(xb, x_in, xb, xa, s_xused, a_var)

            def attention_normed(at):
                dve.wait_ge(a_rstd.sem, at(a_rstd, 2))
                normed(xb, xn, a_rows)

            for stage in (attention_qk, attention_heads, attention_output, attention_residual, attention_normed):
                stage(of_first)
            with dve.Fori(0, B) as b:
                def norm(k, src, dst):
                    moments(src, s_var)
                    dve.wait_ge(s_rstd.sem, s_rstd.at(b, k))
                    normed(src, dst)

                def rows_ready(tiles):
                    dve.drain().then_inc(s_rows.sem, tiles)

                def residual_norm(k, src, x_old, x_new, dst):
                    moments(src, s_var)
                    dve.wait_ge(s_rstd.sem, s_rstd.at(b, k))
                    residual(src, x_old, o_rows, x_new, None, s_var)
                    dve.wait_ge(s_rstd.sem, s_rstd.at(b, k + 1))
                    normed(o_rows, dst, s_rows)

                dve.wait_ge(s_logit.sem, s_logit.at(b, 1))
                dve.tensor_copy(logit[:, :, :], ps[:, 6, 0:T * EXPERTS].rearrange("p (t e) -> p t e", t=T))
                dve.drain()
                for t in range(T):
                    dve.max(top_v[:, t, :], logit[:, t, :])
                dve.drain()
                dve.tensor_tensor(top_d[:, :], top_v[:, :, 1], top_v[:, :, 0], ALU.subtract).then_inc(s_top.sem, 1)
                for t in range(T):
                    dve.max_index(top_i[:, t, :], top_v[:, t, :], logit[:, t, :])
                dve.drain()
                dve.tensor_copy(top_if[:, :, :], top_i[:, :, 0:2])
                dve.drain()
                iota_b = iota.unsqueeze(1).to_broadcast([P, T, EXPERTS])
                for i in range(2):
                    dve.tensor_tensor(disp[:, i, :, :], iota_b,
                                      top_if[:, :, i].unsqueeze(2).to_broadcast([P, T, EXPERTS]), ALU.is_equal)
                dve.drain()
                dve.wait_ge(s_topw.sem, s_topw.at(b, 1))
                for i in range(2):
                    dve.tensor_tensor(disp[:, 2 + i, :, :], disp[:, i, :, :],
                                      top_w[:, i, :].unsqueeze(2).to_broadcast([P, T, EXPERTS]), ALU.mult)
                dve.drain()
                dve.tensor_tensor(disp[:, 0, :, :], disp[:, 2, :, :], disp[:, 3, :, :], ALU.add)
                dve.drain()
                E = EXPERTS
                dve.tensor_copy(disp_p[:, :, 0:E], disp[:, 0, :, :])
                dve.drain()
                dve.tensor_tensor(disp[:, 1, :, :], disp[:, 0, :, :], disp_p[:, :, 0:E], ALU.subtract)
                dve.drain()
                dve.tensor_copy(disp_p[:, :, E:2 * E], disp[:, 1, :, :])
                dve.drain()
                dve.tensor_tensor(disp_p[:, :, 2 * E:3 * E], disp[:, 1, :, :], disp_p[:, :, E:2 * E], ALU.subtract)\
                    .then_inc(s_disp.sem, 1)
                for n in range(UNITS):
                    dve.wait_ge(s_silu.sem, s_silu.at(b, n + 1))
                    if n >= 2:
                        dve.wait_ge(s_down.sem, s_down.at(b, n - 1))
                    dve.tensor_tensor(hid[:, n % 2, :], ps[:, 3 + n % 2, :], act_h[:, n % 2, :], ALU.mult)\
                        .then_inc(s_hid.sem, 1)
                dve.wait_ge(s_down.sem, s_down.at(b, UNITS))
                residual_norm(1, ps[:, 7, :].rearrange("p (t d) -> p t d", t=T), xa, xb, xn)

                def parts(i):
                    g, kind = divmod(i, 3)
                    dve.wait_ge(s_rnd.sem, s_rnd.at(b, i + 1))
                    dst = rnd[:, i % 2, :] if kind == 0 else kk[:, kind - 1, g, :]
                    dve.scalar_tensor_tensor(dst, rnd[:, i % 2, :], (q_low, k_low, kp_low)[kind],
                                             ps[:, proj_bank(i), :], ALU.mult, ALU.add).then_inc(s_part.sem, 1)

                def maxima(n):
                    s, j, qt = n // 16, n // T % 4, n % T
                    g, a = divmod(s, 2)
                    if g >= 2 and n % 32 == 0:
                        dve.wait_ge(s_mps.sem, s_mps.at(b, g - 1))
                    dve.wait_ge(s_aps.sem, s_aps.at(b, n + 1))
                    dve.tensor_reduce(mx[:, g % 2, qt, 2 * j + a:2 * j + a + 1], ps[:, 3 + n % 3, :], AX.X, ALU.max,
                                      negate=True).then_inc(s_amax.sem, 1)

                def output(s):
                    g, a = divmod(s, 2)
                    dve.wait_ge(s_ops.sem, s_ops.at(b, s + 1))
                    o = ps[:, 7, :].rearrange("p (t j c) -> p t j c", t=T, j=4)
                    dve.reciprocal(rec[:, :, :], o[:, :, :, HD])
                    dve.drain()
                    dve.tensor_scalar(rec[:, :, :], rec[:, :, :], alpha_sb[:, a:a + 1], None, ALU.mult)
                    dve.drain()
                    dst = att[:, :, 32 * g:32 * g + 32].rearrange("p t (j d) -> p t j d", j=4)
                    rec_b = rec[:, :, :].unsqueeze(3).to_broadcast([P, T, 4, HD])
                    dve.tensor_tensor(dst if a == 0 else o_nrm[:, :, :, :], o[:, :, :, 0:HD], rec_b, ALU.mult)\
                        .then_inc(s_onrm.sem, 1)
                    dve.drain()
                    if a == 1:
                        dve.tensor_tensor(dst, dst, o_nrm[:, :, :, :], ALU.add)
                        dve.drain()

                for i in range(3):
                    parts(i)
                for n in range(AHEAD):
                    maxima(n)
                    if n - 2 in PROJECT_EARLY:
                        parts(PROJECT_EARLY[n - 2])
                for k in range(8 * STEPS):
                    for n in maxima_in(k):
                        maxima(n)
                    if k - 1 in PROJECT_IN:
                        parts(PROJECT_IN[k - 1])
                    if k % 8 == 7 and k >= 8:
                        output(k // 8 - 1)
                output(STEPS - 1)
                rows_ready(T)
                dve.wait_ge(s_lout.sem, s_lout.at(b, 1))
                dve.wait_ge(s_out.sem, s_out.at(b, 0))
                residual_norm(3, ps[:, 1, :].rearrange("p (t d) -> p t d", t=T), xb, xc, y)

                def half_moments(l, h):
                    dve.wait_ge(l_shps.sem, l_shps.at(b, 2 * l + h + 1))
                    for i in range(2):
                        dve.bn_stats(half_st[:, i, 0, :], rows_of[l][:, 2 * h + i, 0:64])
                        dve.bn_stats(half_st[:, i, 1, :], ps[:, up_bank[h], 64 * i:64 * i + 64])
                    dve.drain()
                    for i in range(2):
                        dve.bn_aggr(ln_mv[:, i, :], half_st[:, i, :, :].rearrange("p a s -> p (a s)"))
                    dve.drain()
                    dve.tensor_scalar(ln_ve[:, 0:2], ln_mv[:, 0:2, 1], EPS, None, ALU.add).then_inc(s_var.sem, 1)

                def half_normed(l, h):
                    dve.wait_ge(s_rstd.sem, s_rstd.at(b, 5 + 2 * l + h))
                    for i in range(2):
                        for dst, src in ((xn[:, 2 * h + i, 0:64], rows_of[l][:, 2 * h + i, 0:64]),
                                         (xn[:, 2 * h + i, 64:P], ps[:, up_bank[h], 64 * i:64 * i + 64])):
                            last = dve.tensor_scalar(dst, src, ln_mv[:, i, 0:1], ln_rs[:, i:i + 1],
                                                     ALU.subtract, ALU.mult)
                        last.then_inc(s_rows.sem, 1)
                    dve.drain()

                def hidden(l, h, c):
                    i, m = chunk_no(l, h, c), FF[c][1]
                    dve.wait_ge(f_act.sem, f_act.at(b, i + 1))
                    if i >= 2:
                        dve.wait_ge(f_down.sem, f_down.at(b, i - 1))
                    dve.scalar_tensor_tensor(hid[0:m, i % 2, 0:H2], ps[0:m, up_bank[h] + c % 2, H2:N],
                                             fb1_sb[0:m, l, 0, c:c + 1], act_h[0:m, i % 2, 0:H2],
                                             ALU.add, ALU.mult).then_inc(f_hid.sem, 1)

                def ff_rows(l, h):
                    src, dst = (v[:, 2 * h:2 * h + 2, :] for v in (rows_of[l], rows_of[l + 1]))
                    dve.tensor_tensor(dst, src, fb2_sb[:, l, :].unsqueeze(1).to_broadcast([P, 2, D]), ALU.add)
                    dve.drain()
                    dve.wait_ge(f_down.sem, f_down.at(b, chunk_no(l, h, 2) + 1))
                    dve.tensor_tensor(dst, dst, ps[:, sum_bank[h], 0:H2].rearrange("p (t d) -> p t d", t=2), ALU.add)
                    if l + 1 < LAYERS:
                        rows_ready(2)
                    else:
                        dve.drain()

                def turned_k(l, t):
                    dve.wait_ge(l_kps.sem, l_kps.at(b, l * T + t + 1))
                    dve.tensor_copy(kT[:, :, t * P:(t + 1) * P], ps[:, 4, :].rearrange("p (a n) -> p a n", a=PAIRS))\
                        .then_inc(l_kT.sem, 1)

                def sums(l, t):
                    i = l * T + t + 1
                    dve.wait_ge(l_sq.sem, l_sq.at(b, i))
                    if t >= 1:
                        dve.wait_ge(l_rnq.sem, l_rnq.at(b, i - 1))
                    dve.tensor_reduce(ssq[:, :, :], sq[:, :, :].rearrange("p i (h d) -> p i h d", d=LD), AX.X, ALU.add)
                    dve.drain()
                    dve.tensor_scalar(ssq[:, :, :], ssq[:, :, :], 1e-24, None, ALU.max).then_inc(l_ss.sem, 1)

                def rotated(l, t, c):
                    pa, pb = (rq[:, i, :].rearrange("p (h d) -> p h d", d=LD) for i in range(2)) if c == 0 else (ra, rb)
                    src = ps[:, qkv_bank(t, c), :].rearrange("p (h d) -> p h d", d=LD)
                    cos = rot[:, l, 2 * c, t, :].unsqueeze(1).to_broadcast([P, LH, LD])
                    dve.tensor_tensor(pa, src, cos, ALU.mult)
                    for a in range(2):
                        sin = rot[:, l, 2 * c + 1, t, a * H:(a + 1) * H].unsqueeze(1).to_broadcast([P, LH, H])
                        last = dve.tensor_tensor(pb[:, :, a * H:(a + 1) * H], src[:, :, (1 - a) * H:(2 - a) * H], sin,
                                                 ALU.mult)
                    if c == 0:
                        last.then_inc(l_qprod.sem, 1)
                    else:
                        dve.drain()
                        dve.tensor_tensor(ra[:, :, :], ra[:, :, :], rb[:, :, :], ALU.add).then_inc(l_kread.sem, 1)

                def scaled_k(l, t):
                    i = l * T + t + 1
                    dve.wait_ge(l_rnk.sem, l_rnk.at(b, i))
                    dve.wait_ge(l_kread.sem, l_kread.at(b, i))
                    dve.tensor_tensor(qk_rows[:, 1, :].rearrange("p (h d) -> p h d", d=LD), ra[:, :, :],
                                      rn[:, t, 1, :].unsqueeze(2).to_broadcast([P, LH, LD]), ALU.mult)\
                        .then_inc(l_krow.sem, 1)

                def local_max(l, n):
                    t, a = divmod(n, PAIRS)
                    r = slice(2 * a, 2 * a + 2)
                    if a == 0:
                        dve.wait_ge(l_rnq.sem, l_rnq.at(b, l * T + t + 1))
                        dve.tensor_scalar(l_sc[:, t % 2, :], rn[:, t, 0, :], 8.0, None, ALU.mult)
                    dve.wait_ge(l_s.sem, l_s.at(b, l * ALL_PAIRS + n + 1))
                    s2 = ps[:, 3 + a % 2, 0:2 * (BACK + P)].rearrange("p (e c) -> p e c", e=2)
                    dve.tensor_reduce(l_mx[:, r], s2[:, :, BACK if t == 0 else 0:], AX.X, ALU.max, negate=True)
                    dve.drain()
                    dve.tensor_tensor(l_nb[:, r], l_mx[:, r], l_sc[:, t % 2, r], ALU.mult).then_inc(l_max.sem, 1)

                def reciprocals(l, n):
                    r = slice(2 * (n % PAIRS), 2 * (n % PAIRS) + 2)
                    dve.wait_ge(l_exp.sem, l_exp.at(b, l * ALL_PAIRS + n + 1))
                    dve.reciprocal(l_rec[:, r], l_sum[:, r]).then_inc(l_r.sem, 1)

                sums(0, 0)
                for l in range(LAYERS):
                    rotated(l, 0, 0)
                    rotated(l, 0, 1)
                    scaled_k(l, 0)
                    turned_k(l, 0)
                    for n in range(SLOTS):
                        t, a = divmod(n, PAIRS)
                        if a == 0 and t + 1 < T:
                            sums(l, t + 1)
                        if n < ALL_PAIRS:
                            local_max(l, n)
                        if 1 <= n <= ALL_PAIRS:
                            reciprocals(l, n - 1)
                        if t + 1 < T:
                            if a in (1, 2):
                                rotated(l, t + 1, a - 1)
                            elif a == 3:
                                scaled_k(l, t + 1)
                                turned_k(l, t + 1)
                        w = n - LAG - 1
                        if w >= 0 and w % PAIRS == PAIRS - 1:
                            u = w // PAIRS
                            dve.wait_ge(l_wo.sem, l_wo.at(b, l * T + u + 1))
                            dve.tensor_tensor(rows_of[l][:, u, :], rows_of[l][:, u, :], ps[:, 7, 0:D], ALU.add)\
                                .then_inc(l_res.sem, 1)
                        if n == HALF_STATS:
                            half_moments(l, 0)
                        if n == HALF_STATS + 1:
                            half_normed(l, 0)
                        if HALF_FF < n < SLOTS - 1:
                            hidden(l, 0, n - HALF_FF - 1)
                        if l == LAYERS - 1 and n == HALF_FF + 2:
                            attention_qk(of_next(b))
                    if l == LAYERS - 1:
                        attention_heads(of_next(b))
                    dve.drain()
                    half_moments(l, 1)
                    hidden(l, 0, 2)
                    half_normed(l, 1)
                    ff_rows(l, 0)
                    if l == LAYERS - 1:
                        attention_output(of_next(b))
                    hidden(l, 1, 0)
                    hidden(l, 1, 1)
                    if l == LAYERS - 1:
                        attention_residual(of_next(b))
                    hidden(l, 1, 2)
                    if l == LAYERS - 1:
                        attention_normed(of_next(b))
                    if l + 1 < LAYERS:
                        sums(l + 1, 0)
                    ff_rows(l, 1)
                norm(NORMS, y, o_rows)
                dve.tensor_tensor(xc[:, :, :], xc[:, :, :], o_rows[:, :, :], ALU.add)
                dve.drain().then_inc(s_final.sem, 1)

        @block.tensor
        def _(pe):
            def turn(src, dst, rows=None, count=0):
                for t in range(T):
                    if rows:
                        pe.wait_ge(rows.sem, count + (t + 1))
                    last = pe.transpose(dst[:, t * P:(t + 1) * P], src[:, t, :], ident)
                return last

            pe.wait_ge(s_w0.sem, FIRST_LOADED)

            def turn_x(value):
                pe.wait_ge(p_rows.sem, value)
                turn(xn, ps[:, 0, :]).then_inc(p_turned.sem, 1)

            def branches(b):
                pe.wait_ge(p_cols.sem, p_cols.at(b, 1))
                for i in range(3):
                    pe.matmul(ps[:, 1 + i, :], w0[:, i, :], xT[:, :], start=True, stop=True).then_inc(p_h.sem, 1)

            turn_x(1)
            with pe.Fori(0, B - 1) as b:
                branches(b)
                turn_x(p_rows.at(b, 2))
                pe.wait_ge(p_kept.sem, p_kept.at(b, 3))
            branches(B - 1)

            def attention_turn(at):
                pe.wait_ge(s_sig.sem, at(s_sig, 3))
                for t in range(T):
                    last = pe.transpose(ps[:, 3, t * P:(t + 1) * P], sig[:, 2, t * P:(t + 1) * P], ident)
                last.then_inc(a_turned.sem, 1)

            def attention_vv(at):
                pe.wait_ge(a_cols.sem, at(a_cols, 1))
                for t in range(T):
                    last = pe.matmul(ps[:, 4, 0:P], v_rows[:, t, :], v_rows[:, t, :], start=(t == 0), stop=(t == T - 1))
                last.then_inc(s_vvps.sem, 1)

            def attention_vvw(at):
                pe.wait_ge(s_vv.sem, at(s_vv, 1))
                pe.matmul(ps[:, 4, P:2 * P], vv[:, :], w0[:, 3, :], start=True, stop=True).then_inc(s_vvwps.sem, 1)

            def attention_o(at):
                pe.wait_ge(s_vvw.sem, at(s_vvw, 1))
                pe.wait_ge(s_qk.sem, at(s_qk, 1))
                for t in range(T):
                    last = pe.matmul(ps[:, 3, t * P:(t + 1) * P], sig[:, 0, t * P:(t + 1) * P], vvw[:, :],
                                     start=True, stop=True)
                last.then_inc(s_oput.sem, 1)

            for stage in (attention_turn, attention_vv, attention_vvw, attention_o):
                stage(of_first)
            pe.wait_ge(s_const.sem, 1)
            pe.wait_ge(s_zero.sem, 1)
            with pe.Fori(0, B) as b:
                def turn_rows(k, src):
                    turn(src, ps[:, 0, :], s_rows, s_rows.at(b, tiles_before(k))).then_inc(s_turned.sem, 1)

                turn(xn, ps[:, 0, :], a_rows, a_rows.at(b, 0)).then_inc(a_turned.sem, 1)
                pe.wait_ge(a_cols.sem, a_cols.at(b, 2))
                for t in range(T):
                    last = pe.matmul(ps[:, 6, t * EXPERTS:(t + 1) * EXPERTS], xT[:, t * P:(t + 1) * P], gate_sb[:, :],
                                     start=True, stop=True)
                last.then_inc(s_logit.sem, 1)

                def down(n):
                    pe.wait_ge(s_hid.sem, s_hid.at(b, n + 1))
                    for t in range(T):
                        last = pe.matmul(ps[:, 7, t * P:(t + 1) * P], hid[:, n % 2, t * P:(t + 1) * P], wd_sb[:, n, :],
                                         start=(n == 0 and t == 0), stop=(n == UNITS - 1), skip_group_check=True)
                    last.then_inc(s_down.sem, 1)

                for n in range(UNITS):
                    if n == 2:
                        pe.wait_ge(s_disp.sem, s_disp.at(b, 1))
                        for t in range(T):
                            last = pe.matmul(ps[0:3 * EXPERTS, 5, t * P:(t + 1) * P], disp_p[:, t, :], ident_bf[:, :],
                                             start=True, stop=True)
                        last.then_inc(s_dispps.sem, 1)
                    if n >= 2:
                        pe.wait_ge(s_hid.sem, s_hid.at(b, n - 1))
                    pe.matmul(ps[:, 1 + n % 2, :], wa_sb[:, n, :], xT[:, :], start=True, stop=True)
                    if n < 2:
                        last = pe.matmul(ps[:, 3 + n % 2, :], wu_sb[:, n, :], xT[:, :], start=True, stop=True)
                    else:
                        if n == 2:
                            pe.wait_ge(s_dispT.sem, s_dispT.at(b, 1))
                        last = pe.matmul(ps[:, 3 + n % 2, :], sel[:, n - 2, :], disp_T[:, :], start=True, stop=True)
                    last.then_inc(s_up.sem, 1)
                    if n >= 1:
                        down(n - 1)
                down(UNITS - 1)

                turn_rows(1, xn)
                pe.wait_ge(s_cols.sem, s_cols.at(b, 1))

                def project_heads(i):
                    g, kind = divmod(i, 3)
                    pe.matmul(ps[:, proj_bank(i), :], waug[:, kind, g, :, :, :].rearrange("p j r d -> p (j r d)"),
                              xT[:, :], start=True, stop=True).then_inc(s_proj.sem, 1)

                def scores_for_maxima(n):
                    s, j, qt = n // 16, n // T % 4, n % T
                    g, a = divmod(s, 2)
                    if n % 32 == 0:
                        pe.wait_ge(s_qput.sem, s_qput.at(b, 64 * (g + 1)))
                    if n % 16 == 0:
                        pe.wait_ge(s_part.sem, s_part.at(b, 3 * g + 2 + a))
                    if n >= 3:
                        pe.wait_ge(s_amax.sem, s_amax.at(b, n - 2))
                    pe.matmul(ps[:, 3 + n % 3, :], qz[:, 4 * g + j, qt * P:(qt + 1) * P], kk[:, a, g, :],
                              start=True, stop=True).then_inc(s_aps.sem, 1)

                def turn_maxima(g):
                    pe.wait_ge(s_amax.sem, s_amax.at(b, 32 * (g + 1)))
                    for qt in range(T):
                        last = pe.transpose(ps[0:8, 7, qt * P:(qt + 1) * P], mx[:, g % 2, qt, :], ident)
                    last.then_inc(s_mps.sem, 1)

                def weigh(u, k):
                    s, half = divmod(u, 2)
                    kt = 2 * half + k
                    if k == 0:
                        pe.wait_ge(s_exp[1].sem, s_exp[1].at(b, 4 * u + 4))
                        if half == 0 and s >= 1:
                            pe.wait_ge(s_oT.sem, s_oT.at(b, s))
                    for j in range(4):
                        last = pe.matmul(ps[32 * j:32 * j + 32, 6, :], v_aug[:, kt, 4 * (s // 2) + j, :],
                                         prob[:, u % 2, j, k, :], start=(kt == 0), stop=(kt == T - 1))
                    if k == 1:
                        last.then_inc(s_pv.sem, 1)

                def turn_output(s):
                    pe.wait_ge(s_oT.sem, s_oT.at(b, s + 1))
                    for t in range(T):
                        last = pe.transpose(ps[:, 7, t * P:(t + 1) * P], oT[:, t * P:(t + 1) * P], ident)
                    last.then_inc(s_ops.sem, 1)

                for i in range(3):
                    project_heads(i)
                for t in range(T):
                    last = pe.matmul(ps[:, 7, t * P:(t + 1) * P], xT[:, t * P:(t + 1) * P], w1_sb[:, 0, :],
                                     start=True, stop=True)
                last.then_inc(s_vps.sem, 1)
                for n in range(AHEAD):
                    scores_for_maxima(n)
                    if n in PROJECT_EARLY:
                        i = PROJECT_EARLY[n]
                        pe.wait_ge(s_part.sem, s_part.at(b, i - 2))
                        project_heads(i)
                    if n == 34:
                        pe.wait_ge(s_vaug.sem, s_vaug.at(b, 1))
                        turn_maxima(0)
                free = (s_mT, 1)
                for k in range(8 * STEPS):
                    s, u, j = k // 8, k // 4, k % 4
                    g, a = divmod(s, 2)
                    if k == 0:
                        pe.wait_ge(s_part.sem, s_part.at(b, 6))
                    if k % 16 == 0:
                        pe.wait_ge(s_shift.sem, s_shift.at(b, 64 * (g + 1)))
                    ahead = maxima_in(k)
                    for i in range(2):
                        if i < len(ahead):
                            scores_for_maxima(ahead[i])
                        m, kt = 2 * k + i, 2 * (u % 2) + i
                        if m >= 3:
                            before = s_exp[(m - 3) % 2]
                            pe.wait_ge(before.sem, before.at(b, (m - 3) // 2 + 1))
                        pe.matmul(ps[:, m % 3, :], kk[:, a, g, kt * P:(kt + 1) * P], qz[:, 4 * g + j, :],
                                  start=True, stop=True).then_inc(s_sps.sem, 1)
                    if k >= 1 and maxima_done(k - 1) > maxima_done(k - 2):
                        m = maxima_done(k - 1) - 1
                        pe.wait_ge(free[0].sem, free[0].at(b, free[1]))
                        turn_maxima(m)
                        free = (s_mT, m + 1)
                    if k in PROJECT_IN:
                        pe.wait_ge(free[0].sem, free[0].at(b, free[1]))
                        project_heads(PROJECT_IN[k])
                        free = (s_part, PROJECT_IN[k] + 1)
                    if j % 2 and u >= 1:
                        weigh(u - 1, j // 2)
                    if k % 8 == 6 and s >= 1:
                        pe.wait_ge(free[0].sem, free[0].at(b, free[1]))
                        turn_output(s - 1)
                        free = (s_onrm, s)
                weigh(2 * STEPS - 1, 0)
                weigh(2 * STEPS - 1, 1)
                pe.wait_ge(free[0].sem, free[0].at(b, free[1]))
                turn_output(STEPS - 1)
                turn_rows(2, att)
                pe.wait_ge(s_cols.sem, s_cols.at(b, 2))
                for t in range(T):
                    last = pe.matmul(ps[:, 1, t * P:(t + 1) * P], xT[:, t * P:(t + 1) * P], w1_sb[:, 1, :],
                                     start=True, stop=True)
                last.then_inc(s_lout.sem, 1)

                def turn_half(l, what, h):
                    k = turn_no(l, what, h)
                    src = (rows_of[l], xn)[what]
                    for i in range(2):
                        pe.wait_ge(s_rows.sem, s_rows.at(b, tiles_before(k) + i + 1))
                        o = H2 * (1 - what) + P * i
                        last = pe.transpose(ps[:, sum_bank[h], o:o + P], src[:, 2 * h + i, :], ident)
                    last.then_inc(s_turned.sem, 1)

                def project(l, t):
                    i = l * T + t + 1
                    if t >= 2:
                        pe.wait_ge(l_qprod.sem, l_qprod.at(b, i - 1))
                        pe.wait_ge(l_kread.sem, l_kread.at(b, i - 1))
                    for c in range(3):
                        if t >= 1 and c == 2:
                            pe.wait_ge(l_v.sem, l_v.at(b, i - 1))
                        pe.matmul(ps[:, qkv_bank(t, c), :], hT[:, t * P:(t + 1) * P], wqkv_sb[:, l, c, :],
                                  start=True, stop=True).then_inc(l_qkv.sem, 1)

                def turn_q_or_k(l, t, c):
                    i = l * T + t + 1
                    rows, turned = ((l_qrow, l_qps), (l_krow, l_kps))[c]
                    pe.wait_ge(rows.sem, rows.at(b, i))
                    if t >= 1:
                        pe.wait_ge(l_exp.sem, l_exp.at(b, (i - 1) * PAIRS - 1 + c))
                    for a in range(PAIRS):
                        last = pe.transpose(ps[:, 3 + c, a * P:(a + 1) * P], qk_rows[:, c, a * P:(a + 1) * P], ident)
                    last.then_inc(turned.sem, 1)

                def local_scores(l, n):
                    t, a = divmod(n, PAIRS)
                    if a == 0:
                        pe.wait_ge(l_qT.sem, l_qT.at(b, l * T + t + 1))
                        pe.wait_ge(l_kT.sem, l_kT.at(b, l * T + t + 1))
                    if a >= 2:
                        pe.wait_ge(l_exp.sem, l_exp.at(b, l * ALL_PAIRS + n - 1))
                    lo = BACK if t == 0 else 0
                    bank = 3 + a % 2
                    for e in range(2):
                        o = (BACK + P) * e
                        pe.matmul(ps[:, bank, o + lo:o + BACK + P], q_bd[:, 2 * a + e, t * P:(t + 1) * P],
                                  kT[:, a, t * P - BACK + lo:(t + 1) * P], start=(e == 0), stop=False,
                                  skip_group_check=True)
                    both = ps[:, bank, 0:2 * (BACK + P)].rearrange("p (e c) -> p e c", e=2)
                    pe.matmul(both[:, :, lo:], ident_bf[:, :], band[:, :, lo:], start=False, stop=True,
                              skip_group_check=True).then_inc(l_s.sem, 1)

                def turn_probs(l, n):
                    t, a = divmod(n, PAIRS)
                    k = l * ALL_PAIRS + n + 1
                    pe.wait_ge(l_pn.sem, l_pn.at(b, k))
                    if n >= 2:
                        pe.wait_ge(l_pT_in.sem, l_pT_in.at(b, k - 2))
                    else:
                        read = (l_qprod, l_kread)[n]
                        pe.wait_ge(read.sem, read.at(b, l * T + 2))
                    for e in range(2):
                        for k in range(0 if t else 1, 2):
                            o = (2 * e + k) * P
                            last = pe.transpose(ps[:, 5 + a % 2, o:o + P], l_p[:, 2 * a + e, k * P:(k + 1) * P], ident)
                    last.then_inc(l_pps.sem, 1)

                def local_weigh(l, n):
                    t, a = divmod(n, PAIRS)
                    pe.wait_ge(l_pT_in.sem, l_pT_in.at(b, l * ALL_PAIRS + n + 1))
                    if a == 0 and t >= 1:
                        pe.wait_ge(l_res.sem, l_res.at(b, l * T + t))
                    for e in range(2):
                        h = 2 * a + e
                        for k in range(0 if t else 1, 2):
                            last = pe.matmul(ps[64 * e:64 * e + 64, 7, a * P:(a + 1) * P],
                                             v_loc[:, t - 1 + k, h * LD:(h + 1) * LD], l_pT[:, a % 2, e, k, :],
                                             start=(a == 0 and k == (0 if t else 1)), stop=(k == 1),
                                             skip_group_check=True)
                    last.then_inc(l_pv.sem, 1)

                def output_rows(l, t):
                    pe.wait_ge(l_o.sem, l_o.at(b, l * T + t + 1))
                    for a in range(PAIRS):
                        last = pe.matmul(ps[:, 7, 0:D], l_oT[:, a, :], wo_sb[:, l, a, :],
                                         start=(a == 0), stop=(a == PAIRS - 1))
                    last.then_inc(l_wo.sem, 1)

                def shift_upper(l, h):
                    pe.wait_ge(l_res.sem, l_res.at(b, l * T + 2 * h + 2))
                    up, v = up_bank[h], rows_of[l]
                    pe.matmul(ps[:, up, 0:P].rearrange("p (t d) -> p t d", t=2), shift, v[:, 2 * h:2 * h + 2, 64:P],
                              start=True, stop=False)
                    if h == 0:
                        last = pe.matmul(ps[:, up, 64:P], carry, v[:, 0, 64:P], start=False, stop=True)
                    else:
                        last = pe.matmul(ps[:, up, 0:P].rearrange("p (t d) -> p t d", t=2), carry, v[:, 1:3, 64:P],
                                         start=False, stop=True)
                    last.then_inc(l_shps.sem, 1)

                def ff_up(l, h, c):
                    o, m = FF[c]
                    if c == 0:
                        pe.wait_ge(s_cols.sem, s_cols.at(b, turn_no(l, 1, h)))
                    if c >= 2:
                        pe.wait_ge(f_hid.sem, f_hid.at(b, chunk_no(l, h, c) - 1))
                    for a in range(2):
                        w = (1 - a) * HID_F + o
                        last = pe.matmul(ps[0:m, up_bank[h] + c % 2, H2 * a:H2 * a + H2], fw1_sb[:, l, w:w + m],
                                         xT[:, H2 * h:H2 * h + H2], start=True, stop=True)
                    last.then_inc(f_up.sem, 1)

                def ff_down(l, h, c):
                    i, m = chunk_no(l, h, c), FF[c][1]
                    pe.wait_ge(f_hid.sem, f_hid.at(b, i + 1))
                    for t in range(2):
                        last = pe.matmul(ps[:, sum_bank[h], t * P:(t + 1) * P], hid[0:m, i % 2, t * P:(t + 1) * P],
                                         fw2_sb[0:m, l, c, :], start=(c == 0 and t == 0), stop=(c == 2),
                                         skip_group_check=True)
                    last.then_inc(f_down.sem, 1)

                turn_half(0, 0, 0)
                pe.wait_ge(s_cols.sem, s_cols.at(b, turn_no(0, 0, 0)))
                project(0, 0)
                project(0, 1)
                turn_half(0, 0, 1)
                pe.wait_ge(s_cols.sem, s_cols.at(b, turn_no(0, 0, 1)))
                for l in range(LAYERS):
                    turn_q_or_k(l, 0, 0)
                    turn_q_or_k(l, 0, 1)
                    for n in range(SLOTS):
                        t, a = divmod(n, PAIRS)
                        if n < ALL_PAIRS and a == 0:
                            local_scores(l, n)
                        if 0 <= n - LAG < ALL_PAIRS:
                            turn_probs(l, n - LAG)
                        if n < ALL_PAIRS and a > 0:
                            local_scores(l, n)
                        w = n - LAG - 1
                        if w >= 0:
                            local_weigh(l, w)
                        if a == 3 and t + 1 < T:
                            turn_q_or_k(l, t + 1, 0)
                            if t + 2 < T:
                                project(l, t + 2)
                            turn_q_or_k(l, t + 1, 1)
                        if w >= 0 and w % PAIRS == PAIRS - 1:
                            output_rows(l, w // PAIRS)
                        if n == HALF_SHIFT:
                            shift_upper(l, 0)
                        if n == HALF_FF:
                            turn_half(l, 1, 0)
                        if n == HALF_FF + 1:
                            ff_up(l, 0, 0)
                        if l == LAYERS - 1 and n == HALF_FF + 1:
                            attention_turn(of_next(b))
                        if n == HALF_FF + 2:
                            ff_up(l, 0, 1)
                    if l == LAYERS - 1:
                        attention_vv(of_next(b))
                    ff_down(l, 0, 0)
                    shift_upper(l, 1)
                    ff_up(l, 0, 2)
                    if l == LAYERS - 1:
                        attention_vvw(of_next(b))
                    ff_down(l, 0, 1)
                    ff_down(l, 0, 2)
                    if l == LAYERS - 1:
                        attention_o(of_next(b))
                    turn_half(l, 1, 1)
                    ff_up(l, 1, 0)
                    ff_up(l, 1, 1)
                    if l + 1 < LAYERS:
                        turn_half(l + 1, 0, 0)
                    ff_down(l, 1, 0)
                    ff_up(l, 1, 2)
                    if l + 1 < LAYERS:
                        pe.wait_ge(s_cols.sem, s_cols.at(b, turn_no(l + 1, 0, 0)))
                        project(l + 1, 0)
                    ff_down(l, 1, 1)
                    ff_down(l, 1, 2)
                    if l + 1 < LAYERS:
                        project(l + 1, 1)
                        turn_half(l + 1, 0, 1)
                        pe.wait_ge(s_cols.sem, s_cols.at(b, turn_no(l + 1, 0, 1)))


def rotary_tables():
    half = np.arange(0, LD, 2, dtype=np.float32)
    inv_freq = (np.float32(1.0) / np.float32(10000.0) ** (half / np.float32(LD))).astype(np.float32)
    t = np.arange(N, dtype=np.float32)
    freqs = (t[:, None] * inv_freq[None, :]).astype(np.float32)
    freqs = np.concatenate([freqs, freqs], axis=-1)
    base = (half + np.float32(0.4 * LD)) / np.float32(1.4 * LD)
    power = (t - N // 2) / np.float32(32.0)
    scale = base[None, :] ** power[:, None]
    scale = np.concatenate([scale, scale], axis=-1)
    sign = np.where(np.arange(LD) < LD // 2, -1.0, 1.0).astype(np.float32)
    cos, sin = np.cos(freqs), np.sin(freqs) * sign
    tables = np.stack([cos * scale, sin * scale, cos / scale, sin / scale])
    return tables.astype(np.float32).reshape(4, T, P, LD).transpose(2, 0, 1, 3)


def constants():
    mats = np.zeros((P, 4, P), np.float32)
    mats[:, 0] = np.eye(P)
    mats[:, 1] = np.eye(P, k=1)
    mats[P - 1, 2, 0] = 1.0
    mats[:, 3] = np.kron(np.eye(HEADS), np.ones((HD, HD))) * HD ** -0.5
    sel = np.zeros((3 * EXPERTS, 8, P), np.float32)
    for e in range(EXPERTS):
        sel[e::EXPERTS, e // 2, HID_E * (e % 2):HID_E * (e % 2) + HID_E] = 1.0
    q, c = np.arange(P)[:, None], np.arange(BACK + P)[None, :]
    band = np.repeat(np.where((q <= c) & (c <= q + BACK), 0.0, NEG)[:, None, :], 2, axis=1)
    small = np.zeros((P, 81), np.float32)
    small[:, 48 + HD] = 1.0
    small[:, 0:16] = -0.5
    small[:, 16:32] = np.arange(16)
    r = np.arange(P) % 32
    small[:, 32] = np.where((r >= 16) & (r < 24), -1.0, 0.0)
    for i in range(2):
        small[:, 33 + i] = np.where((r >= 8) & (r < 16), -1.0, 0.0) + (r == 24 + i)
        small[:, 35 + i] = r == 24 + i
    return [mats, sel, band.astype(np.float32), small, rotary_tables()]


def kernel(**inputs):
    import concourse.bacc as bacc
    from concourse.bass_utils import run_bass_kernel_spmd

    i = {k: np.asarray(v) for k, v in inputs.items()}
    L0, F0, L1, F1 = "L0_attn_", "L0_ffn_", "L1_attn_", "L1_ffn_"

    def cat(parts, axis=1):
        return np.concatenate(parts, axis=axis)

    def rows(v, shape):
        return np.broadcast_to(v, shape)

    fb1 = np.zeros((LAYERS, 2, 3 * P), np.float32)
    fb1[:, :, 0:HID_F] = i[F1 + "b1"].reshape(LAYERS, 2, HID_F)
    fw2 = np.zeros((LAYERS, 3 * P, D), np.float32)
    fw2[:, 0:HID_F] = i[F1 + "w2"]
    arrays = {
        "x": i[L0 + "x"],
        "wl0": np.stack([i[L0 + w].T for w in ("Wq", "Wk", "Wv", "Wp")], axis=1),
        "gb": np.stack([i[L0 + w] for w in ("gq", "bq", "gk", "bk", "gv", "bv")], axis=1),
        "bp": rows(i[L0 + "bp"], (P, D)),
        "gate": i[F0 + "gate_w"].T,
        "ew_a": cat([i[F0 + "sfc1"].T, i[F0 + "w1"].reshape(EXPERTS * HID_E, D).T]).reshape(D, UNITS, P),
        "ew_u": i[F0 + "sfc2"].T.reshape(D, 2, P),
        "ew_d": cat([i[F0 + "sfc3"].T, i[F0 + "w2"].transpose(0, 2, 1).reshape(EXPERTS * HID_E, D)], 0)
                .reshape(UNITS, P, D).transpose(1, 0, 2),
        "wl1": np.stack([i[L1 + w].T for w in ("W_Q", "W_K", "W_K_prime", "W_V", "W_O")], axis=1),
        "alpha": rows(i[L1 + "alpha"].reshape(1, 1), (P, 1)),
        "wqkv": i[F1 + "wqkv"].reshape(LAYERS, D, 3, INNER).transpose(1, 0, 2, 3),
        "qks": rows(np.stack([i[F1 + "q_scale"], i[F1 + "k_scale"]], axis=1)[None], (P, LAYERS, 2, LD)),
        "wo": i[F1 + "wo"].reshape(LAYERS, PAIRS, P, D).transpose(2, 0, 1, 3),
        "lngb": np.stack([i[F1 + "ln_g"], i[F1 + "ln_b"]], axis=1).transpose(2, 0, 1),
        "fw1": i[F1 + "w1"].transpose(1, 0, 2),
        "fb1": fb1.reshape(LAYERS, 2, 3, P).transpose(3, 0, 1, 2),
        "fw2": fw2.reshape(LAYERS, 3, P, D).transpose(2, 0, 1, 3),
        "fb2": rows(i[F1 + "b2"][None], (P, LAYERS, D)),
    }
    for name, a in zip(("c_mat", "c_sel", "c_band", "c_small", "c_rot"), constants()):
        arrays[name] = a
    arrays = {k: np.ascontiguousarray(a) for k, a in arrays.items()}

    nc = bacc.Bacc("TRN2", target_bir_lowering=False, num_devices=1)
    args = [nc.dram_tensor(k, a.shape, mybir.dt.from_np(a.dtype), kind="ExternalInput").ap() for k, a in arrays.items()]
    args.append(nc.dram_tensor("out", (B, N, D), F32, kind="ExternalOutput").ap())
    build(nc, *args)
    result = run_bass_kernel_spmd(nc, [arrays], core_ids=[0])
    return result.results[0]["out"]
```
